# Optimizing a Trainium2 kernel written in Bass

```python
import numpy as np
import jax
import jax.numpy as jnp

def _softmax(x, axis=-1):
    return jax.nn.softmax(x, axis=axis)

def _gelu(x):
    return jax.nn.gelu(x, approximate=True)

def _silu(x):
    return jax.nn.silu(x)

def _sigmoid(x):
    return jax.nn.sigmoid(x)

def _layernorm(x, axis=-1, eps=1e-05):
    m = jnp.mean(x, axis=axis, keepdims=True)
    v = jnp.var(x, axis=axis, keepdims=True)
    return (x - m) / jnp.sqrt(v + eps)

def _scatter_add(tgt, idx, src, axis=0):
    return tgt.at[idx].add(src)

def _segment_sum(src, seg, n):
    return jax.ops.segment_sum(src, seg, n)
kernel_name = 'mk_flamingo_gated_d2_seqx_r2_f8375e'

def setup_inputs(seed: int=0):
    np.random.seed(seed)
    _w = jnp.asarray

    def _rec_inputs():
        import jax
        import jax.numpy as jnp
        _rk = jax.random.key(seed)
        x = 7.22e-05 + 1 * jax.random.normal(jax.random.fold_in(_rk, 1), (2, 2048, 512), jnp.float32)
        _lenS = 2048 - jax.random.randint(jax.random.fold_in(_rk, 7), (2,), 0, max(1, 2048 // 4) + 1, jnp.int32)
        _lenS2 = 77 - jax.random.randint(jax.random.fold_in(_rk, 8), (2,), 0, max(1, 77 // 4) + 1, jnp.int32)
        _ctx_1024P = jax.random.normal(jax.random.fold_in(_rk, 11), (2, 16, 512), jnp.float32)
        _ctx_1024c = jax.random.dirichlet(jax.random.fold_in(_rk, 511), 0.3 * jnp.ones((16,), jnp.float32), (2, 77))
        _ctx_1024t = jnp.einsum('bsk,bkd->bsd', _ctx_1024c, _ctx_1024P)
        _ctx_1024t = _ctx_1024t * jax.lax.rsqrt(jnp.mean(jnp.square(_ctx_1024t)) + 1e-12) * 0.953939
        ctx_1024 = 4.13588e-05 + 0.999923 * (_ctx_1024t + 0.3 * jax.random.normal(jax.random.fold_in(_rk, 611), (2, 77, 512), jnp.float32))
        _validS = jnp.arange(2048)[None, :] < _lenS[:, None]
        _validS2 = jnp.arange(77)[None, :] < _lenS2[:, None]
        _causal = jnp.tril(jnp.ones((2048, 2048), dtype=bool))
        mask_BxS2_ff1 = jnp.where(jnp.ones((2, 77), dtype=bool), 1.0, 0.0).astype(jnp.float32)
        _g = jax.random.normal(jax.random.fold_in(_rk, 9001), (2, 2), jnp.float32)
        _g = jnp.sign(_g) * jnp.maximum(jnp.abs(_g), 1.0) + (_g == 0) * 1.0
        g_xattn = _g[0]
        g_ffn = _g[1]
        return (x, ctx_1024, mask_BxS2_ff1, g_xattn, g_ffn)
    x, ctx_1024, mask_BxS2_ff1, g_xattn, g_ffn = _rec_inputs()

    def _L0_xattn_setup():
        import jax, jax.numpy as jnp
        import numpy as np
        EMBED_DIM = 512
        NUM_HEADS = 16
        HEAD_DIM = EMBED_DIM // NUM_HEADS
        BSZ, TGT, SRC = (4, 1024, 1024)

        def _split_heads(x, bsz, seqlen):
            return x.reshape(bsz, seqlen, NUM_HEADS, HEAD_DIM).transpose(0, 2, 1, 3)
        key = jax.random.key(seed)
        ks = jax.random.split(key, 8)
        s = EMBED_DIM ** (-0.5)
        return {'query': jax.random.normal(ks[0], (BSZ, TGT, EMBED_DIM), jnp.float32), 'key': jax.random.normal(ks[1], (BSZ, SRC, EMBED_DIM), jnp.float32), 'key_padding_mask': jnp.ones((BSZ, SRC), jnp.float32), 'Wq': jax.random.normal(ks[2], (EMBED_DIM, EMBED_DIM), jnp.float32) * s, 'bq': jnp.zeros((EMBED_DIM,), jnp.float32), 'Wk': jax.random.normal(ks[3], (EMBED_DIM, EMBED_DIM), jnp.float32) * s, 'bk': jnp.zeros((EMBED_DIM,), jnp.float32), 'Wv': jax.random.normal(ks[4], (EMBED_DIM, EMBED_DIM), jnp.float32) * s, 'bv': jnp.zeros((EMBED_DIM,), jnp.float32), 'Wo': jax.random.normal(ks[5], (EMBED_DIM, EMBED_DIM), jnp.float32) * s, 'bo': jnp.zeros((EMBED_DIM,), jnp.float32)}
    _L0_xattn_all = _L0_xattn_setup()
    _L0_xattn_in = {k: v for k, v in _L0_xattn_all.items() if k in ('Wq', 'bq', 'Wk', 'bk', 'Wv', 'bv', 'Wo', 'bo')}
    del _L0_xattn_all

    def _L0_ffn_setup():
        import jax, jax.numpy as jnp
        import numpy as np
        INT8_MAX = 127.0

        def _absmax_scale(x, axes):
            amax = jnp.max(jnp.abs(x), axis=axes, keepdims=True)
            return jnp.maximum(amax, 1e-12) / INT8_MAX
        key = jax.random.key(seed)
        k1, k2 = jax.random.split(key)
        lhs = jax.random.normal(k1, (4, 4096, 512), dtype=jnp.float32)
        rhs = jax.random.normal(k2, (512, 512), dtype=jnp.float32)
        return {'lhs': lhs, 'rhs': rhs}
    _L0_ffn_all = _L0_ffn_setup()
    _L0_ffn_in = {k: v for k, v in _L0_ffn_all.items() if k in ('rhs',)}
    del _L0_ffn_all

    def _L1_xattn_setup():
        import jax, jax.numpy as jnp
        import numpy as np
        B, NQ, NK = (4, 1024, 1024)
        QDIM = CDIM = 512
        H, DH = (16, 64)
        SCALE = DH ** (-0.5)
        WSTD = 0.02
        key = jax.random.key(seed)
        ks = jax.random.split(key, 6)
        inner = H * DH
        return {'x': jax.random.normal(ks[0], (B, NQ, QDIM), dtype=jnp.float32), 'context': jax.random.normal(ks[1], (B, NK, CDIM), dtype=jnp.float32), 'Wq': jax.random.normal(ks[2], (inner, QDIM), dtype=jnp.float32) * WSTD, 'Wk': jax.random.normal(ks[3], (inner, CDIM), dtype=jnp.float32) * WSTD, 'Wv': jax.random.normal(ks[4], (inner, CDIM), dtype=jnp.float32) * WSTD, 'Wo': jax.random.normal(ks[5], (QDIM, inner), dtype=jnp.float32) * WSTD, 'bo': jnp.zeros((QDIM,), dtype=jnp.float32)}
    _L1_xattn_all = _L1_xattn_setup()
    _L1_xattn_in = {k: v for k, v in _L1_xattn_all.items() if k in ('Wq', 'Wk', 'Wv', 'Wo', 'bo')}
    del _L1_xattn_all

    def _L1_ffn_setup():
        import jax, jax.numpy as jnp
        import numpy as np
        IN_DIM, OUT_DIM, N_PROTO, RANK = (512, 512, 32, 16)
        key = jax.random.key(seed)
        ks = jax.random.split(key, 5)
        x = jax.random.normal(ks[0], (2, 2048, IN_DIM), dtype=jnp.float32)
        prototypes = jax.random.normal(ks[1], (N_PROTO, IN_DIM), dtype=jnp.float32) * 0.02
        B = jax.random.normal(ks[2], (N_PROTO, RANK, IN_DIM), dtype=jnp.float32) * 0.02
        A = jax.random.normal(ks[3], (N_PROTO, OUT_DIM, RANK), dtype=jnp.float32) * 0.02
        bias = jnp.zeros((N_PROTO, OUT_DIM), dtype=jnp.float32)
        temp = jnp.asarray(1.0, dtype=jnp.float32)
        return {'x': x, 'prototypes': prototypes, 'B': B, 'A': A, 'bias': bias, 'temp': temp}
    _L1_ffn_all = _L1_ffn_setup()
    _L1_ffn_in = {k: v for k, v in _L1_ffn_all.items() if k in ('prototypes', 'B', 'A', 'bias', 'temp')}
    del _L1_ffn_all
    return {'x': x, 'ctx_1024': ctx_1024, 'mask_BxS2_ff1': mask_BxS2_ff1, 'g_xattn': g_xattn, 'g_ffn': g_ffn, 'L0_xattn_Wq': _L0_xattn_in['Wq'], 'L0_xattn_bq': _L0_xattn_in['bq'], 'L0_xattn_Wk': _L0_xattn_in['Wk'], 'L0_xattn_bk': _L0_xattn_in['bk'], 'L0_xattn_Wv': _L0_xattn_in['Wv'], 'L0_xattn_bv': _L0_xattn_in['bv'], 'L0_xattn_Wo': _L0_xattn_in['Wo'], 'L0_xattn_bo': _L0_xattn_in['bo'], 'L0_ffn_rhs': _L0_ffn_in['rhs'], 'L1_xattn_Wq': _L1_xattn_in['Wq'], 'L1_xattn_Wk': _L1_xattn_in['Wk'], 'L1_xattn_Wv': _L1_xattn_in['Wv'], 'L1_xattn_Wo': _L1_xattn_in['Wo'], 'L1_xattn_bo': _L1_xattn_in['bo'], 'L1_ffn_prototypes': _L1_ffn_in['prototypes'], 'L1_ffn_B': _L1_ffn_in['B'], 'L1_ffn_A': _L1_ffn_in['A'], 'L1_ffn_bias': _L1_ffn_in['bias'], 'L1_ffn_temp': _L1_ffn_in['temp']}

def reference(x, ctx_1024, mask_BxS2_ff1, g_xattn, g_ffn, L0_xattn_Wq, L0_xattn_bq, L0_xattn_Wk, L0_xattn_bk, L0_xattn_Wv, L0_xattn_bv, L0_xattn_Wo, L0_xattn_bo, L0_ffn_rhs, L1_xattn_Wq, L1_xattn_Wk, L1_xattn_Wv, L1_xattn_Wo, L1_xattn_bo, L1_ffn_prototypes, L1_ffn_B, L1_ffn_A, L1_ffn_bias, L1_ffn_temp):
    import jax
    import jax.numpy as jnp

    def _L0_xattn_ref(query, key, key_padding_mask, Wq, bq, Wk, bk, Wv, bv, Wo, bo):
        import jax, jax.numpy as jnp
        import numpy as np
        EMBED_DIM = 512
        NUM_HEADS = 16
        HEAD_DIM = EMBED_DIM // NUM_HEADS
        BSZ, TGT, SRC = (4, 1024, 1024)

        def _split_heads(x, bsz, seqlen):
            return x.reshape(bsz, seqlen, NUM_HEADS, HEAD_DIM).transpose(0, 2, 1, 3)
        bsz, src_len, embed_dim = key.shape
        tgt_len = query.shape[1]
        scaling = HEAD_DIM ** (-0.5)
        q = (query @ Wq.T + bq) * scaling
        k = key @ Wk.T + bk
        v = key @ Wv.T + bv
        qh = _split_heads(q, bsz, tgt_len)
        kh = _split_heads(k, bsz, src_len)
        vh = _split_heads(v, bsz, src_len)
        scores = jnp.einsum('bhtd,bhsd->bhts', qh, kh)
        inv = 1.0 - key_padding_mask.astype(scores.dtype)
        neg = jnp.finfo(scores.dtype).min
        add_mask = jnp.where(inv.astype(bool), neg, inv)
        scores = scores + add_mask[:, None, None, :]
        probs = jax.nn.softmax(scores, axis=-1)
        out = jnp.einsum('bhts,bhsd->bhtd', probs, vh)
        out = out.transpose(0, 2, 1, 3).reshape(bsz, tgt_len, embed_dim)
        return out @ Wo.T + bo

    def _L0_ffn_ref(lhs, rhs):
        import jax, jax.numpy as jnp
        import numpy as np
        INT8_MAX = 127.0

        def _absmax_scale(x, axes):
            amax = jnp.max(jnp.abs(x), axis=axes, keepdims=True)
            return jnp.maximum(amax, 1e-12) / INT8_MAX
        lhs_scale = _absmax_scale(lhs, (2,))
        rhs_scale = _absmax_scale(rhs, (0,))
        q_lhs = jnp.clip(jnp.round(lhs / lhs_scale), -INT8_MAX, INT8_MAX).astype(jnp.int8)
        q_rhs = jnp.clip(jnp.round(rhs / rhs_scale), -INT8_MAX, INT8_MAX).astype(jnp.int8)
        acc = jax.lax.dot_general(q_lhs, q_rhs, (((2,), (0,)), ((), ())), preferred_element_type=jnp.int32)
        return acc.astype(jnp.float32) * lhs_scale * rhs_scale

    def _L1_xattn_ref(x, context, Wq, Wk, Wv, Wo, bo):
        import jax, jax.numpy as jnp
        import numpy as np
        B, NQ, NK = (4, 1024, 1024)
        QDIM = CDIM = 512
        H, DH = (16, 64)
        SCALE = DH ** (-0.5)
        WSTD = 0.02
        b, nq, _ = x.shape
        nk = context.shape[1]
        q = (x @ Wq.T).reshape(b, nq, H, DH)
        k = (context @ Wk.T).reshape(b, nk, H, DH)
        v = (context @ Wv.T).reshape(b, nk, H, DH)
        sim = jnp.einsum('bihd,bjhd->bhij', q, k) * SCALE
        attn = jax.nn.softmax(sim, axis=-1)
        out = jnp.einsum('bhij,bjhd->bihd', attn, v).reshape(b, nq, H * DH)
        return out @ Wo.T + bo

    def _L1_ffn_ref(x, prototypes, B, A, bias, temp):
        import jax, jax.numpy as jnp
        import numpy as np
        IN_DIM, OUT_DIM, N_PROTO, RANK = (512, 512, 32, 16)
        lead = x.shape[:-1]
        xf = x.reshape(-1, IN_DIM)
        x2 = jnp.sum(xf * xf, axis=1, keepdims=True)
        p2 = jnp.sum(prototypes * prototypes, axis=1)
        d2 = x2 + p2[None, :] - 2.0 * (xf @ prototypes.T)
        dists = jnp.sqrt(jnp.maximum(d2, 0.0))
        t = jnp.maximum(jnp.abs(temp), 0.1)
        w = jax.nn.softmax(-dists / t, axis=1)
        topw, topi = jax.lax.top_k(w, 2)
        topw = topw / jnp.sum(topw, axis=1, keepdims=True)
        out = jnp.zeros((xf.shape[0], OUT_DIM), dtype=xf.dtype)
        for tslot in range(2):
            idx = topi[:, tslot]
            wt = topw[:, tslot:tslot + 1]
            h = jnp.einsum('nri,ni->nr', B[idx], xf)
            y = jnp.einsum('nor,nr->no', A[idx], h) + bias[idx]
            out = out + wt * y
        return out.reshape(*lead, OUT_DIM)
    x = x + jnp.tanh(g_xattn[0]) * _L0_xattn_ref(_layernorm(x, axis=-1), ctx_1024, mask_BxS2_ff1, L0_xattn_Wq, L0_xattn_bq, L0_xattn_Wk, L0_xattn_bk, L0_xattn_Wv, L0_xattn_bv, L0_xattn_Wo, L0_xattn_bo)
    x = x + jnp.tanh(g_ffn[0]) * _L0_ffn_ref(_layernorm(x, axis=-1), L0_ffn_rhs)
    x = x + jnp.tanh(g_xattn[1]) * _L1_xattn_ref(_layernorm(x, axis=-1), ctx_1024, L1_xattn_Wq, L1_xattn_Wk, L1_xattn_Wv, L1_xattn_Wo, L1_xattn_bo)
    x = x + jnp.tanh(g_ffn[1]) * _L1_ffn_ref(_layernorm(x, axis=-1), L1_ffn_prototypes, L1_ffn_B, L1_ffn_A, L1_ffn_bias, L1_ffn_temp)
    return x

_drawn_inputs = setup_inputs


def setup_inputs(seed=0):
    import zlib

    import numpy as np

    out = dict(_drawn_inputs(seed))
    spreads = {'g_ffn': (-1.0, 0.6),
     'L0_xattn_bq': (0.0, 0.1),
     'L0_xattn_bk': (0.0, 0.1),
     'L0_xattn_bv': (0.0, 0.1),
     'L0_xattn_bo': (0.0, 0.1),
     'L1_xattn_bo': (0.0, 0.8),
     'L1_ffn_bias': (0.0, 2.0)}
    factors = {'L1_xattn_Wq': 8.0,
     'L1_xattn_Wk': 8.0,
     'L1_xattn_Wv': 6.843,
     'L1_xattn_Wo': 7.037,
     'L1_ffn_prototypes': 8.0,
     'L1_ffn_B': 8.0,
     'L1_ffn_A': 8.0}
    for name, (base, spread) in spreads.items():
        noise = np.random.default_rng([zlib.crc32(name.encode()), seed]).standard_normal(out[name].shape)
        drawn = base * np.exp(spread * noise) if base else spread * noise
        out[name] = jnp.asarray(drawn.astype(out[name].dtype))
    for name, factor in factors.items():
        out[name] = (out[name] * factor).astype(out[name].dtype)
    return out
```

```python
from contextlib import ExitStack

import concourse.bass as bass
from concourse import mybir

P = 128
D = 512
FT = D // P
B, T = 2, 2048
TILES = B * T // P
PER_B = T // P
HEADS = 16
KEYS = 77
HK = HEADS * KEYS
BANK_HEADS = (6, 6, 4)
ROWT = (HK + 1 + P - 1) // P
HKP = ROWT * P
PROTOS, RANK = 32, 16
EPS = 1e-5
TINY = 1e-12
INT8_MAX = 127.0
MAGIC = 1.5 * 2.0 ** 23
NEG = -(2.0 ** 127)
XS = 2.0 ** 11
PSC = 2.0 ** 15
WS = 2.0 ** 14
HS = 2.0 ** 6
SLOTS = 6

ALU = mybir.AluOpType
ACT = mybir.ActivationFunctionType
AX = mybir.AxisListType.X
F32 = mybir.dt.float32
F16 = mybir.dt.float16
BF16 = mybir.dt.bfloat16
U32 = mybir.dt.uint32
RMAX = bass.bass_isa.ReduceOp.max


def build(nc, x, ctx_in, mask, g_xattn, g_ffn, Wq0, bq0, Wk0, bk0, Wv0, bv0, Wo0, bo0, rhs,
          Wq1, Wk1, Wv1, Wo1, bo1, protos, Bw, Aw, biasw, temp, out):
    with ExitStack() as ctx:
        def sb(name, shape, dt=F32):
            return ctx.enter_context(nc.sbuf_tensor(name, shape, dt))

        def sem(name):
            return ctx.enter_context(nc.semaphore(name))

        PS = ctx.enter_context(nc.psum_tensor("PS", [P, 8, 512], F32))
        S_BANK, PT_BANK, G6, G7 = 0, 3, 6, 7
        FFN1 = PS[:, PT_BANK + 1, :]
        W_T = PS[0:PROTOS, PT_BANK + 2, 256:256 + P]

        X = sb("X", [P, TILES, D])
        KF = sb("KF", [P, B * 2 * FT * HK], F16)
        VW = sb("VW", [P, B * 2 * ROWT * D], F16)
        Kf = KF[:, :].rearrange("p (b w f k) -> p b w f k", b=B, w=2, f=FT)
        Vw = VW[:, :].rearrange("p (b w i o) -> p b w i o", b=B, w=2, i=ROWT)

        ARENA = sb("ARENA", [P, 57 * 256])
        at = [0]

        def arena(words, dt=F32, start=None):
            a = at[0] if start is None else start
            at[0] = a + words
            assert at[0] <= 57 * 256
            return ARENA[:, a:a + words] if dt == F32 else ARENA[:, a:a + words].bitcast(dt)

        xn = arena(2 * D).rearrange("p (u d) -> p u d", u=2)
        xh = arena(D, F16).rearrange("p (u f t) -> p u f t", u=2, f=FT)
        xl = arena(D, F16).rearrange("p (u f t) -> p u f t", u=2, f=FT)
        sS = arena(HK)
        Pb = arena(2 * HKP).rearrange("p (u k) -> p u k", u=2)
        pth = arena(HKP // 2, F16).rearrange("p (i t) -> p i t", i=ROWT)
        ptl = arena(HKP // 2, F16).rearrange("p (i t) -> p i t", i=ROWT)
        ffn0 = at[0]
        xf = arena(D)
        xq = arena(D)
        xqT = arena(D // 2, F16).rearrange("p (f t) -> p f t", f=FT)
        dq = arena(D)
        after_b = at[0]
        dh = arena(D // 2, F16, start=ffn0 + D).rearrange("p (f t) -> p f t", f=FT)
        dl = arena(D // 2, F16).rearrange("p (f t) -> p f t", f=FT)
        hw = arena(D)
        hh = arena(D // 2, F16).rearrange("p (f t) -> p f t", f=FT)
        hl = arena(D // 2, F16).rearrange("p (f t) -> p f t", f=FT)
        junk = arena(D // 2, F16)
        loop_end = max(at[0], after_b)
        rq = arena(FT * D // 2, F16, start=loop_end).rearrange("p (f o) -> p f o", f=FT)
        cg = arena(D)
        row = arena(B * HK // 2, BF16).rearrange("p (b k) -> p b k", b=B)
        bt = arena(FT * D, F16, start=loop_end).rearrange("p (w f n) -> p w f n", w=2, f=FT)
        ad = arena(FT * D, F16).rearrange("p (w f n) -> p w f n", w=2, f=FT)
        pw = arena(FT * PROTOS, F16).rearrange("p (w f n) -> p w f n", w=2, f=FT)
        p2 = arena(PROTOS)
        bs = arena(D)

        VB = arena(8 * 384, start=0)
        VT = arena(8 * B * KEYS)
        WOT = arena(8 * D)
        BO = arena(D)
        f32vw = VW[:, :].bitcast(F32)
        ring = f32vw[:, 0:SLOTS * D].rearrange("p (s d) -> p s d", s=SLOTS)
        wqn = f32vw[:, SLOTS * D:SLOTS * D + 8 * D].rearrange("p (j d) -> p j d", j=8)
        KB = f32vw[:, SLOTS * D + 8 * D:SLOTS * D + 8 * D + HEADS * B * KEYS]
        f32kf = KF[:, :].bitcast(F32)
        craw = f32kf[:, 0:B * D].rearrange("p (b d) -> p b d", b=B)
        cT = f32kf[:, 1024:1024 + FT * B * KEYS].rearrange("p (f k) -> p f k", f=FT)
        WT = f32kf[:, 2048:2048 + 2 * D].rearrange("p (u f n) -> p u f n", u=2, f=FT)
        rraw = f32kf[:, 4096:4096 + FT * D].rearrange("p (f o) -> p f o", f=FT)
        rabs = f32kf[:, 6144:6144 + D]
        btf = arena(FT * D, start=0).rearrange("p (f n) -> p f n", f=FT)
        adf = arena(FT * D).rearrange("p (f n) -> p f n", f=FT)
        ptf = arena(FT * PROTOS).rearrange("p (f n) -> p f n", f=FT)
        psq = arena(FT * PROTOS).rearrange("p (f n) -> p f n", f=FT)
        praw = arena(D)

        ident = sb("ident", [P, P])
        ones16 = sb("ones16", [P, P], BF16)
        ones32 = sb("ones32", [P, P])
        e80 = sb("e80", [P, P])
        iota32 = sb("iota32", [P, PROTOS])
        gates = sb("gates", [P, 4])
        tinv = sb("tinv", [P, 1])
        nmagic = sb("nmagic", [P, 1])
        half = sb("half", [P, 2])
        mone = sb("mone", [P, 1])
        bias_q = sb("bias_q", [P, 3, 4])
        mk = sb("mk", [P, B, KEYS])
        amx = sb("amx", [P, 8])
        amr = sb("amr", [P, 8])
        sc = sb("sc", [P, 16])
        st = sb("st", [P, 2, 2, 6])
        mv = sb("mv", [P, 2, 2, 2])
        rstd = sb("rstd", [P, 2, 2, 2])
        mx = sb("mx", [P, 2, HEADS])
        smx = sb("smx", [P, 2, 2, HEADS])
        lsb = sb("lsb", [P, 2, 4])
        rt = sb("rt", [P, 2, PROTOS])
        m8 = sb("m8", [P, 8])
        i8 = sb("i8", [P, 8], U32)
        rw = sb("rw", [P, 16])
        x2 = sb("x2", [P, 2])
        oh = sb("oh", [P, 2, PROTOS])
        wt = sb("wt", [P, PROTOS])
        wtT = sb("wtT", [PROTOS, P])
        tg = sb("tg", [P, 8])

        def tiles_of(layer):
            return 4 * (layer + 1)

        def per_tile(layer):
            return HEADS // tiles_of(layer)

        def first_row_tile(layer, j):
            return per_tile(layer) * KEYS * j // P

        def last_row_tile(layer, j):
            return (per_tile(layer) * KEYS * (j + 1) - 1) // P

        def window(layer):
            return 512 if layer == 0 else 384

        def scores_bank(k):
            return PS[:, S_BANK + k, 0:BANK_HEADS[k] * KEYS]

        def by_head(ap):
            return ap.rearrange("p (h k) -> p h k", k=KEYS)

        def scores_parts():
            two = PS[:, S_BANK:S_BANK + 2, 0:6 * KEYS].rearrange("p b (h k) -> p b h k", k=KEYS)
            return [(two, slice(0, 12 * KEYS), slice(0, 12), (2, 6)),
                    (by_head(PS[:, S_BANK + 2, 0:4 * KEYS]), slice(12 * KEYS, HK), slice(12, 16), (4,))]

        def cut(ap, shape):
            return ap.rearrange("p (a b) -> p a b", a=shape[0]) if len(shape) == 2 else ap

        KBlk = [KB.rearrange("p (j b k) -> p j b k", j=tiles_of(l), b=B) for l in range(2)]
        VBlk = [VB[:, 0:tiles_of(l) * window(l)].rearrange("p (j c) -> p j c", j=tiles_of(l)) for l in range(2)]
        VTl = [VT[:, 0:tiles_of(l) * B * KEYS].rearrange("p (j b k) -> p j b k", j=tiles_of(l), b=B) for l in range(2)]
        WOl = WOT.rearrange("p (j d) -> p j d", j=8)

        s_const = sem("consts_made")
        s_constv = sem("scalar_inputs_used")
        s_x = sem("x_loaded")
        s_small = sem("small_inputs_loaded")
        s_ctx = sem("context_loaded")
        s_slot = [sem(f"chunk_slot{i}_loaded") for i in range(SLOTS)]
        s_wq = sem("wq_loaded")
        s_bo = sem("bo_loaded")
        s_zero = sem("setup_zeroed")
        s_pad = sem("probs_padded")
        s_cT_ps = sem("context_turned")
        s_cT = sem("context_turned_copied")
        s_turn = sem("chunk_turned")
        s_turned = sem("chunk_turned_copied")
        s_kv_ps = sem("kv_projected")
        s_kv = sem("kv_copied")
        s_am = sem("absmax_per_partition")
        s_amr = sem("absmax_over_partitions")
        s_sc = sem("scales_step")
        s_scale = sem("scales_ready")
        s_kf_ps = sem("folded_keys_product")
        s_kfh = sem("folded_keys_hi")
        s_kfl = sem("folded_keys_lo")
        s_vb = sem("value_window_filled")
        s_vw_ps = sem("folded_values_product")
        s_vwh = sem("folded_values_hi")
        s_vwl = sem("folded_values_lo")
        s_row_ps = sem("score_row_product")
        s_row = sem("score_row_step")
        s_rhs = sem("rhs_loaded")
        s_rmax = sem("rhs_absmax")
        s_rmaxr = sem("rhs_absmax_over_partitions")
        s_rq = sem("rhs_step")
        s_pr_ps = sem("prototypes_turned")
        s_pr = sem("prototypes_step")
        s_p2_ps = sem("prototype_norms")
        s_dw = sem("expert_weights_hi")
        s_dwl = sem("expert_weights_lo")
        s_gate = sem("gates_ready")

        L = {}
        for name in ("stats", "mean_var", "var_eps", "rstd", "ln", "turned", "ln_hi", "ln_lo", "scores", "max",
                     "shifted", "exp", "sum", "inv_sum", "probs", "probs_turned", "probs_hi", "probs_lo", "attn_out",
                     "x_attn", "f_stats", "f_mean_var", "f_var_eps", "f_rstd", "f_ln", "absmax", "lhs_scale",
                     "lhs_inv", "quant", "clamped", "quant_turned", "quant_T", "ffn0_out", "ffn0_scaled", "x_ffn0",
                     "sq_sum", "d_turned", "d_hi", "d_lo", "hidden", "dots", "dist_a", "dist_b", "best", "best_at",
                     "route", "gap", "gap_exp", "weights", "weighted", "h_turned", "h_hi", "h_lo", "w_T", "ffn1_out",
                     "x_ffn1", "stored"):
            L[name] = sem(name)

        def chunk_list(layer):
            n = tiles_of(layer)
            wk, wv, wo = ((Wk0, Wv0, Wo0), (Wk1, Wv1, Wo1))[layer]
            src = []
            if layer == 1:
                rows = Bw.rearrange("n r d -> (n r) d")
                src += [rows[P * j:P * j + P, :] for j in range(FT)]
                src += [Aw[:, P * j:P * j + P, :].rearrange("n o r -> o n r") for j in range(FT)]
            src += [w[P * j:P * j + P, :] for w in (wk, wv) for j in range(n)]
            src += [wo[:, P * j:P * j + P].rearrange("(q p) c -> p q c", p=P) for j in range(n)]
            return src

        first_chunk = [0, len(chunk_list(0))]
        first_kv = [0, 2 * tiles_of(0)]
        first_am = [0, 1]
        units = B * FT

        def setup(layer):
            J, hpt = tiles_of(layer), per_tile(layer)
            dhd = P // hpt
            c0 = first_chunk[layer]
            chunks = chunk_list(layer)
            n_exp = 2 * FT * layer
            n_kv = 2 * J
            a0 = c0 + n_exp
            turned_all = c0 + len(chunks)
            kv0 = first_kv[layer]
            scaling = float(dhd) ** -0.5
            wq = (Wq0, Wq1)[layer]
            bo = (bo0, bo1)[layer]

            with nc.Block() as block:
                @block.sync
                def _(sp):
                    sp.dma_start(craw[0:KEYS], ctx_in.rearrange("b k d -> k b d")).then_inc(s_ctx, 16)
                    for c, src in enumerate(chunks):
                        g = c0 + c
                        if c >= SLOTS:
                            sp.wait_ge(s_turn, g - SLOTS + 1)
                        dst = ring[:, c % SLOTS, :]
                        if c >= n_exp + n_kv:
                            dst = dst.rearrange("p (q c) -> p q c", q=FT)
                        elif FT <= c < n_exp:
                            dst = dst.rearrange("p (n r) -> p n r", r=RANK)
                        sp.dma_start(dst, src).then_inc(s_slot[c % SLOTS], 16)

                @block.gpsimd
                def _(pool):
                    if layer == 0:
                        pool.memset(ident[:], 0.0).then_inc(s_const, 1)
                        pool.memset(e80[:], 0.0).then_inc(s_const, 1)
                        pool.memset(ones16[:], 1.0)
                        pool.memset(ones32[:], 1.0)
                        pool.memset(nmagic[:], -MAGIC)
                        pool.memset(half[:, 0:1], -0.5)
                        pool.memset(half[:, 1:2], 0.5)
                        pool.memset(mone[:], -1.0)
                        pool.memset(amx[:], 0.0)
                        pool.memset(row, 0.0)
                        pool.iota(iota32[:], [[1, PROTOS]], base=0, channel_multiplier=0,
                                  allow_small_or_imprecise_dtypes=True)
                        pool.wait_ge(s_const, 2)
                        pool.affine_select(out=ident[:], in_=ident[:], compare_op=ALU.not_equal, fill=1.0, base=0,
                                           pattern=[[-1, P]], channel_multiplier=1)
                        pool.affine_select(out=e80[:], in_=e80[:], compare_op=ALU.not_equal, fill=1.0,
                                           base=-(HK % P), pattern=[[1, P]],
                                           channel_multiplier=P).then_inc(s_const, 1)
                    pool.memset(BO, 0.0)
                    pool.memset(KB, 0.0).then_inc(s_zero, 1)
                    if layer == 1:
                        pool.wait_ge(s_am, 2)
                        pool.partition_all_reduce(amr[:], amx[:], P, RMAX).then_inc(s_amr, 1)
                        pool.wait_ge(s_amr, 2)
                        pool.wait_ge(s_dwl, 1)
                    pool.memset(VB[:, 0:J * window(layer)], 0.0)
                    if layer == 0:
                        pool.wait_ge(s_rmax, 1)
                        pool.partition_all_reduce(cg, rabs, P, RMAX).then_inc(s_rmaxr, 1)
                        pool.wait_ge(s_rmaxr, 1)
                    pool.wait_ge(s_am, 2 * layer + 1)
                    pool.partition_all_reduce(amr[:], amx[:], P, RMAX).then_inc(s_amr, 1)
                    pool.wait_ge(s_amr, 2 * layer + 1)
                    for b in range(B):
                        if b:
                            pool.wait_ge(s_vw_ps, (2 * layer + b) * ROWT)
                        if b == 0:
                            pool.wait_ge(s_kv, kv0 + n_kv)
                        for j in range(J):
                            off = hpt * KEYS * j - P * first_row_tile(layer, j)
                            for r in range(hpt):
                                rows = slice(dhd * r, dhd * r + dhd)
                                last = pool.tensor_copy(VBlk[layer][rows, j, off + KEYS * r:off + KEYS * r + KEYS],
                                                        VTl[layer][rows, j, b, :])
                        last.then_inc(s_vb, 1)

                @block.scalar
                def _(act):
                    if layer == 0:
                        act.dma_start(tg[:, 0:2], g_xattn.partition_broadcast(P)).then_inc(s_small, 16)
                        act.dma_start(tg[:, 2:4], g_ffn.partition_broadcast(P)).then_inc(s_small, 16)
                        act.dma_start(tg[:, 4:5], temp.partition_broadcast(P)).then_inc(s_small, 16)
                        act.dma_start(mk[96:97], mask.rearrange("(a b) k -> a b k", a=1)).then_inc(s_small, 16)
                        for k, vec in enumerate((bq0, bk0, bv0)):
                            act.dma_start(bias_q[:, k, :], vec.rearrange("(j p) -> p j", p=P),
                                          allow_slow_non_contiguous=True).then_inc(s_small, 16)
                        act.wait_ge(s_small, 16 * 7)
                        act.activation(gates[:], tg[:, 0:4], ACT.Tanh).then_inc(s_gate, 1)
                        act.dma_start(rraw, rhs.rearrange("(f p) o -> p f o", p=P)).then_inc(s_rhs, 16)
                    act.wait_ge(s_zero, layer + 1)
                    act.dma_start(BO[0:1, :], bo.rearrange("(a d) -> a d", a=1)).then_inc(s_bo, 16)
                    act.dma_start(wqn[:, 0:J, :], wq.rearrange("(j p) d -> p j d", p=P)).then_inc(s_wq, 16)
                    if layer == 0:
                        act.dma_start(X[:], x.rearrange("b (t p) d -> p (b t) d", p=P)).then_inc(s_x, 16)
                    if layer == 1:
                        act.dma_start(praw[0:PROTOS, :], protos).then_inc(s_small, 16)
                        act.dma_start(bs[0:PROTOS, :], biasw).then_inc(s_small, 16)
                    act.wait_ge(s_cT_ps, layer + 1)
                    act.copy(cT, PS[:, 0:2, 0:2 * B * KEYS].rearrange("p a (f k) -> p a f k", f=2)).then_inc(s_cT, 1)
                    for c in range(n_exp):
                        act.wait_ge(s_turn, c0 + c + 1)
                        dst = (btf if c < FT else adf)[:, :, P * (c % FT):P * (c % FT) + P]
                        act.copy(dst, PS[:, G6 + c % 2, :].rearrange("p (f n) -> p f n", f=FT)).then_inc(s_turned, 1)
                    if layer == 1:
                        act.wait_ge(s_scale, 2)
                        for dst, src, k in ((bt, btf, 8), (ad, adf, 9), (pw, ptf, 10)):
                            act.activation(dst[:, 0], src, ACT.Copy, scale=sc[:, k:k + 1]).then_inc(s_dw, 1)
                    for c in range(len(chunks) - n_exp):
                        act.wait_ge(s_turn, a0 + c + 1)
                        src = PS[:, G6 + c % 2, :]
                        if c < n_kv:
                            if c >= 2:
                                act.wait_ge(s_kv_ps, kv0 + c - 1)
                            act.copy(WT[:, c % 2].rearrange("p f n -> p (f n)"), src).then_inc(s_turned, 1)
                        else:
                            act.copy(WOl[:, c - n_kv, :], src).then_inc(s_turned, 1)
                    act.wait_ge(s_scale, 2 * layer + 1)
                    for u in range(units):
                        b, f = divmod(u, FT)
                        k0 = 3 * (u % 2)
                        act.wait_ge(s_kf_ps, units * layer + u + 1)
                        act.activation(Kf[:, b, 0, f, 0:12 * KEYS].rearrange("p (a k) -> p a k", a=2),
                                       PS[:, k0:k0 + 2, 0:6 * KEYS], ACT.Copy, scale=sc[:, 0:1])
                        act.activation(Kf[:, b, 0, f, 12 * KEYS:HK], PS[:, k0 + 2, 0:4 * KEYS], ACT.Copy,
                                       scale=sc[:, 0:1]).then_inc(s_kfh, 1)
                    for v in range(B * ROWT):
                        b, i = divmod(v, ROWT)
                        act.wait_ge(s_vw_ps, B * ROWT * layer + v + 1)
                        act.activation(Vw[:, b, 0, i, :], PS[:, G6 + v % 2, :], ACT.Copy,
                                       scale=sc[:, 1:2]).then_inc(s_vwh, 1)

                @block.tensor
                def _(pe):
                    def turn(c):
                        pe.wait_ge(s_slot[c % SLOTS], 16 * (first_use[layer][c % SLOTS] + c // SLOTS + 1))
                        if c >= 2:
                            pe.wait_ge(s_turned, c0 + c - 1)
                        for q in range(FT):
                            mm = pe.transpose(PS[:, G6 + c % 2, P * q:P * q + P], ring[:, c % SLOTS, P * q:P * q + P],
                                              ident[:])
                        mm.then_inc(s_turn, 1)

                    def project(c):
                        pe.wait_ge(s_turned, a0 + c + 1)
                        if c >= 2:
                            pe.wait_ge(s_kv, kv0 + c - 1)
                        for f in range(FT):
                            mm = pe.matmul(PS[:, 4 + c % 2, 0:B * KEYS], WT[:, c % 2, f, :], cT[:, f, :],
                                           start=(f == 0), stop=(f == FT - 1))
                        mm.then_inc(s_kv_ps, 1)

                    if layer == 0:
                        pe.wait_ge(s_const, 3)
                    pe.wait_ge(s_ctx, 16 * (layer + 1))
                    for b in range(B):
                        for f in range(FT):
                            mm = pe.transpose(PS[:, f // 2, B * KEYS * (f % 2) + KEYS * b:B * KEYS * (f % 2) + KEYS * b + KEYS],
                                              craw[0:KEYS, b, P * f:P * f + P], ident[0:KEYS, 0:KEYS])
                    mm.then_inc(s_cT_ps, 1)
                    for c in range(n_exp):
                        turn(c)
                    if layer == 1:
                        pe.wait_ge(s_small, 16 * 9)
                        for f in range(FT):
                            mm = pe.transpose(PS[:, 2, PROTOS * f:PROTOS * f + PROTOS], praw[0:PROTOS, P * f:P * f + P],
                                              ident[0:PROTOS, 0:PROTOS])
                        mm.then_inc(s_pr_ps, 1)
                        pe.wait_ge(s_pr, 2)
                        for f in range(FT):
                            mm = pe.matmul(PS[:, 3, 0:PROTOS], ones32[:], psq[:, f, :], start=(f == 0), stop=(f == FT - 1))
                        mm.then_inc(s_p2_ps, 1)
                    turn(n_exp)
                    pe.wait_ge(s_cT, layer + 1)
                    for c in range(len(chunks) - n_exp):
                        if n_exp + c + 1 < len(chunks):
                            turn(n_exp + c + 1)
                        if c < n_kv:
                            project(c)

                    pe.wait_ge(s_wq, 16 * (layer + 1))
                    pe.wait_ge(s_kv, kv0 + n_kv)
                    for u in range(units):
                        b, f = divmod(u, FT)
                        if u >= 2:
                            pe.wait_ge(s_kfl, units * layer + u - 1)
                        for p in range(HEADS // 2):
                            j, r = divmod(2 * p, hpt)
                            mm = pe.matmul(PS[:, 3 * (u % 2) + p // 3, 2 * KEYS * (p % 3):2 * KEYS * (p % 3) + 2 * KEYS],
                                           wqn[:, j, P * f:P * f + P], KBlk[layer][:, j, b, KEYS * r:KEYS * r + 2 * KEYS],
                                           start=True, stop=True)
                        mm.then_inc(s_kf_ps, 1)
                    if layer == 0:
                        for b in range(B):
                            if b == 0:
                                pe.wait_ge(s_kfl, units)
                            for p in range(HEADS // 2):
                                j, r = divmod(2 * p, hpt)
                                mm = pe.matmul(PS[:, 3 * b + p // 3, 2 * KEYS * (p % 3):2 * KEYS * (p % 3) + 2 * KEYS],
                                               bias_q[:, 0, j:j + 1].to_broadcast([P, P]),
                                               KBlk[layer][:, j, b, KEYS * r:KEYS * r + 2 * KEYS], start=True, stop=True)
                            mm.then_inc(s_row_ps, 1)

                    pe.wait_ge(s_bo, 16 * (layer + 1))
                    pe.wait_ge(s_turned, turned_all)
                    for v in range(B * ROWT):
                        b, i = divmod(v, ROWT)
                        if i == 0:
                            pe.wait_ge(s_vb, 2 * layer + b + 1)
                        if v >= 2:
                            pe.wait_ge(s_vwl, B * ROWT * layer + v - 1)
                        todo = [(VBlk[layer][:, j, P * (i - first_row_tile(layer, j)):P * (i - first_row_tile(layer, j)) + P],
                                 WOl[:, j, :]) for j in range(J) if first_row_tile(layer, j) <= i <= last_row_tile(layer, j)]
                        if i == HK // P:
                            todo.append((e80[:], BO))
                        for n, (lhsT, r) in enumerate(todo):
                            mm = pe.matmul(PS[:, G6 + v % 2, :], lhsT, r, start=(n == 0), stop=(n == len(todo) - 1))
                        mm.then_inc(s_vw_ps, 1)

                @block.vector
                def _(dve):
                    done = [sum(sc_steps[:layer])]

                    def link(ins, s=s_sc):
                        done[0] += 1
                        ins.then_inc(s, 1)
                        dve.wait_ge(s, done[0])

                    if layer == 0:
                        dve.wait_ge(s_const, 3)
                        dve.wait_ge(s_rhs, 16)
                        dve.tensor_reduce(rabs, rraw.rearrange("p f o -> p o f"), AX, ALU.max,
                                          apply_absolute_value=True).then_inc(s_rmax, 1)
                    if layer == 1:
                        expert_weights(dve, link, a0)
                    dve.wait_ge(s_zero, layer + 1)
                    for c in range(n_kv):
                        dve.wait_ge(s_kv_ps, kv0 + c + 1)
                        j = c % J
                        src = PS[:, 4 + c % 2, 0:B * KEYS].rearrange("p (b k) -> p b k", b=B)
                        if layer == 0 and c == 0:
                            dve.wait_ge(s_small, 16 * 7)
                        bias = bias_q[:, 1 + c // J, j:j + 1] if layer == 0 else None
                        if c >= J:
                            dst = VTl[layer][:, j]
                            ins = (dve.tensor_scalar(dst, src, bias, None, ALU.add) if layer == 0
                                   else dve.tensor_copy(dst, src))
                        else:
                            for r in range(hpt):
                                rows = slice(dhd * r, dhd * r + dhd)
                                dst = KBlk[layer][rows, j, :, KEYS * r:KEYS * r + KEYS]
                                ins = (dve.tensor_scalar(dst, src[rows], bias[rows], None, ALU.add) if layer == 0
                                       else dve.tensor_copy(dst, src[rows]))
                        ins.then_inc(s_kv, 1)
                    if layer == 0:
                        quantise_rhs(dve)
                    dve.wait_ge(s_wq, 16 * (layer + 1))
                    dve.tensor_reduce(amx[:, 0:1], wqn[:, 0:J, :].rearrange("p j d -> p (j d)"), AX, ALU.max,
                                      apply_absolute_value=True)
                    dve.wait_ge(s_kv, kv0 + n_kv)
                    dve.tensor_reduce(amx[:, 1:2], KB, AX, ALU.max, apply_absolute_value=True)
                    dve.tensor_reduce(amx[:, 2:3], VT[:, 0:J * B * KEYS], AX, ALU.max, apply_absolute_value=True)
                    dve.wait_ge(s_turned, turned_all)
                    dve.tensor_reduce(amx[:, 3:4], WOT[:, 0:J * D], AX, ALU.max, apply_absolute_value=True)
                    dve.wait_ge(s_bo, 16 * (layer + 1))
                    dve.tensor_reduce(amx[:, 4:5], BO, AX, ALU.max, apply_absolute_value=True).then_inc(s_am, 1)
                    dve.wait_ge(s_amr, 2 * layer + 1)
                    link(dve.tensor_scalar(sc[:, 4:9], amr[:, 0:5], TINY, None, ALU.max))
                    link(dve.tensor_tensor(sc[:, 2:3], sc[:, 4:5], sc[:, 5:6], ALU.mult))
                    link(dve.tensor_tensor(sc[:, 3:4], sc[:, 6:7], sc[:, 7:8], ALU.mult))
                    link(dve.tensor_scalar(sc[:, 2:4], sc[:, 2:4], float(dhd), None, ALU.mult))
                    link(dve.tensor_tensor(sc[:, 3:4], sc[:, 3:4], sc[:, 8:9], ALU.max))
                    link(dve.reciprocal(sc[:, 0:2], sc[:, 2:4]))
                    link(dve.tensor_scalar(sc[:, 0:2], sc[:, 0:2], WS, None, ALU.mult))
                    link(dve.tensor_scalar(sc[:, 2:3], sc[:, 2:3], scaling / (WS * XS), None, ALU.mult))
                    dve.wait_ge(s_gate, 1)
                    link(dve.tensor_scalar(sc[:, 3:4], sc[:, 3:4], 1.0 / (WS * PSC), gates[:, layer:layer + 1],
                                           ALU.mult, ALU.mult))
                    dve.tensor_scalar(sc[:, 4:5], sc[:, 0:1], XS, None, ALU.mult).then_inc(s_scale, 1)
                    for u in range(units):
                        b, f = divmod(u, FT)
                        k0 = 3 * (u % 2)
                        dve.wait_ge(s_kfh, units * layer + u + 1)
                        dve.scalar_tensor_tensor(Kf[:, b, 1, f, 0:12 * KEYS].rearrange("p (a k) -> p a k", a=2),
                                                 PS[:, k0:k0 + 2, 0:6 * KEYS], sc[:, 0:1],
                                                 Kf[:, b, 0, f, 0:12 * KEYS].rearrange("p (a k) -> p a k", a=2),
                                                 ALU.mult, ALU.subtract)
                        dve.scalar_tensor_tensor(Kf[:, b, 1, f, 12 * KEYS:HK], PS[:, k0 + 2, 0:4 * KEYS], sc[:, 0:1],
                                                 Kf[:, b, 0, f, 12 * KEYS:HK], ALU.mult, ALU.subtract).then_inc(s_kfl, 1)

                    def values_lo(v):
                        b, i = divmod(v, ROWT)
                        dve.wait_ge(s_vwh, B * ROWT * layer + v + 1)
                        dve.scalar_tensor_tensor(Vw[:, b, 1, i, :], PS[:, G6 + v % 2, :], sc[:, 1:2], Vw[:, b, 0, i, :],
                                                 ALU.mult, ALU.subtract).then_inc(s_vwl, 1)

                    for v in range(B * ROWT):
                        values_lo(v)
                    if layer == 0:
                        score_row(dve)
                        link(dve.tensor_scalar(tg[:, 5:6], tg[:, 4:5], -1.0, None, ALU.mult))
                        link(dve.tensor_tensor(tg[:, 5:6], tg[:, 5:6], tg[:, 4:5], ALU.max))
                        link(dve.tensor_scalar(tg[:, 5:6], tg[:, 5:6], 0.1, None, ALU.max))
                        dve.reciprocal(tinv[:], tg[:, 5:6])

        sc_steps = [12, 12]
        first_use = [[0] * SLOTS, [-(-(first_chunk[1] - i) // SLOTS) for i in range(SLOTS)]]

        def score_row(dve):
            n = 0

            def link(ins):
                nonlocal n
                n += 1
                ins.then_inc(s_row, 1)
                dve.wait_ge(s_row, n)

            work = WOT[:, 0:HK]
            piece = WOT[:, HK:HK + HK // 2].bitcast(BF16)
            dve.wait_ge(s_vw_ps, B * ROWT)
            for b in range(B):
                dve.wait_ge(s_row_ps, b + 1)
                dve.tensor_scalar(work[:, 0:12 * KEYS].rearrange("p (a k) -> p a k", a=2),
                                  PS[:, 3 * b:3 * b + 2, 0:6 * KEYS], sc[:, 4:5], None, ALU.mult)
                link(dve.tensor_scalar(work[:, 12 * KEYS:HK], PS[:, 3 * b + 2, 0:4 * KEYS], sc[:, 4:5], None, ALU.mult))
                for k in range(3):
                    link(dve.tensor_copy(piece, work))
                    dve.tensor_copy(row[32 * k:32 * k + 1, b, :], piece[32 * k:32 * k + 1])
                    link(dve.tensor_tensor(work, work, piece, ALU.subtract))
                dve.tensor_scalar(by_head(row[96:97, b, :]), mk[96:97, b:b + 1, :].to_broadcast([1, HEADS, KEYS]),
                                  1.0, NEG, ALU.not_equal, ALU.mult)

        def quantise_rhs(dve):
            n = 0

            def link(ins):
                nonlocal n
                n += 1
                ins.then_inc(s_rq, 1)
                dve.wait_ge(s_rq, n)

            dve.wait_ge(s_rmaxr, 1)
            dve.wait_ge(s_gate, 1)
            link(dve.tensor_scalar(cg, cg, TINY, 1.0 / INT8_MAX, ALU.max, ALU.mult))
            link(dve.reciprocal(rabs, cg))
            link(dve.tensor_tensor(rraw, rraw, rabs.unsqueeze(1).to_broadcast([P, FT, D]), ALU.mult))
            link(dve.tensor_scalar(rraw, rraw, MAGIC, MAGIC + INT8_MAX, ALU.add, ALU.min))
            link(dve.tensor_scalar(rq, rraw, MAGIC - INT8_MAX, -MAGIC, ALU.max, ALU.add))
            link(dve.tensor_scalar(cg, cg, gates[:, 2:3], None, ALU.mult))

        def expert_weights(dve, link, chunks_done):
            dve.wait_ge(s_pr_ps, 1)
            dve.tensor_copy(ptf, PS[:, 2, 0:FT * PROTOS].rearrange("p (f n) -> p f n", f=FT)).then_inc(s_pr, 1)
            dve.wait_ge(s_pr, 1)
            dve.tensor_tensor(psq, ptf, ptf, ALU.mult).then_inc(s_pr, 1)
            dve.wait_ge(s_turned, chunks_done)
            dve.tensor_reduce(amx[:, 0:1], btf.rearrange("p f n -> p (f n)"), AX, ALU.max, apply_absolute_value=True)
            dve.tensor_reduce(amx[:, 1:2], adf.rearrange("p f n -> p (f n)"), AX, ALU.max, apply_absolute_value=True)
            dve.tensor_reduce(amx[:, 2:3], ptf.rearrange("p f n -> p (f n)"), AX, ALU.max,
                              apply_absolute_value=True).then_inc(s_am, 1)
            dve.wait_ge(s_amr, 2)
            link(dve.tensor_scalar(sc[:, 11:14], amr[:, 0:3], TINY, None, ALU.max))
            link(dve.reciprocal(sc[:, 8:11], sc[:, 11:14]))
            link(dve.tensor_scalar(sc[:, 8:11], sc[:, 8:11], WS, None, ALU.mult))
            link(dve.tensor_tensor(sc[:, 11:12], sc[:, 11:12], sc[:, 12:13], ALU.mult))
            link(dve.reciprocal(sc[:, 12:13], sc[:, 11:12]))
            link(dve.tensor_scalar(sc[:, 12:13], sc[:, 12:13], HS * WS, None, ALU.mult))
            link(dve.tensor_scalar(sc[:, 11:12], sc[:, 11:12], 1.0 / (HS * WS), gates[:, 3:4], ALU.mult, ALU.mult))
            link(dve.tensor_scalar(sc[:, 13:14], sc[:, 13:14], 2.0 / (WS * XS), None, ALU.mult))
            dve.tensor_scalar(bs[0:PROTOS, :], bs[0:PROTOS, :], sc[0:PROTOS, 12:13], None, ALU.mult).then_inc(s_scale, 1)
            for n, (dst, src, k) in enumerate(((bt, btf, 8), (ad, adf, 9), (pw, ptf, 10))):
                dve.wait_ge(s_dw, n + 1)
                dve.scalar_tensor_tensor(dst[:, 1].rearrange("p f n -> p (f n)"), src.rearrange("p f n -> p (f n)"),
                                         sc[:, k:k + 1], dst[:, 0].rearrange("p f n -> p (f n)"), ALU.mult, ALU.subtract)
            dve.wait_ge(s_p2_ps, 1)
            dve.tensor_copy(p2, PS[:, 3, 0:PROTOS]).then_inc(s_dwl, 1)

        def loop(layer):
            base = TILES * layer
            fs = 0 if layer == 0 else 1

            LAST = TILES + 4
            LOOPS = ((6, PER_B, 0), (PER_B + 2, TILES, 1))

            def steps(eng, step):
                s = 0
                while s < LAST:
                    span = [x for x in LOOPS if x[0] == s]
                    if span:
                        first, end, batch = span[0]
                        with eng.Fori(0, (end - first) // 2) as i:
                            for u in range(2):
                                step(first + 2 * i + u, u, batch)
                        s = end
                    else:
                        step(s, s % 2, None)
                        s += 1

            class At:

                def __init__(self, s, u, batch, lag):
                    self.n = s - lag
                    self.u = (u - lag) % 2
                    self.on = batch is not None or 0 <= s - lag < TILES
                    self.b = batch if batch is not None else (s - lag) // PER_B

            def after(eng, name, at, back=0, per=1, alone=False):
                if isinstance(at.n, int) and at.n - back < 0:
                    return
                wait(eng, L[name], (at.n + (base_of(name) + 1 - back)) * per, alone)

            def wait(eng, signal, value, alone):
                if alone and not isinstance(value, int):
                    value = eng.snap(value)
                    eng.to_reg(value)
                    eng.wait_ge(s_const, 3)
                eng.wait_ge(signal, value)

            def base_of(name):
                shared = ("stats", "mean_var", "var_eps", "rstd", "ln", "turned", "ln_hi", "ln_lo", "scores", "max",
                          "shifted", "exp", "sum", "inv_sum", "probs", "probs_turned", "probs_hi", "probs_lo",
                          "attn_out", "x_attn", "f_stats", "f_mean_var", "f_var_eps", "f_rstd", "f_ln")
                return base if name in shared else 0

            with nc.Block() as block:
                @block.gpsimd
                def _(pool):
                    def inv_std(at, k, stage):
                        after(pool, stage + "mean_var", at, alone=True)
                        pool.tensor_scalar(rstd[:, k, at.u, 0:1], mv[:, k, at.u, 1:2], EPS, None,
                                           ALU.add).then_inc(L[stage + "var_eps"], 1)
                        after(pool, stage + "var_eps", at)
                        pool.tensor_tensor(rstd[:, k, at.u, 1:2], rstd[:, k, at.u, 0:1], half[:, 0:1],
                                           ALU.pow).then_inc(L[stage + "rstd"], 1)

                    def normalise(at):
                        after(pool, "inv_sum", at)
                        pool.tensor_tensor(by_head(Pb[:, at.u, 0:HK]), by_head(Pb[:, at.u, 0:HK]),
                                           smx[:, at.u, 1, :].unsqueeze(2).to_broadcast([P, HEADS, KEYS]),
                                           ALU.mult).then_inc(L["probs"], 1)

                    def clamp(at):
                        after(pool, "quant", at, alone=True)
                        pool.tensor_scalar(xq, xq, MAGIC + INT8_MAX, MAGIC - INT8_MAX, ALU.min,
                                           ALU.max).then_inc(L["clamped"], 1)

                    def add_ffn0(at):
                        after(pool, "ffn0_scaled", at, alone=True)
                        pool.tensor_tensor(X[:, at.n, :], X[:, at.n, :], dq, ALU.add).then_inc(L["x_ffn0"], 1)

                    def route(at):
                        n = [0]

                        def link(ins):
                            n[0] += 1
                            ins.then_inc(L["route"], 1)
                            wait(pool, L["route"], at.n * 8 + n[0], True)

                        after(pool, "best_at", at, alone=True)
                        link(pool.tensor_scalar(rw[:, 0:2], m8[:, 0:2], -1.0, None, ALU.mult))
                        link(pool.tensor_tensor(rw[:, 2:4], rw[:, 0:2], half[:, 1:2].to_broadcast([P, 2]), ALU.pow))
                        pool.tensor_copy(rw[:, 4:6], i8[:, 0:2])
                        pool.tensor_tensor(rw[:, 6:7], rw[:, 2:3], rw[:, 3:4], ALU.subtract).then_inc(L["gap"], 1)
                        after(pool, "gap_exp", at, alone=True)
                        link(pool.tensor_scalar(rw[:, 8:9], rw[:, 7:8], 1.0, None, ALU.add))
                        link(pool.tensor_tensor(rw[:, 9:10], rw[:, 8:9], mone[:, 0:1], ALU.pow))
                        link(pool.tensor_tensor(rw[:, 10:11], rw[:, 9:10], rw[:, 7:8], ALU.mult))
                        link(pool.tensor_scalar(oh[:, 0], iota32[:], rw[:, 4:5], rw[:, 9:10], ALU.is_equal, ALU.mult))
                        link(pool.tensor_scalar(oh[:, 1], iota32[:], rw[:, 5:6], rw[:, 10:11], ALU.is_equal, ALU.mult))
                        after(pool, "w_T", at, back=1)
                        link(pool.tensor_tensor(wt[:], oh[:, 0], oh[:, 1], ALU.add))

                    pool.memset(Pb[:, :, HK:HK + 1], 1.0)
                    pool.memset(Pb[:, :, HK + 1:HKP], 0.0).then_inc(s_pad, 1)

                    def step(s, u, batch):
                        tile = [At(s, u, batch, k) for k in range(5)]
                        if layer == 1 and tile[4].on:
                            route(tile[4])
                        if tile[0].on:
                            inv_std(tile[0], 0, "")
                        if layer == 0 and tile[3].on:
                            clamp(tile[3])
                        if layer == 0 and tile[4].on:
                            add_ffn0(tile[4])
                        if tile[1].on:
                            normalise(tile[1])
                        if tile[2].on:
                            inv_std(tile[2], 1, "f_")
                    steps(pool, step)

                @block.scalar
                def _(act):
                    def ln_hi(at):
                        after(act, "turned", at)
                        after(act, "scores", at, back=2)
                        act.activation(xh[:, at.u].rearrange("p f t -> p (f t)"), PS[:, G6, :], ACT.Copy,
                                       scale=XS).then_inc(L["ln_hi"], 1)

                    def probs_hi(at):
                        after(act, "probs_turned", at)
                        after(act, "attn_out", at, back=1)
                        for k in range(3):
                            w = min(4, ROWT - 4 * k)
                            act.activation(pth[:, 4 * k:4 * k + w, :].rearrange("p i t -> p (i t)"),
                                           PS[:, PT_BANK + k, 0:P * w], ACT.Copy, scale=PSC).then_inc(L["probs_hi"], 1)

                    def exponentials(at):
                        after(act, "shifted", at)
                        after(act, "probs_turned", at, back=2)
                        act.activation(Pb[:, at.u, 0:HK], sS, ACT.Exp, scale=sc[:, 2:3]).then_inc(L["exp"], 1)

                    def quant_T(at):
                        after(act, "quant_turned", at)
                        act.activation(xqT.rearrange("p f t -> p (f t)"), PS[:, G7, :], ACT.Identity,
                                       bias=nmagic[:, 0:1]).then_inc(L["quant_T"], 1)

                    def gap_exp(at):
                        after(act, "gap", at)
                        act.activation(rw[:, 7:8], rw[:, 6:7], ACT.Exp, scale=tinv[:, 0:1]).then_inc(L["gap_exp"], 1)

                    def h_hi(at):
                        after(act, "h_turned", at)
                        act.copy(hh.rearrange("p f t -> p (f t)"), PS[:, G7, :]).then_inc(L["h_hi"], 1)
                        act.copy(wtT[:], W_T).then_inc(L["w_T"], 1)

                    def d_hi(at):
                        after(act, "d_turned", at)
                        act.activation(dh.rearrange("p f t -> p (f t)"), PS[:, G6, :], ACT.Copy,
                                       scale=XS).then_inc(L["d_hi"], 1)

                    def sq_sum(at):
                        after(act, "f_ln", at)
                        act.activation(junk, xf, ACT.Square, accum_out=x2[:, at.u:at.u + 1]).then_inc(L["sq_sum"], 1)

                    def step(s, u, batch):
                        tile = [At(s, u, batch, k) for k in range(5)]
                        if layer == 1 and tile[4].on:
                            gap_exp(tile[4])
                        if layer == 1 and tile[3].on:
                            sq_sum(tile[3])
                        if tile[2].on:
                            probs_hi(tile[2])
                        if layer == 0 and tile[3].on:
                            quant_T(tile[3])
                        if layer == 0 and tile[0].on:
                            ln_hi(tile[0])
                        if layer == 1 and tile[3].on:
                            d_hi(tile[3])
                        if layer == 1 and tile[4].on:
                            h_hi(tile[4])
                        if tile[1].on:
                            exponentials(tile[1])
                        if layer == 1 and tile[0].on:
                            ln_hi(tile[0])
                    steps(act, step)

                @block.tensor
                def _(pe):
                    def turn_ln(at, routed):
                        after(pe, "ln", at)
                        if layer == 1 and routed.on:
                            after(pe, "dist_a", routed)
                        after(pe, "ln_lo", at, back=1)
                        for f in range(FT):
                            mm = pe.transpose(PS[:, G6, P * f:P * f + P], xn[:, at.u, P * f:P * f + P], ident[:])
                        mm.then_inc(L["turned"], 1)

                    def scores(at, part):
                        if part == 0:
                            after(pe, "ln_lo", at)
                            after(pe, "shifted", at, back=1)
                            if layer == 0:
                                for k in range(3):
                                    pe.matmul(scores_bank(k), ones16[:], row[:, at.b, KEYS * 6 * k:KEYS * 6 * k + KEYS * BANK_HEADS[k]],
                                              start=True, stop=False)
                        for f in range(2 * part, 2 * part + 2):
                            for w, half_x in ((0, xh), (1, xh), (0, xl)):
                                for k in range(3):
                                    c = 6 * KEYS * k
                                    mm = pe.matmul(scores_bank(k), half_x[:, at.u, f, :],
                                                   Kf[:, at.b, w, f, c:c + KEYS * BANK_HEADS[k]],
                                                   start=(layer == 1 and f == 0 and w == 0 and half_x is xh),
                                                   stop=(f == FT - 1 and half_x is xl))
                        if part == 1:
                            mm.then_inc(L["scores"], 1)

                    def turn_probs(at):
                        after(pe, "probs", at)
                        after(pe, "x_attn", at, back=1)
                        if layer == 1:
                            after(pe, "x_ffn1", at, back=3)
                        for i in range(ROWT):
                            mm = pe.transpose(PS[:, PT_BANK + i // 4, P * (i % 4):P * (i % 4) + P],
                                              Pb[:, at.u, P * i:P * i + P], ident[:])
                        mm.then_inc(L["probs_turned"], 1)

                    def attn_out(at):
                        after(pe, "probs_hi", at, per=3)
                        after(pe, "probs_lo", at, per=3)
                        for w, half_p in ((0, pth), (1, pth), (0, ptl)):
                            for i in range(ROWT):
                                mm = pe.matmul(PS[:, PT_BANK, :], half_p[:, i, :], Vw[:, at.b, w, i, :],
                                               start=(w == 0 and half_p is pth and i == 0),
                                               stop=(half_p is ptl and i == ROWT - 1))
                        mm.then_inc(L["attn_out"], 1)

                    def turn_quant(at):
                        after(pe, "clamped", at)
                        after(pe, "ffn0_scaled", at, back=1)
                        for f in range(FT):
                            mm = pe.transpose(PS[:, G7, P * f:P * f + P], xq[:, P * f:P * f + P], ident[:])
                        mm.then_inc(L["quant_turned"], 1)

                    def ffn0_out(at):
                        after(pe, "quant_T", at)
                        for f in range(FT):
                            mm = pe.matmul(PS[:, G7, :], xqT[:, f, :], rq[:, f, :], start=(f == 0), stop=(f == FT - 1))
                        mm.then_inc(L["ffn0_out"], 1)

                    def turn_hidden(at, newest):
                        after(pe, "weighted", at)
                        for f in range(FT):
                            pe.transpose(PS[:, G7, P * f:P * f + P], hw[:, P * f:P * f + P], ident[:])
                        if newest.on:
                            after(pe, "probs_lo", newest, per=3)
                        mm = pe.transpose(W_T, wt[:], ident[:])
                        mm.then_inc(L["h_turned"], 1)

                    def turn_d(at):
                        after(pe, "f_ln", at)
                        for f in range(FT):
                            mm = pe.transpose(PS[:, G6, P * f:P * f + P], xf[:, P * f:P * f + P], ident[:])
                        mm.then_inc(L["d_turned"], 1)

                    def three(outp, hi, lo, w, start=True, stop=True):
                        for f in range(FT):
                            pe.matmul(outp, hi[:, f, :], w[:, 0, f, :], start=(start and f == 0), stop=False)
                            pe.matmul(outp, hi[:, f, :], w[:, 1, f, :], start=False, stop=False)
                            mm = pe.matmul(outp, lo[:, f, :], w[:, 0, f, :], start=False, stop=(stop and f == FT - 1))
                        return mm

                    def hidden(at):
                        after(pe, "d_lo", at)
                        after(pe, "h_lo", at, back=1)
                        three(PS[:, G6, 0:PROTOS], dh, dl, pw).then_inc(L["dots"], 1)
                        three(PS[:, G7, :], dh, dl, bt).then_inc(L["hidden"], 1)

                    def ffn1_out(at):
                        after(pe, "w_T", at)
                        after(pe, "h_lo", at)
                        pe.matmul(FFN1, wtT[:], bs[0:PROTOS, :], start=True, stop=False)
                        three(FFN1, hh, hl, ad, start=False).then_inc(L["ffn1_out"], 1)

                    pe.wait_ge(s_pad, layer + 1)

                    def step(s, u, batch):
                        tile = [At(s, u, batch, k) for k in range(5)]
                        if tile[1].on:
                            scores(tile[1], 0)
                        if tile[2].on:
                            turn_probs(tile[2])
                        if tile[1].on:
                            scores(tile[1], 1)
                        if layer == 0 and tile[3].on:
                            turn_quant(tile[3])
                        if layer == 0 and tile[0].on:
                            turn_ln(tile[0], tile[3])
                        if layer == 1 and tile[3].on:
                            turn_d(tile[3])
                        if layer == 1 and tile[4].on:
                            turn_hidden(tile[4], tile[2])
                        if tile[2].on:
                            attn_out(tile[2])
                        if layer == 0 and tile[3].on:
                            ffn0_out(tile[3])
                        if layer == 1 and tile[3].on:
                            hidden(tile[3])
                        if layer == 1 and tile[0].on:
                            turn_ln(tile[0], tile[3])
                        if layer == 1 and tile[4].on:
                            ffn1_out(tile[4])
                    steps(pe, step)

                @block.vector
                def _(dve):
                    def statistics(at, k, stage, src):
                        if src:
                            after(dve, src, at, alone=True)
                        dve.bn_stats(st[:, k, at.u, :], X[:, at.n, :]).then_inc(L[stage + "stats"], 1)
                        after(dve, stage + "stats", at, alone=True)
                        dve.bn_aggr(mv[:, k, at.u, :], st[:, k, at.u, :]).then_inc(L[stage + "mean_var"], 1)

                    def layernorm(at, k, stage, dst, used):
                        after(dve, stage + "rstd", at)
                        for name, back in used:
                            after(dve, name, at, back=back)
                        dve.tensor_scalar(dst, X[:, at.n, :], mv[:, k, at.u, 0:1], rstd[:, k, at.u, 1:2],
                                          ALU.subtract, ALU.mult).then_inc(L[stage + "ln"], 1)

                    def ln_lo(at):
                        after(dve, "ln_hi", at)
                        dve.scalar_tensor_tensor(xl[:, at.u].rearrange("p f t -> p (f t)"), PS[:, G6, :], XS,
                                                 xh[:, at.u].rearrange("p f t -> p (f t)"), ALU.mult,
                                                 ALU.subtract).then_inc(L["ln_lo"], 1)

                    def shift_scores(at):
                        after(dve, "scores", at)
                        for n, (ps, cols, heads, shape) in enumerate(scores_parts()):
                            ins = dve.tensor_reduce(cut(mx[:, at.u, heads], shape), ps, AX, ALU.max)
                        ins.then_inc(L["max"], 1)
                        after(dve, "max", at)
                        after(dve, "exp", at, back=1)
                        for ps, cols, heads, shape in scores_parts():
                            o = sS[:, cols].rearrange("p (a h k) -> p a h k", a=2, k=KEYS) if len(shape) == 2 else by_head(sS[:, cols])
                            m = cut(mx[:, at.u, heads], shape)
                            m = m.unsqueeze(len(shape) + 1).to_broadcast([P, *shape, KEYS])
                            ins = dve.tensor_tensor(o, ps, m, ALU.subtract)
                        ins.then_inc(L["shifted"], 1)

                    def sums(at):
                        after(dve, "exp", at)
                        dve.tensor_reduce(smx[:, at.u, 0, :], by_head(Pb[:, at.u, 0:HK]), AX, ALU.add).then_inc(L["sum"], 1)
                        after(dve, "sum", at)
                        dve.reciprocal(smx[:, at.u, 1, :], smx[:, at.u, 0, :]).then_inc(L["inv_sum"], 1)

                    def probs_lo(at):
                        for k in range(3):
                            w = min(4, ROWT - 4 * k)
                            dve.wait_ge(L["probs_hi"], (at.n + base) * 3 + (k + 1))
                            dve.scalar_tensor_tensor(ptl[:, 4 * k:4 * k + w, :].rearrange("p i t -> p (i t)"),
                                                     PS[:, PT_BANK + k, 0:P * w], PSC,
                                                     pth[:, 4 * k:4 * k + w, :].rearrange("p i t -> p (i t)"),
                                                     ALU.mult, ALU.subtract).then_inc(L["probs_lo"], 1)

                    def add_attn(at):
                        after(dve, "attn_out", at)
                        dve.scalar_tensor_tensor(X[:, at.n, :], PS[:, PT_BANK, :], sc[:, 3:4], X[:, at.n, :], ALU.mult,
                                                 ALU.add).then_inc(L["x_attn"], 1)

                    def lhs_scales(at):
                        after(dve, "f_ln", at)
                        dve.tensor_reduce(lsb[:, at.u, 0:1], xf, AX, ALU.max, apply_absolute_value=True).then_inc(L["absmax"], 1)
                        after(dve, "absmax", at)
                        dve.tensor_scalar(lsb[:, at.u, 1:2], lsb[:, at.u, 0:1], TINY, 1.0 / INT8_MAX, ALU.max,
                                          ALU.mult).then_inc(L["lhs_scale"], 1)
                        after(dve, "lhs_scale", at)
                        dve.reciprocal(lsb[:, at.u, 2:3], lsb[:, at.u, 1:2]).then_inc(L["lhs_inv"], 1)

                    def quantise(at):
                        after(dve, "lhs_inv", at)
                        after(dve, "quant_turned", at, back=1)
                        dve.tensor_scalar(xq, xf, lsb[:, at.u, 2:3], MAGIC, ALU.mult, ALU.add).then_inc(L["quant"], 1)

                    def scale_ffn0(at):
                        after(dve, "ffn0_out", at)
                        after(dve, "x_ffn0", at, back=1)
                        dve.scalar_tensor_tensor(dq, PS[:, G7, :], lsb[:, at.u, 1:2], cg, ALU.mult,
                                                 ALU.mult).then_inc(L["ffn0_scaled"], 1)

                    def weigh_hidden(at):
                        dve.wait_ge(L["route"], at.n * 8 + 8)
                        after(dve, "hidden", at)
                        dve.scalar_tensor_tensor(hw.rearrange("p (n r) -> p n r", r=RANK),
                                                 PS[:, G7, :].rearrange("p (n r) -> p n r", r=RANK), HS / (WS * XS),
                                                 wt[:].unsqueeze(2).to_broadcast([P, PROTOS, RANK]), ALU.mult,
                                                 ALU.mult).then_inc(L["weighted"], 1)

                    def h_lo(at):
                        after(dve, "h_hi", at)
                        dve.tensor_tensor(hl.rearrange("p f t -> p (f t)"), PS[:, G7, :], hh.rearrange("p f t -> p (f t)"),
                                          ALU.subtract).then_inc(L["h_lo"], 1)

                    def d_lo(at):
                        after(dve, "d_hi", at)
                        dve.scalar_tensor_tensor(dl.rearrange("p f t -> p (f t)"), PS[:, G6, :], XS,
                                                 dh.rearrange("p f t -> p (f t)"), ALU.mult,
                                                 ALU.subtract).then_inc(L["d_lo"], 1)

                    def add_ffn1(at):
                        after(dve, "ffn1_out", at)
                        dve.scalar_tensor_tensor(X[:, at.n, :], FFN1, sc[:, 11:12], X[:, at.n, :], ALU.mult,
                                                 ALU.add).then_inc(L["x_ffn1"], 1)

                    def nearest(at):
                        after(dve, "dots", at)
                        after(dve, "best_at", at, back=1)
                        dve.scalar_tensor_tensor(rt[:, 0], PS[:, G6, 0:PROTOS], sc[:, 13:14], p2, ALU.mult,
                                                 ALU.subtract).then_inc(L["dist_a"], 1)
                        after(dve, "dist_a", at)
                        after(dve, "sq_sum", at)
                        dve.tensor_scalar(rt[:, 1], rt[:, 0], x2[:, at.u:at.u + 1], 0.0, ALU.subtract,
                                          ALU.min).then_inc(L["dist_b"], 1)
                        after(dve, "dist_b", at, alone=True)
                        dve.max(m8[:], rt[:, 1]).then_inc(L["best"], 1)
                        after(dve, "best", at, alone=True)
                        dve.max_index(i8[:], m8[:], rt[:, 1]).then_inc(L["best_at"], 1)

                    if layer == 0:
                        dve.wait_ge(s_x, 16)

                    def step(s, u, batch):
                        tile = [At(s, u, batch, k) for k in range(5)]
                        if tile[0].on:
                            statistics(tile[0], 0, "", None)
                        if layer == 1 and tile[4].on:
                            weigh_hidden(tile[4])
                        if tile[3].on and layer == 0:
                            layernorm(tile[3], 1, "f_", xf, [("quant", 1)])
                            lhs_scales(tile[3])
                            quantise(tile[3])
                        if layer == 1 and tile[3].on:
                            layernorm(tile[3], 1, "f_", xf, [("d_turned", 1), ("sq_sum", 1)])
                        if tile[0].on:
                            layernorm(tile[0], 0, "", xn[:, tile[0].u, :], [("turned", 2)])
                        if tile[2].on:
                            probs_lo(tile[2])
                        if tile[1].on:
                            shift_scores(tile[1])
                        if layer == 0 and tile[0].on:
                            ln_lo(tile[0])
                        if layer == 1 and tile[3].on:
                            d_lo(tile[3])
                        if layer == 1 and tile[4].on:
                            h_lo(tile[4])
                        if tile[1].on:
                            sums(tile[1])
                        if tile[2].on:
                            add_attn(tile[2])
                            statistics(tile[2], 1, "f_", "x_attn")
                        if layer == 0 and tile[3].on:
                            scale_ffn0(tile[3])
                        if layer == 1 and tile[3].on:
                            nearest(tile[3])
                        if layer == 1 and tile[0].on:
                            ln_lo(tile[0])
                        if layer == 1 and tile[4].on:
                            add_ffn1(tile[4])
                    steps(dve, step)

                if layer == 1:
                    @block.sync
                    def _(sp):
                        rows = out.rearrange("b (t p) d -> p (b t) d", p=P)
                        with sp.Fori(0, TILES) as t:
                            sp.wait_ge(L["x_ffn1"], t + 1)
                            sp.dma_start(rows[:, t, :], X[:, t, :]).then_inc(L["stored"], 16)
                        sp.wait_ge(L["stored"], 16 * TILES)

        setup(0)
        loop(0)
        setup(1)
        loop(1)


_INS = ['x', 'ctx_1024', 'mask_BxS2_ff1', 'g_xattn', 'g_ffn', 'L0_xattn_Wq', 'L0_xattn_bq', 'L0_xattn_Wk', 'L0_xattn_bk',
        'L0_xattn_Wv', 'L0_xattn_bv', 'L0_xattn_Wo', 'L0_xattn_bo', 'L0_ffn_rhs', 'L1_xattn_Wq', 'L1_xattn_Wk',
        'L1_xattn_Wv', 'L1_xattn_Wo', 'L1_xattn_bo', 'L1_ffn_prototypes', 'L1_ffn_B', 'L1_ffn_A', 'L1_ffn_bias',
        'L1_ffn_temp']


def kernel(**inputs):
    import numpy as _np
    import concourse.bacc as _bacc
    from concourse.bass_utils import run_bass_kernel_spmd as _run

    nc = _bacc.Bacc("TRN2", target_bir_lowering=False, num_devices=1)
    arrays, args = {}, []
    for name in _INS:
        a = _np.ascontiguousarray(inputs[name])
        a = a.reshape(a.shape or (1,))
        arrays[f"in_{name}"] = a
        args.append(nc.dram_tensor(f"in_{name}", a.shape, F32, kind="ExternalInput").ap())
    args.append(nc.dram_tensor("out", (B, T, D), F32, kind="ExternalOutput").ap())
    build(nc, *args)
    return _run(nc, [arrays], core_ids=[0]).results[0]["out"]
```

```python
from contextlib import ExitStack

import concourse.bass as bass
from concourse import mybir

P = 128
D = 512
FT = D // P
B, T = 2, 2048
TILES = B * T // P
PER_B = T // P
HEADS = 16
KEYS = 77
HK = HEADS * KEYS
BANK_HEADS = (6, 6, 4)
ROWT = (HK + 1 + P - 1) // P
HKP = ROWT * P
PROTOS, RANK = 32, 16
EPS = 1e-5
TINY = 1e-12
INT8_MAX = 127.0
MAGIC = 1.5 * 2.0 ** 23
NEG = -(2.0 ** 127)
XS = 2.0 ** 11
PSC = 2.0 ** 15
WS = 2.0 ** 14
HS = 2.0 ** 6
WTS = 2.0 ** 5
SLOTS = 6
ARENA_WORDS = 60 * 256

ALU = mybir.AluOpType
ACT = mybir.ActivationFunctionType
AX = mybir.AxisListType.X
F32 = mybir.dt.float32
F16 = mybir.dt.float16
BF16 = mybir.dt.bfloat16
U32 = mybir.dt.uint32
RMAX = bass.bass_isa.ReduceOp.max


def build(nc, x, ctx_in, mask, g_xattn, g_ffn, Wq0, bq0, Wk0, bk0, Wv0, bv0, Wo0, bo0, rhs,
          Wq1, Wk1, Wv1, Wo1, bo1, protos, Bw, Aw, biasw, temp, out):
    with ExitStack() as ctx:
        def sb(name, shape, dt=F32):
            return ctx.enter_context(nc.sbuf_tensor(name, shape, dt))

        def sem(name):
            return ctx.enter_context(nc.semaphore(name))

        PS = ctx.enter_context(nc.psum_tensor("PS", [P, 8, 512], F32))
        S_BANK, G6 = 0, 6
        ATTN, FFN0, HIDDEN, DOTS, FFN1 = (PS[:, k, :] for k in (3, 4, 4, 5, 6))

        X = sb("X", [P, TILES, D])
        KF = sb("KF", [P, B * 2 * FT * HK], F16)
        VW = sb("VW", [P, B * 2 * ROWT * D], F16)
        Kf = KF[:, :].rearrange("p (b w f k) -> p b w f k", b=B, w=2, f=FT)
        Vw = VW[:, :].rearrange("p (b w i o) -> p b w i o", b=B, w=2, i=ROWT)

        ARENA = sb("ARENA", [P, ARENA_WORDS])
        at = [0]

        def arena(words, dt=F32, start=None):
            a = at[0] if start is None else start
            at[0] = a + words
            assert at[0] <= ARENA_WORDS
            return ARENA[:, a:a + words] if dt == F32 else ARENA[:, a:a + words].bitcast(dt)

        xn = arena(D)
        xs = arena(D, F16).rearrange("p (w d) -> p w d", w=2)
        xT = arena(D, F16).rearrange("p (w f t) -> p w f t", w=2, f=FT)
        sS = arena(HK)
        ps = arena(HKP, F16).rearrange("p (w k) -> p w k", w=2)
        pT = arena(HKP, F16).rearrange("p (w i t) -> p w i t", w=2, i=ROWT)
        xf = arena(D)
        ffn = at[0]
        xq = arena(D)
        qs = arena(D // 2, F16)
        qT = arena(D // 2, F16).rearrange("p (f t) -> p f t", f=FT)
        dq = arena(D)
        loop_end = [at[0]]
        ds = arena(D, F16, start=ffn).rearrange("p (w d) -> p w d", w=2)
        dT = arena(D, F16).rearrange("p (w f t) -> p w f t", w=2, f=FT)
        hw = arena(D)
        hs = arena(D + P // 2, F16)
        hT = arena(D + P // 2, F16).rearrange("p (i t) -> p i t", t=P)
        junk = arena(D // 2, F16)
        loop_end.append(at[0])
        rq = arena(FT * D // 2, F16, start=loop_end[0]).rearrange("p (f o) -> p f o", f=FT)
        cg = arena(D)
        row = arena(B * HK // 2, BF16).rearrange("p (b k) -> p b k", b=B)
        spare = at[0]
        early = arena(2 * FT * D).rearrange("p (c d) -> p c d", c=2 * FT)
        rraw = arena(FT * D, start=spare).rearrange("p (f o) -> p f o", f=FT)
        rabs = arena(D)
        rest = arena(HK, start=spare)
        bt = arena(FT * D, F16, start=loop_end[1]).rearrange("p (w f n) -> p w f n", w=2, f=FT)
        ad = arena(FT * D, F16).rearrange("p (w f n) -> p w f n", w=2, f=FT)
        pw = arena(FT * PROTOS, F16).rearrange("p (w f n) -> p w f n", w=2, f=FT)
        p2 = arena(PROTOS)
        bs = arena(D // 2, F16)
        bsf = arena(D)

        VB = arena(8 * 384, start=0)
        VT = arena(8 * B * KEYS)
        WOT = arena(8 * D).rearrange("p (j d) -> p j d", j=8)
        assert at[0] <= loop_end[1]
        BO = arena(D, start=spare + 2 * FT * D)
        f32vw = VW[:, :].bitcast(F32)
        ring = f32vw[:, 0:SLOTS * D].rearrange("p (s d) -> p s d", s=SLOTS)
        wqn = f32vw[:, SLOTS * D:SLOTS * D + 8 * D].rearrange("p (j d) -> p j d", j=8)
        KB = f32vw[:, SLOTS * D + 8 * D:SLOTS * D + 8 * D + HEADS * B * KEYS]
        f32kf = KF[:, :].bitcast(F32)
        craw = f32kf[:, 0:B * D].rearrange("p (b d) -> p b d", b=B)
        cT = f32kf[:, 1024:1024 + FT * B * KEYS].rearrange("p (f k) -> p f k", f=FT)
        WT = f32kf[:, 2048:2048 + 2 * D].rearrange("p (u f n) -> p u f n", u=2, f=FT)
        btf = f32kf[:, 3072:3072 + FT * D].rearrange("p (f n) -> p f n", f=FT)
        adf = f32kf[:, 5120:5120 + FT * D].rearrange("p (f n) -> p f n", f=FT)
        ptf = f32kf[:, 7168:7168 + FT * PROTOS].rearrange("p (f n) -> p f n", f=FT)
        psq = f32kf[:, 7296:7296 + FT * PROTOS].rearrange("p (f n) -> p f n", f=FT)
        praw = f32kf[:, 7424:7424 + D]

        ident = sb("ident", [P, P])
        sel16 = sb("sel16", [P, P], BF16)
        ones32 = sb("ones32", [P, P])
        e80 = sb("e80", [P, P])
        iota32 = sb("iota32", [P, PROTOS])
        gates = sb("gates", [P, 4])
        tinv = sb("tinv", [P, 1])
        nmagic = sb("nmagic", [P, 1])
        half = sb("half", [P, 2])
        mone = sb("mone", [P, 1])
        bias_q = sb("bias_q", [P, 3, 4])
        mk = sb("mk", [P, B, KEYS])
        amx = sb("amx", [P, 5, 8])
        amr = sb("amr", [P, 5, 8])
        amxe = sb("amxe", [P, 4])
        amre = sb("amre", [P, 4])
        sc = sb("sc", [P, 16])
        st = sb("st", [P, 2, 2, 6])
        mv = sb("mv", [P, 2, 2, 2])
        rstd = sb("rstd", [P, 2, 2, 2])
        mx = sb("mx", [P, 2, HEADS])
        smx = sb("smx", [P, 2, 2, HEADS])
        lsb = sb("lsb", [P, 2, 4])
        rt = sb("rt", [P, 2, PROTOS])
        m8 = sb("m8", [P, 8])
        i8 = sb("i8", [P, 8], U32)
        rw = sb("rw", [P, 16])
        x2 = sb("x2", [P, 2])
        oh = sb("oh", [P, 2, PROTOS])
        wt = sb("wt", [P, PROTOS])
        tg = sb("tg", [P, 8])

        def tiles_of(layer):
            return 4 * (layer + 1)

        def per_tile(layer):
            return HEADS // tiles_of(layer)

        def first_row_tile(layer, j):
            return per_tile(layer) * KEYS * j // P

        def last_row_tile(layer, j):
            return (per_tile(layer) * KEYS * (j + 1) - 1) // P

        def window(layer):
            return 512 if layer == 0 else 384

        def scores_bank(k):
            return PS[:, S_BANK + k, 0:BANK_HEADS[k] * KEYS]

        def by_head(ap):
            return ap.rearrange("p (h k) -> p h k", k=KEYS)

        def scores_parts():
            two = PS[:, S_BANK:S_BANK + 2, 0:6 * KEYS].rearrange("p b (h k) -> p b h k", k=KEYS)
            return [(two, slice(0, 12 * KEYS), slice(0, 12), (2, 6)),
                    (by_head(PS[:, S_BANK + 2, 0:4 * KEYS]), slice(12 * KEYS, HK), slice(12, 16), (4,))]

        def cut(ap, shape):
            return ap.rearrange("p (a b) -> p a b", a=shape[0]) if len(shape) == 2 else ap

        KBlk = [KB.rearrange("p (j b k) -> p j b k", j=tiles_of(l), b=B) for l in range(2)]
        VBlk = [VB[:, 0:tiles_of(l) * window(l)].rearrange("p (j c) -> p j c", j=tiles_of(l)) for l in range(2)]
        VTl = [VT[:, 0:tiles_of(l) * B * KEYS].rearrange("p (j b k) -> p j b k", j=tiles_of(l), b=B) for l in range(2)]

        s_const = sem("consts_made")
        s_constv = sem("scalar_inputs_used")
        s_x = sem("x_loaded")
        s_small = sem("small_inputs_loaded")
        s_ctx = sem("context_loaded")
        s_slot = [sem(f"chunk_slot{i}_loaded") for i in range(SLOTS)]
        s_wq = sem("wq_loaded")
        s_early = sem("experts_loaded")
        s_praw = sem("prototypes_loaded")
        s_bo = sem("bo_loaded")
        s_zero = sem("setup_zeroed")
        s_pad = sem("probs_padded")
        s_cT_ps = sem("context_turned")
        s_cT = sem("context_turned_copied")
        s_turn = sem("chunk_turned")
        s_turned = sem("chunk_turned_copied")
        s_kv_ps = sem("kv_projected")
        s_kv = sem("kv_copied")
        s_am = sem("absmax_per_partition")
        s_amr = sem("absmax_over_partitions")
        s_ame = sem("expert_absmax_per_partition")
        s_amre = sem("expert_absmax_over_partitions")
        s_sc = sem("scales_step")
        s_scale = sem("scales_ready")
        s_escale = sem("expert_scales_ready")
        s_kf_ps = sem("folded_keys_product")
        s_kfh = sem("folded_keys_hi")
        s_kfl = sem("folded_keys_lo")
        s_vb = sem("value_window_filled")
        s_vw_ps = sem("folded_values_product")
        s_vwh = sem("folded_values_hi")
        s_vwl = sem("folded_values_lo")
        s_row_ps = sem("score_row_product")
        s_row = sem("score_row_step")
        s_rhs = sem("rhs_loaded")
        s_rmax = sem("rhs_absmax")
        s_rmaxr = sem("rhs_absmax_over_partitions")
        s_rq = sem("rhs_step")
        s_pr_ps = sem("prototypes_turned")
        s_pr = sem("prototypes_step")
        s_p2_ps = sem("prototype_norms")
        s_dw = sem("expert_weights_hi")
        s_dwl = sem("expert_weights_lo")
        s_gate = sem("gates_ready")

        L = {}
        for name in ("stats", "mean_var", "var_eps", "rstd", "ln", "ln_hi", "ln_lo", "x_T", "scores", "max",
                     "shifted", "exp", "sum", "inv_sum", "probs", "probs_hi", "probs_lo", "p_T_hi", "p_T_lo", "attn_out",
                     "x_attn", "f_stats", "f_mean_var", "f_var_eps", "f_rstd", "f_ln", "absmax", "lhs_scale",
                     "lhs_inv", "quant", "clamped", "quant_int", "q_T", "ffn0_out", "ffn0_scaled", "x_ffn0",
                     "sq_sum", "d_hi", "d_lo", "d_T", "hidden", "dots", "dist_a", "dist_b", "best", "best_at",
                     "route", "gap", "gap_exp", "weighted", "h_hi", "w_hi", "h_lo", "w_lo", "h_T", "ffn1_out",
                     "x_ffn1", "stored"):
            L[name] = sem(name)

        def chunk_list(layer):
            n = tiles_of(layer)
            wk, wv, wo = ((Wk0, Wv0, Wo0), (Wk1, Wv1, Wo1))[layer]
            src = [w[P * j:P * j + P, :] for w in (wk, wv) for j in range(n)]
            src += [wo[:, P * j:P * j + P].rearrange("(q p) c -> p q c", p=P) for j in range(n)]
            return src

        first_load = [0, 3 * tiles_of(0)]
        n_exp = [0, 2 * FT]
        first_turn = [0, 3 * tiles_of(0) + n_exp[1]]
        first_kv = [0, 2 * tiles_of(0)]
        first_vb = [0, B * tiles_of(0)]
        first_link = [0, 13]
        units = B * FT
        x_parts = 4
        VALUE_BANKS = 5
        LN_AT = B * ROWT - 5

        def values_bank(v):
            return 8 - VALUE_BANKS + v % VALUE_BANKS


        def setup(layer):
            J, hpt = tiles_of(layer), per_tile(layer)
            dhd = P // hpt
            chunks = chunk_list(layer)
            n_kv = 2 * J
            l0 = first_load[layer]
            a0 = first_turn[layer]
            e0 = a0 - n_exp[layer]
            turned_all = a0 + len(chunks)
            kv0 = first_kv[layer]
            vb0 = first_vb[layer]
            vw0 = B * ROWT * layer
            n0 = TILES * layer
            scaling = float(dhd) ** -0.5
            wq = (Wq0, Wq1)[layer]
            bo = (bo0, bo1)[layer]

            with nc.Block() as block:
                @block.sync
                def _(sp):
                    sp.dma_start(craw[0:KEYS], ctx_in.rearrange("b k d -> k b d")).then_inc(s_ctx, 16)
                    for c, src in enumerate(chunks):
                        if c >= SLOTS:
                            sp.wait_ge(s_turn, a0 + c - SLOTS + 1)
                        dst = ring[:, c % SLOTS, :]
                        if c >= n_kv:
                            dst = dst.rearrange("p (q c) -> p q c", q=FT)
                        sp.dma_start(dst, src).then_inc(s_slot[c % SLOTS], 16)
                    if layer == 0:
                        rows = x.rearrange("b (t p) d -> p (b t) d", p=P)
                        n = TILES // x_parts
                        for k in range(x_parts):
                            sp.dma_start(X[:, n * k:n * k + n, :], rows[:, n * k:n * k + n, :]).then_inc(s_x, 16)
                    sp.wait_ge(L["ln_lo"], n0 + 1)
                    sp.dma_start_transpose(xT.rearrange("p w f t -> p (w f) t"),
                                           xs.rearrange("p w d -> p (w d)")).then_inc(L["x_T"], 16)

                @block.gpsimd
                def _(pool):
                    if layer == 0:
                        pool.memset(ident[:], 0.0).then_inc(s_const, 1)
                        pool.memset(e80[:], 0.0).then_inc(s_const, 1)
                        pool.memset(sel16[:], 0.0).then_inc(s_const, 1)
                        pool.wait_ge(s_const, 3)
                        pool.affine_select(out=ident[:], in_=ident[:], compare_op=ALU.not_equal, fill=1.0, base=0,
                                           pattern=[[-1, P]], channel_multiplier=1)
                        pool.affine_select(out=e80[:], in_=e80[:], compare_op=ALU.not_equal, fill=1.0,
                                           base=-(HK % P), pattern=[[1, P]],
                                           channel_multiplier=P).then_inc(s_const, 1)
                        pool.memset(amx[:], 0.0)
                        pool.memset(amxe[:], 0.0)
                    pool.memset(BO, 0.0)
                    pool.memset(KB, 0.0).then_inc(s_zero, 1)
                    if layer == 0:
                        pool.memset(ones32[:], 1.0)
                        pool.memset(nmagic[:], -MAGIC)
                        pool.memset(half[:, 0:1], -0.5)
                        pool.memset(half[:, 1:2], 0.5)
                        pool.memset(mone[:], -1.0)
                        pool.iota(iota32[:], [[1, PROTOS]], base=0, channel_multiplier=0,
                                  allow_small_or_imprecise_dtypes=True)
                    pool.memset(VB[:, 0:J * window(layer)], 0.0).then_inc(s_zero, 1)
                    pool.wait_ge(s_zero, 2 * layer + 2)

                    def fill_window(b, j):
                        off = hpt * KEYS * j - P * first_row_tile(layer, j)
                        for r in range(hpt):
                            rows = slice(dhd * r, dhd * r + dhd)
                            last = pool.tensor_copy(VBlk[layer][rows, j, off + KEYS * r:off + KEYS * r + KEYS],
                                                    VTl[layer][rows, j, b, :])
                        last.then_inc(s_vb, 1)

                    for j in range(J):
                        if layer == 1 and j == 0:
                            pool.wait_ge(s_ame, 1)
                            pool.partition_all_reduce(amre[:], amxe[:], P, RMAX).then_inc(s_amre, 1)
                            pool.wait_ge(s_amre, 1)
                        pool.wait_ge(s_kv, kv0 + J + j + 1)
                        fill_window(0, j)
                    pool.wait_ge(s_vb, vb0 + J)
                    for n, kinds in enumerate((slice(0, 2), slice(2, 5))):
                        pool.wait_ge(s_am, 2 * layer + n + 1)
                        pool.partition_all_reduce(amr[:, kinds].rearrange("p a b -> p (a b)"),
                                                  amx[:, kinds].rearrange("p a b -> p (a b)"),
                                                  P, RMAX).then_inc(s_amr, 1)
                        pool.wait_ge(s_amr, 2 * layer + n + 1)
                    if layer == 0:
                        pool.wait_ge(s_rmax, 1)
                        pool.partition_all_reduce(cg, rabs, P, RMAX).then_inc(s_rmaxr, 1)
                        pool.wait_ge(s_rmaxr, 1)
                    for j in range(J):
                        pool.wait_ge(s_vw_ps, vw0 + last_row_tile(layer, j) + 1)
                        fill_window(1, j)
                    pool.wait_ge(s_vb, vb0 + B * J)
                    pool.wait_ge(L["mean_var"], n0 + 1)
                    pool.tensor_scalar(rstd[:, 0, 0, 0:1], mv[:, 0, 0, 1:2], EPS, None, ALU.add).then_inc(L["var_eps"], 1)
                    pool.wait_ge(L["var_eps"], n0 + 1)
                    pool.tensor_tensor(rstd[:, 0, 0, 1:2], rstd[:, 0, 0, 0:1], half[:, 0:1],
                                       ALU.pow).then_inc(L["rstd"], 1)

                @block.scalar
                def _(act):
                    if layer == 0:
                        act.dma_start(wqn[:, 0:J, :], wq.rearrange("(j p) d -> p j d", p=P)).then_inc(s_wq, 16)
                        act.dma_start(tg[:, 0:2], g_xattn.partition_broadcast(P)).then_inc(s_small, 16)
                        act.dma_start(tg[:, 2:4], g_ffn.partition_broadcast(P)).then_inc(s_small, 16)
                        act.dma_start(tg[:, 4:5], temp.partition_broadcast(P)).then_inc(s_small, 16)
                        act.dma_start(mk[32:33], mask.rearrange("(a b) k -> a b k", a=1)).then_inc(s_small, 16)
                        for k, vec in enumerate((bq0, bk0, bv0)):
                            act.dma_start(bias_q[:, k, :], vec.rearrange("(j p) -> p j", p=P),
                                          allow_slow_non_contiguous=True).then_inc(s_small, 16)
                        act.wait_ge(s_small, 16 * 7)
                        act.activation(gates[:], tg[:, 0:4], ACT.Tanh).then_inc(s_gate, 1)
                        act.dma_start(rraw, rhs.rearrange("(f p) o -> p f o", p=P)).then_inc(s_rhs, 16)
                    if layer == 1:
                        act.dma_start(praw[0:PROTOS, :], protos).then_inc(s_praw, 16)
                    for c in range(n_exp[layer]):
                        act.wait_ge(s_turn, e0 + c + 1)
                        dst = (btf if c < FT else adf)[:, :, P * (c % FT):P * (c % FT) + P]
                        act.copy(dst, PS[:, G6 + c % 2, :].rearrange("p (f n) -> p f n", f=FT)).then_inc(s_turned, 1)
                    act.wait_ge(s_cT_ps, layer + 1)
                    act.copy(cT, PS[:, 0:2, 0:2 * B * KEYS].rearrange("p a (f k) -> p a f k", f=2)).then_inc(s_cT, 1)
                    if layer == 1:
                        for q in range(3):
                            act.dma_start(bsf[PROTOS * q:PROTOS * q + PROTOS, :], biasw).then_inc(s_small, 16)
                        act.dma_start(wqn[:, 0:J, :], wq.rearrange("(j p) d -> p j d", p=P)).then_inc(s_wq, 16)
                    act.wait_ge(s_zero, 2 * layer + 1)
                    act.dma_start(BO[0:1, :], bo.rearrange("(a d) -> a d", a=1)).then_inc(s_bo, 16)
                    for c in range(len(chunks)):
                        act.wait_ge(s_turn, a0 + c + 1)
                        src = PS[:, G6 + c % 2, :]
                        if c < n_kv:
                            if c >= 2:
                                act.wait_ge(s_kv_ps, kv0 + c - 1)
                            act.copy(WT[:, c % 2].rearrange("p f n -> p (f n)"), src).then_inc(s_turned, 1)
                        else:
                            act.copy(WOT[:, c - n_kv, :], src).then_inc(s_turned, 1)
                        if layer == 1 and 10 <= c < 13:
                            if c == 10:
                                act.wait_ge(s_escale, 1)
                            dst, raw, k = ((bt, btf, 8), (ad, adf, 9), (pw, ptf, 10))[c - 10]
                            act.activation(dst[:, 0], raw, ACT.Copy, scale=sc[:, k:k + 1]).then_inc(s_dw, 1)
                        if layer == 1 and c == 13:
                            rows = slice(0, 3 * PROTOS)
                            act.activation(bs[rows], bsf[rows], ACT.Copy, scale=sc[rows, 14:15]).then_inc(s_dw, 1)
                    act.wait_ge(s_scale, 2 * layer + 1)
                    if layer == 1:
                        act.wait_ge(s_dwl, 1)
                    for u in range(units):
                        b, f = divmod(u, FT)
                        k0 = 3 * (u % 2)
                        act.wait_ge(s_kf_ps, units * layer + u + 1)
                        act.activation(Kf[:, b, 0, f, 0:12 * KEYS].rearrange("p (a k) -> p a k", a=2),
                                       PS[:, k0:k0 + 2, 0:6 * KEYS], ACT.Copy, scale=sc[:, 0:1]).then_inc(s_kfh, 1)
                        act.activation(Kf[:, b, 0, f, 12 * KEYS:HK], PS[:, k0 + 2, 0:4 * KEYS], ACT.Copy,
                                       scale=sc[:, 0:1]).then_inc(s_kfh, 1)
                    act.wait_ge(s_scale, 2 * layer + 2)
                    for v in range(B * ROWT):
                        b, i = divmod(v, ROWT)
                        act.wait_ge(s_vw_ps, vw0 + v + 1)
                        act.activation(Vw[:, b, 0, i, :], PS[:, values_bank(v), :], ACT.Copy,
                                       scale=sc[:, 1:2]).then_inc(s_vwh, 1)
                        if layer == 0:
                            row_piece(act, *divmod(v, ROWT))
                        if v == LN_AT + 2:
                            act.wait_ge(L["ln"], n0 + 1)
                            act.activation(xs[:, 0], xn, ACT.Copy, scale=XS).then_inc(L["ln_hi"], 1)

                @block.tensor
                def _(pe):
                    def turn(c, src):
                        if a0 + c >= 2:
                            pe.wait_ge(s_turned, a0 + c - 1)
                        for q in range(FT):
                            mm = pe.transpose(PS[:, G6 + c % 2, P * q:P * q + P], src[:, P * q:P * q + P], ident[:])
                        mm.then_inc(s_turn, 1)

                    def turn_loaded(c):
                        loads = (l0 + c) // SLOTS + 1
                        pe.wait_ge(s_slot[c % SLOTS], 16 * loads)
                        turn(c, ring[:, c % SLOTS, :])

                    def project(c):
                        pe.wait_ge(s_turned, a0 + c + 1)
                        if c >= 2:
                            pe.wait_ge(s_kv, kv0 + c - 1)
                        for f in range(FT):
                            mm = pe.matmul(PS[:, 4 + c % 2, 0:B * KEYS], WT[:, c % 2, f, :], cT[:, f, :],
                                           start=(f == 0), stop=(f == FT - 1))
                        mm.then_inc(s_kv_ps, 1)

                    if layer == 0:
                        pe.wait_ge(s_const, 4)
                    if layer == 1:
                        pe.wait_ge(s_early, 16 * n_exp[1])
                        for c in range(n_exp[1]):
                            turn(c - n_exp[1], early[:, c, :])
                    pe.wait_ge(s_ctx, 16 * (layer + 1))
                    for b in range(B):
                        for f in range(FT):
                            mm = pe.transpose(PS[:, f // 2, B * KEYS * (f % 2) + KEYS * b:B * KEYS * (f % 2) + KEYS * b + KEYS],
                                              craw[0:KEYS, b, P * f:P * f + P], ident[0:KEYS, 0:KEYS])
                    mm.then_inc(s_cT_ps, 1)
                    if layer == 1:
                        pe.wait_ge(s_praw, 16)
                        for f in range(FT):
                            mm = pe.transpose(PS[:, 2, PROTOS * f:PROTOS * f + PROTOS], praw[0:PROTOS, P * f:P * f + P],
                                              ident[0:PROTOS, 0:PROTOS])
                        mm.then_inc(s_pr_ps, 1)
                    turn_loaded(0)
                    pe.wait_ge(s_cT, layer + 1)
                    for c in range(len(chunks)):
                        if c + 1 < len(chunks):
                            turn_loaded(c + 1)
                        if c < n_kv:
                            project(c)
                        if layer == 1 and c == 0:
                            pe.wait_ge(s_pr, 2)
                            for f in range(FT):
                                mm = pe.matmul(PS[:, 3, 0:PROTOS], ones32[:], psq[:, f, :], start=(f == 0),
                                               stop=(f == FT - 1))
                            mm.then_inc(s_p2_ps, 1)

                    pe.wait_ge(s_wq, 16 * (layer + 1))
                    pe.wait_ge(s_kv, kv0 + n_kv)
                    if layer == 1:
                        pe.wait_ge(s_dwl, 1)
                    for u in range(units):
                        b, f = divmod(u, FT)
                        if u >= 2:
                            pe.wait_ge(s_kfl, units * layer + u - 1)
                        for p in range(HEADS // 2):
                            j, r = divmod(2 * p, hpt)
                            mm = pe.matmul(PS[:, 3 * (u % 2) + p // 3, 2 * KEYS * (p % 3):2 * KEYS * (p % 3) + 2 * KEYS],
                                           wqn[:, j, P * f:P * f + P], KBlk[layer][:, j, b, KEYS * r:KEYS * r + 2 * KEYS],
                                           start=True, stop=True)
                        mm.then_inc(s_kf_ps, 1)
                    def score_row(b):
                        if b:
                            pe.wait_ge(s_row, ROW_STEP * (b - 1) + 2)
                        for p in range(HEADS // 2):
                            j, r = divmod(2 * p, hpt)
                            mm = pe.matmul(PS[:, p // 3, 2 * KEYS * (p % 3):2 * KEYS * (p % 3) + 2 * KEYS],
                                           bias_q[:, 0, j:j + 1].to_broadcast([P, P]),
                                           KBlk[layer][:, j, b, KEYS * r:KEYS * r + 2 * KEYS], start=True, stop=True)
                        mm.then_inc(s_row_ps, 1)

                    pe.wait_ge(s_bo, 16 * (layer + 1))
                    pe.wait_ge(s_turned, turned_all)
                    pe.wait_ge(s_kfl, units * (layer + 1))
                    for v in range(B * ROWT):
                        b, i = divmod(v, ROWT)
                        if layer == 0 and i == 0:
                            score_row(b)
                        reach = [j for j in range(J) if first_row_tile(layer, j) <= i <= last_row_tile(layer, j)]
                        pe.wait_ge(s_vb, vb0 + b * J + reach[-1] + 1)
                        if v >= VALUE_BANKS:
                            pe.wait_ge(s_vwl, vw0 + v - VALUE_BANKS + 1)
                        todo = [(VBlk[layer][:, j, P * (i - first_row_tile(layer, j)):P * (i - first_row_tile(layer, j)) + P],
                                 WOT[:, j, :]) for j in reach]
                        if i == HK // P:
                            todo.append((e80[:], BO))
                        for n, (lhsT, r) in enumerate(todo):
                            mm = pe.matmul(PS[:, values_bank(v), :], lhsT, r, start=(n == 0), stop=(n == len(todo) - 1))
                        mm.then_inc(s_vw_ps, 1)

                @block.vector
                def _(dve):
                    done = [first_link[layer]]

                    def link(ins):
                        done[0] += 1
                        ins.then_inc(s_sc, 1)
                        dve.wait_ge(s_sc, done[0])

                    def largest(kind, j, src):
                        return dve.tensor_reduce(amx[:, kind, j:j + 1], src, AX, ALU.max, apply_absolute_value=True)

                    if layer == 0:
                        dve.wait_ge(s_const, 4)
                        for q in range(0, P, 32):
                            dve.memset(sel16[q:q + 1, :], 1.0)
                    dve.wait_ge(s_zero, 2 * layer + 1)
                    if layer == 1:
                        prototypes(dve)
                    for c in range(n_kv):
                        dve.wait_ge(s_kv_ps, kv0 + c + 1)
                        j = c % J
                        src = PS[:, 4 + c % 2, 0:B * KEYS].rearrange("p (b k) -> p b k", b=B)
                        if layer == 0 and c == 0:
                            dve.wait_ge(s_small, 16 * 7)
                        bias = bias_q[:, 1 + c // J, j:j + 1] if layer == 0 else None
                        if c >= J:
                            dst = VTl[layer][:, j]
                            ins = (dve.tensor_scalar(dst, src, bias, None, ALU.add) if layer == 0
                                   else dve.tensor_copy(dst, src))
                        else:
                            for r in range(hpt):
                                rows = slice(dhd * r, dhd * r + dhd)
                                dst = KBlk[layer][rows, j, :, KEYS * r:KEYS * r + KEYS]
                                ins = (dve.tensor_scalar(dst, src[rows], bias[rows], None, ALU.add) if layer == 0
                                       else dve.tensor_copy(dst, src[rows]))
                        ins.then_inc(s_kv, 1)
                        dve.wait_ge(s_kv, kv0 + c + 1)
                        if c < J:
                            largest(1, j, KBlk[layer][:, j].rearrange("p b k -> p (b k)"))
                        else:
                            largest(2, j, VTl[layer][:, j].rearrange("p b k -> p (b k)"))
                            if j == 0:
                                dve.wait_ge(s_wq, 16 * (layer + 1))
                            ins = largest(0, j, wqn[:, j, :])
                            if j == J - 1:
                                ins.then_inc(s_am, 1)
                        if layer == 1:
                            expert_weights(dve, link, c)
                    dve.wait_ge(s_amr, 2 * layer + 1)
                    link(dve.tensor_reduce(sc[:, 4:6], amr[:, 0:2], AX, ALU.max))
                    link(dve.tensor_scalar(sc[:, 4:6], sc[:, 4:6], TINY, None, ALU.max))
                    link(dve.scalar_tensor_tensor(sc[:, 2:3], sc[:, 4:5], float(dhd), sc[:, 5:6], ALU.mult, ALU.mult))
                    link(dve.reciprocal(sc[:, 0:1], sc[:, 2:3]))
                    link(dve.tensor_scalar(sc[:, 0:1], sc[:, 0:1], WS, None, ALU.mult))
                    dve.tensor_scalar(sc[:, 4:5], sc[:, 0:1], XS, None, ALU.mult)
                    dve.tensor_scalar(sc[:, 2:3], sc[:, 2:3], scaling / (WS * XS), None, ALU.mult).then_inc(s_scale, 1)
                    for u in range(units):
                        b, f = divmod(u, FT)
                        k0 = 3 * (u % 2)
                        dve.wait_ge(s_kfh, 2 * (units * layer + u) + 1)
                        dve.scalar_tensor_tensor(Kf[:, b, 1, f, 0:12 * KEYS].rearrange("p (a k) -> p a k", a=2),
                                                 PS[:, k0:k0 + 2, 0:6 * KEYS], sc[:, 0:1],
                                                 Kf[:, b, 0, f, 0:12 * KEYS].rearrange("p (a k) -> p a k", a=2),
                                                 ALU.mult, ALU.subtract)
                        dve.wait_ge(s_kfh, 2 * (units * layer + u) + 2)
                        dve.scalar_tensor_tensor(Kf[:, b, 1, f, 12 * KEYS:HK], PS[:, k0 + 2, 0:4 * KEYS], sc[:, 0:1],
                                                 Kf[:, b, 0, f, 12 * KEYS:HK], ALU.mult, ALU.subtract).then_inc(s_kfl, 1)
                        for j in range(u * J // 4, (u + 1) * J // 4):
                            if j < J:
                                dve.wait_ge(s_turned, a0 + n_kv + j + 1)
                                largest(3, j, WOT[:, j, :])
                        if u == 3:
                            dve.wait_ge(s_bo, 16 * (layer + 1))
                            dve.tensor_reduce(amx[:, 4, 0:1], BO, AX, ALU.max, apply_absolute_value=True).then_inc(s_am, 1)
                        if u == 4 and layer == 0:
                            dve.wait_ge(s_rhs, 16)
                            dve.tensor_reduce(rabs, rraw.rearrange("p f o -> p o f"), AX, ALU.max,
                                              apply_absolute_value=True).then_inc(s_rmax, 1)
                        if u == 5:
                            dve.wait_ge(s_amr, 2 * layer + 2)
                            link(dve.tensor_reduce(sc[:, 5:8], amr[:, 2:5], AX, ALU.max))
                            link(dve.tensor_scalar(sc[:, 5:8], sc[:, 5:8], TINY, None, ALU.max))
                            link(dve.scalar_tensor_tensor(sc[:, 3:4], sc[:, 5:6], float(dhd), sc[:, 6:7], ALU.mult, ALU.mult))
                            link(dve.tensor_tensor(sc[:, 3:4], sc[:, 3:4], sc[:, 7:8], ALU.max))
                            link(dve.reciprocal(sc[:, 1:2], sc[:, 3:4]))
                            dve.wait_ge(s_gate, 1)
                            dve.tensor_scalar(sc[:, 1:2], sc[:, 1:2], WS, None, ALU.mult)
                            dve.tensor_scalar(sc[:, 3:4], sc[:, 3:4], 1.0 / (WS * PSC), gates[:, layer:layer + 1],
                                              ALU.mult, ALU.mult).then_inc(s_scale, 1)
                    for v in range(B * ROWT):
                        b, i = divmod(v, ROWT)
                        dve.wait_ge(s_vwh, vw0 + v + 1)
                        dve.scalar_tensor_tensor(Vw[:, b, 1, i, :], PS[:, values_bank(v), :], sc[:, 1:2], Vw[:, b, 0, i, :],
                                                 ALU.mult, ALU.subtract).then_inc(s_vwl, 1)
                        if layer == 0:
                            quantise_rhs(dve, v)
                            row_rest(dve, b, i)
                        if v == LN_AT - 3:
                            if layer == 0:
                                dve.wait_ge(s_x, 16 * x_parts)
                            dve.bn_stats(st[:, 0, 0, :], X[:, 0, :]).then_inc(L["stats"], 1)
                            dve.wait_ge(L["stats"], n0 + 1)
                            dve.bn_aggr(mv[:, 0, 0, :], st[:, 0, 0, :]).then_inc(L["mean_var"], 1)
                        if v == LN_AT:
                            dve.wait_ge(L["rstd"], n0 + 1)
                            dve.tensor_scalar(xn, X[:, 0, :], mv[:, 0, 0, 0:1], rstd[:, 0, 0, 1:2], ALU.subtract,
                                              ALU.mult).then_inc(L["ln"], 1)
                        if v == LN_AT + 3:
                            dve.wait_ge(L["ln_hi"], n0 + 1)
                            dve.scalar_tensor_tensor(xs[:, 1], xn, XS, xs[:, 0], ALU.mult,
                                                     ALU.subtract).then_inc(L["ln_lo"], 1)
                    if layer == 0:
                        link(dve.tensor_scalar(tg[:, 5:6], tg[:, 4:5], -1.0, None, ALU.mult))
                        link(dve.tensor_tensor(tg[:, 5:6], tg[:, 5:6], tg[:, 4:5], ALU.max))
                        link(dve.tensor_scalar(tg[:, 5:6], tg[:, 5:6], 0.1, None, ALU.max))
                        dve.reciprocal(tinv[:], tg[:, 5:6])

        ROW_STEP = 5

        def row_sums(b, rows):
            return [(PS[rows, 0:2, 0:6 * KEYS], slice(0, 12 * KEYS), True),
                    (PS[rows, 2, 0:4 * KEYS], slice(12 * KEYS, HK), False)]

        def halves(ap, two):
            return ap.rearrange("p (a k) -> p a k", a=2) if two else ap

        def row_piece(act, b, i):
            if i == 2:
                act.wait_ge(s_row_ps, b + 1)
                for ps, cols, two in row_sums(b, slice(0, P)):
                    ins = act.activation(halves(row[:, b, cols], two), ps, ACT.Copy, scale=sc[:, 4:5])
                ins.then_inc(s_row, 1)
            if i in (5, 8):
                k = (2, 4)[i == 8]
                rows = slice((64, 96)[i == 8], P)
                act.wait_ge(s_row, ROW_STEP * b + k)
                act.copy(row[rows, b, :], rest[rows]).then_inc(s_row, 1)

        def row_rest(dve, b, i):
            if i == 4:
                dve.wait_ge(s_row, ROW_STEP * b + 1)
                rows = slice(64, P)
                for ps, cols, two in row_sums(b, rows):
                    ins = dve.scalar_tensor_tensor(halves(rest[rows, cols], two), ps, sc[rows, 4:5],
                                                   halves(row[rows, b, cols], two), ALU.mult, ALU.subtract)
                ins.then_inc(s_row, 1)
                dve.tensor_scalar(by_head(row[32:33, b, :]), mk[32:33, b:b + 1, :].to_broadcast([1, HEADS, KEYS]),
                                  1.0, NEG, ALU.not_equal, ALU.mult)
            if i == 7:
                dve.wait_ge(s_row, ROW_STEP * b + 3)
                rows = slice(96, P)
                dve.tensor_tensor(rest[rows], rest[rows], row[rows, b, :], ALU.subtract).then_inc(s_row, 1)

        def quantise_rhs(dve, v):
            if v == 0:
                dve.wait_ge(s_rmaxr, 1)
                dve.wait_ge(s_gate, 1)
                dve.tensor_scalar(cg, cg, TINY, 1.0 / INT8_MAX, ALU.max, ALU.mult).then_inc(s_rq, 1)
            if v == 1:
                dve.wait_ge(s_rq, 1)
                dve.reciprocal(rabs, cg).then_inc(s_rq, 1)
                dve.wait_ge(s_rq, 2)
                dve.tensor_scalar(cg, cg, gates[:, 2:3], None, ALU.mult)
            if v == 2:
                dve.tensor_tensor(rraw, rraw, rabs.unsqueeze(1).to_broadcast([P, FT, D]), ALU.mult).then_inc(s_rq, 1)
            if v == 3:
                dve.wait_ge(s_rq, 3)
                dve.tensor_scalar(rraw, rraw, MAGIC, MAGIC + INT8_MAX, ALU.add, ALU.min).then_inc(s_rq, 1)
            if v == 4:
                dve.wait_ge(s_rq, 4)
                dve.tensor_scalar(rq, rraw, MAGIC - INT8_MAX, -MAGIC, ALU.max, ALU.add).then_inc(s_rq, 1)
                dve.wait_ge(s_rq, 5)

        def prototypes(dve):
            dve.wait_ge(s_pr_ps, 1)
            dve.tensor_copy(ptf, PS[:, 2, 0:FT * PROTOS].rearrange("p (f n) -> p f n", f=FT)).then_inc(s_pr, 1)
            dve.wait_ge(s_pr, 1)
            dve.tensor_tensor(psq, ptf, ptf, ALU.mult).then_inc(s_pr, 1)

        def expert_weights(dve, link, c):
            if c in (2, 3, 4, 5):
                if c == 2:
                    dve.wait_ge(s_turned, first_turn[1])
                    dve.wait_ge(s_small, 16 * 10)
                raw = (btf.rearrange("p f n -> p (f n)"), adf.rearrange("p f n -> p (f n)"),
                       ptf.rearrange("p f n -> p (f n)"), bsf[0:PROTOS])[c - 2]
                ins = dve.tensor_reduce(amxe[0:raw.shape[0], c - 2:c - 1], raw, AX, ALU.max,
                                        apply_absolute_value=True)
                if c == 5:
                    ins.then_inc(s_ame, 1)
            if c == 7:
                dve.wait_ge(s_amre, 1)
                link(dve.tensor_scalar(sc[:, 11:15], amre[:], TINY, None, ALU.max))
                link(dve.tensor_tensor(sc[:, 12:13], sc[:, 11:12], sc[:, 12:13], ALU.mult))
                link(dve.tensor_tensor(sc[:, 12:13], sc[:, 12:13], sc[:, 14:15], ALU.max))
                link(dve.reciprocal(sc[:, 8:11], sc[:, 11:14]))
                link(dve.tensor_scalar(sc[:, 8:11], sc[:, 8:11], WS, None, ALU.mult))
                link(dve.tensor_scalar(sc[:, 14:15], sc[:, 9:10], HS / WTS, None, ALU.mult))
                link(dve.tensor_tensor(sc[:, 9:10], sc[:, 9:10], sc[:, 11:12], ALU.mult))
                link(dve.tensor_scalar(sc[:, 11:12], sc[:, 12:13], 1.0 / (HS * WS), gates[:, 3:4], ALU.mult, ALU.mult))
                dve.tensor_scalar(sc[:, 13:14], sc[:, 13:14], 2.0 / (WS * XS), None, ALU.mult).then_inc(s_escale, 1)
            if 12 <= c < 15:
                dst, src, k = ((bt, btf, 8), (ad, adf, 9), (pw, ptf, 10))[c - 12]
                dve.wait_ge(s_dw, c - 11)
                ins = dve.scalar_tensor_tensor(dst[:, 1].rearrange("p f n -> p (f n)"), src.rearrange("p f n -> p (f n)"),
                                               sc[:, k:k + 1], dst[:, 0].rearrange("p f n -> p (f n)"), ALU.mult,
                                               ALU.subtract)
            if c == 15:
                lo = slice(PROTOS, 2 * PROTOS)
                dve.wait_ge(s_dw, 4)
                dve.scalar_tensor_tensor(bs[lo], bsf[lo], sc[lo, 14:15], bs[lo], ALU.mult, ALU.subtract)
                dve.wait_ge(s_p2_ps, 1)
                dve.tensor_copy(p2, PS[:, 3, 0:PROTOS]).then_inc(s_dwl, 1)

        def loop(layer):
            base = TILES * layer
            fs = 0 if layer == 0 else 1

            LAST = TILES + 4
            LOOPS = ((6, PER_B, 0), (PER_B + 2, TILES, 1))

            def steps(eng, step):
                s = 1
                while s < LAST:
                    span = [x for x in LOOPS if x[0] == s]
                    if span:
                        first, end, batch = span[0]
                        with eng.Fori(0, (end - first) // 2) as i:
                            for u in range(2):
                                step(first + 2 * i + u, u, batch)
                        s = end
                    else:
                        step(s, s % 2, None)
                        s += 1

            class At:

                def __init__(self, s, u, batch, lag):
                    self.n = s - lag
                    self.u = (u - lag) % 2
                    self.on = batch is not None or 0 <= s - lag < TILES
                    self.b = batch if batch is not None else (s - lag) // PER_B

            def after(eng, name, at, back=0, per=1, alone=False):
                if isinstance(at.n, int) and at.n - back < 0:
                    return
                wait(eng, L[name], (at.n + (base_of(name) + 1 - back)) * per, alone)

            def wait(eng, signal, value, alone):
                if alone and not isinstance(value, int):
                    value = eng.snap(value)
                    eng.to_reg(value)
                    eng.wait_ge(s_const, 4)
                eng.wait_ge(signal, value)

            def base_of(name):
                shared = ("stats", "mean_var", "var_eps", "rstd", "ln", "ln_hi", "ln_lo", "x_T", "scores", "max",
                          "shifted", "exp", "sum", "inv_sum", "probs", "probs_hi", "probs_lo", "p_T_hi", "p_T_lo",
                          "attn_out", "x_attn", "f_stats", "f_mean_var", "f_var_eps", "f_rstd", "f_ln")
                return base if name in shared else 0

            with nc.Block() as block:
                @block.gpsimd
                def _(pool):
                    def inv_std(at, k, stage):
                        after(pool, stage + "mean_var", at, alone=True)
                        pool.tensor_scalar(rstd[:, k, at.u, 0:1], mv[:, k, at.u, 1:2], EPS, None,
                                           ALU.add).then_inc(L[stage + "var_eps"], 1)
                        after(pool, stage + "var_eps", at)
                        pool.tensor_tensor(rstd[:, k, at.u, 1:2], rstd[:, k, at.u, 0:1], half[:, 0:1],
                                           ALU.pow).then_inc(L[stage + "rstd"], 1)

                    def normalise(at):
                        after(pool, "inv_sum", at)
                        pool.tensor_tensor(by_head(sS), by_head(sS),
                                           smx[:, at.u, 1, :].unsqueeze(2).to_broadcast([P, HEADS, KEYS]),
                                           ALU.mult).then_inc(L["probs"], 1)

                    def clamp(at):
                        after(pool, "quant", at, alone=True)
                        pool.tensor_scalar(xq, xq, MAGIC + INT8_MAX, MAGIC - INT8_MAX, ALU.min,
                                           ALU.max).then_inc(L["clamped"], 1)

                    def add_ffn0(at):
                        after(pool, "ffn0_scaled", at, alone=True)
                        pool.tensor_tensor(X[:, at.n, :], X[:, at.n, :], dq, ALU.add).then_inc(L["x_ffn0"], 1)

                    def route(at):
                        n = [0]

                        def link(ins):
                            n[0] += 1
                            ins.then_inc(L["route"], 1)
                            wait(pool, L["route"], at.n * 8 + n[0], True)

                        after(pool, "best_at", at, alone=True)
                        link(pool.tensor_scalar(rw[:, 0:2], m8[:, 0:2], -1.0, None, ALU.mult))
                        link(pool.tensor_tensor(rw[:, 2:4], rw[:, 0:2], half[:, 1:2].to_broadcast([P, 2]), ALU.pow))
                        pool.tensor_copy(rw[:, 4:6], i8[:, 0:2])
                        pool.tensor_tensor(rw[:, 6:7], rw[:, 2:3], rw[:, 3:4], ALU.subtract).then_inc(L["gap"], 1)
                        after(pool, "gap_exp", at, alone=True)
                        link(pool.tensor_scalar(rw[:, 8:9], rw[:, 7:8], 1.0, None, ALU.add))
                        link(pool.tensor_tensor(rw[:, 9:10], rw[:, 8:9], mone[:, 0:1], ALU.pow))
                        link(pool.tensor_tensor(rw[:, 10:11], rw[:, 9:10], rw[:, 7:8], ALU.mult))
                        link(pool.tensor_scalar(oh[:, 0], iota32[:], rw[:, 4:5], rw[:, 9:10], ALU.is_equal, ALU.mult))
                        link(pool.tensor_scalar(oh[:, 1], iota32[:], rw[:, 5:6], rw[:, 10:11], ALU.is_equal, ALU.mult))
                        after(pool, "w_lo", at, back=1)
                        link(pool.tensor_tensor(wt[:], oh[:, 0], oh[:, 1], ALU.add))

                    pool.memset(ps[:, 0, HK:HK + 1], PSC)
                    pool.memset(ps[:, 0, HK + 1:HKP], 0.0)
                    pool.memset(ps[:, 1, HK:HKP], 0.0).then_inc(s_pad, 1)
                    if layer == 1:
                        pool.memset(hs[:, 2 * D + 3 * PROTOS:], 0.0).then_inc(s_pad, 1)

                    def step(s, u, batch):
                        tile = [At(s, u, batch, k) for k in range(5)]
                        if layer == 1 and tile[4].on:
                            route(tile[4])
                        if tile[0].on:
                            inv_std(tile[0], 0, "")
                        if layer == 0 and tile[3].on:
                            clamp(tile[3])
                        if layer == 0 and tile[4].on:
                            add_ffn0(tile[4])
                        if tile[1].on:
                            normalise(tile[1])
                        if tile[2].on:
                            inv_std(tile[2], 1, "f_")
                    steps(pool, step)

                @block.scalar
                def _(act):
                    def ln_hi(at):
                        after(act, "ln", at)
                        after(act, "x_T", at, back=1, per=16)
                        act.activation(xs[:, 0], xn, ACT.Copy, scale=XS).then_inc(L["ln_hi"], 1)

                    def probs_hi(at):
                        after(act, "probs", at)
                        after(act, "p_T_hi", at, back=1, per=16)
                        act.activation(ps[:, 0, 0:HK], sS, ACT.Copy, scale=PSC).then_inc(L["probs_hi"], 1)

                    def exponentials(at):
                        after(act, "shifted", at)
                        act.activation(sS, sS, ACT.Exp, scale=sc[:, 2:3]).then_inc(L["exp"], 1)

                    def quant_int(at):
                        after(act, "clamped", at)
                        after(act, "q_T", at, back=1, per=16)
                        act.activation(qs, xq, ACT.Identity, bias=nmagic[:, 0:1]).then_inc(L["quant_int"], 1)

                    def gap_exp(at):
                        after(act, "gap", at)
                        act.activation(rw[:, 7:8], rw[:, 6:7], ACT.Exp, scale=tinv[:, 0:1]).then_inc(L["gap_exp"], 1)

                    def h_hi(at):
                        after(act, "weighted", at)
                        after(act, "h_T", at, back=1, per=16)
                        act.copy(hs[:, 0:D], hw).then_inc(L["h_hi"], 1)
                        act.activation(hs[:, 2 * D:2 * D + 2 * PROTOS].rearrange("p (c n) -> p c n", c=2),
                                       wt[:].unsqueeze(1).to_broadcast([P, 2, PROTOS]), ACT.Copy,
                                       scale=WTS).then_inc(L["w_hi"], 1)

                    def d_hi(at):
                        after(act, "f_ln", at)
                        after(act, "d_T", at, back=1, per=16)
                        act.activation(ds[:, 0], xf, ACT.Copy, scale=XS).then_inc(L["d_hi"], 1)

                    def sq_sum(at):
                        after(act, "f_ln", at)
                        act.activation(junk, xf, ACT.Square, accum_out=x2[:, at.u:at.u + 1]).then_inc(L["sq_sum"], 1)

                    def step(s, u, batch):
                        tile = [At(s, u, batch, k) for k in range(5)]
                        if layer == 1 and tile[4].on:
                            gap_exp(tile[4])
                        if tile[2].on:
                            probs_hi(tile[2])
                        if layer == 1 and tile[3].on:
                            d_hi(tile[3])
                            sq_sum(tile[3])
                        if layer == 1 and tile[4].on:
                            h_hi(tile[4])
                        if tile[0].on:
                            ln_hi(tile[0])
                        if layer == 0 and tile[3].on:
                            quant_int(tile[3])
                        if tile[1].on:
                            exponentials(tile[1])
                    steps(act, step)

                @block.tensor
                def _(pe):
                    def scores(at):
                        after(pe, "x_T", at, per=16)
                        after(pe, "shifted", at, back=1)
                        if layer == 0:
                            for k in range(3):
                                pe.matmul(scores_bank(k), sel16[:], row[:, at.b, KEYS * 6 * k:KEYS * 6 * k + KEYS * BANK_HEADS[k]],
                                          start=True, stop=False)
                        for f in range(FT):
                            for w, half in ((0, 0), (1, 0), (0, 1)):
                                for k in range(3):
                                    c = 6 * KEYS * k
                                    mm = pe.matmul(scores_bank(k), xT[:, half, f, :],
                                                   Kf[:, at.b, w, f, c:c + KEYS * BANK_HEADS[k]],
                                                   start=(layer == 1 and f == 0 and w == 0 and half == 0),
                                                   stop=(f == FT - 1 and half == 1))
                        mm.then_inc(L["scores"], 1)

                    def attn_out(at):
                        after(pe, "x_attn", at, back=1)
                        for w, half, name in ((0, 0, "p_T_hi"), (1, 0, None), (0, 1, "p_T_lo")):
                            if name:
                                after(pe, name, at, per=16)
                            for i in range(ROWT):
                                mm = pe.matmul(ATTN, pT[:, half, i, :], Vw[:, at.b, w, i, :],
                                               start=(w == 0 and half == 0 and i == 0), stop=(half == 1 and i == ROWT - 1))
                        mm.then_inc(L["attn_out"], 1)

                    def ffn0_out(at):
                        after(pe, "q_T", at, per=16)
                        after(pe, "ffn0_scaled", at, back=1)
                        for f in range(FT):
                            mm = pe.matmul(FFN0, qT[:, f, :], rq[:, f, :], start=(f == 0), stop=(f == FT - 1))
                        mm.then_inc(L["ffn0_out"], 1)

                    def three(outp, hi, lo, w, start=True):
                        for f in range(FT):
                            pe.matmul(outp, hi[:, f, :], w[:, 0, f, :], start=(start and f == 0), stop=False)
                            pe.matmul(outp, hi[:, f, :], w[:, 1, f, :], start=False, stop=False)
                            mm = pe.matmul(outp, lo[:, f, :], w[:, 0, f, :], start=False, stop=(f == FT - 1))
                        return mm

                    def hidden(at):
                        after(pe, "d_T", at, per=16)
                        after(pe, "dist_a", at, back=1)
                        three(DOTS[:, 0:PROTOS], dT[:, 0], dT[:, 1], pw).then_inc(L["dots"], 1)
                        after(pe, "weighted", at, back=1)
                        three(HIDDEN, dT[:, 0], dT[:, 1], bt).then_inc(L["hidden"], 1)

                    def ffn1_out(at):
                        after(pe, "h_T", at, per=16)
                        after(pe, "x_ffn1", at, back=1)
                        pe.matmul(FFN1, hT[0:3 * PROTOS, 2 * FT, :], bs[0:3 * PROTOS, :], start=True, stop=False)
                        three(FFN1, hT[:, 0:FT], hT[:, FT:2 * FT], ad, start=False).then_inc(L["ffn1_out"], 1)

                    def step(s, u, batch):
                        tile = [At(s, u, batch, k) for k in range(5)]
                        if tile[1].on:
                            scores(tile[1])
                        if tile[2].on:
                            attn_out(tile[2])
                        if layer == 0 and tile[3].on:
                            ffn0_out(tile[3])
                        if layer == 1 and tile[3].on:
                            hidden(tile[3])
                        if layer == 1 and tile[4].on:
                            ffn1_out(tile[4])
                    steps(pe, step)

                @block.vector
                def _(dve):
                    def statistics(at, k, stage, src):
                        if src:
                            after(dve, src, at, alone=True)
                        dve.bn_stats(st[:, k, at.u, :], X[:, at.n, :]).then_inc(L[stage + "stats"], 1)
                        after(dve, stage + "stats", at, alone=True)
                        dve.bn_aggr(mv[:, k, at.u, :], st[:, k, at.u, :]).then_inc(L[stage + "mean_var"], 1)

                    def layernorm(at, k, stage, dst, used):
                        after(dve, stage + "rstd", at)
                        for name, back in used:
                            after(dve, name, at, back=back)
                        dve.tensor_scalar(dst, X[:, at.n, :], mv[:, k, at.u, 0:1], rstd[:, k, at.u, 1:2],
                                          ALU.subtract, ALU.mult).then_inc(L[stage + "ln"], 1)

                    def ln_lo(at):
                        after(dve, "ln_hi", at)
                        dve.scalar_tensor_tensor(xs[:, 1], xn, XS, xs[:, 0], ALU.mult,
                                                 ALU.subtract).then_inc(L["ln_lo"], 1)

                    def shift_scores(at):
                        after(dve, "scores", at)
                        for src, cols, heads, shape in scores_parts():
                            ins = dve.tensor_reduce(cut(mx[:, at.u, heads], shape), src, AX, ALU.max)
                        ins.then_inc(L["max"], 1)
                        after(dve, "max", at)
                        after(dve, "probs_lo", at, back=1)
                        for src, cols, heads, shape in scores_parts():
                            o = sS[:, cols].rearrange("p (a h k) -> p a h k", a=2, k=KEYS) if len(shape) == 2 else by_head(sS[:, cols])
                            m = cut(mx[:, at.u, heads], shape)
                            m = m.unsqueeze(len(shape) + 1).to_broadcast([P, *shape, KEYS])
                            ins = dve.tensor_tensor(o, src, m, ALU.subtract)
                        ins.then_inc(L["shifted"], 1)

                    def sums(at):
                        after(dve, "exp", at)
                        dve.tensor_reduce(smx[:, at.u, 0, :], by_head(sS), AX, ALU.add).then_inc(L["sum"], 1)
                        after(dve, "sum", at)
                        dve.reciprocal(smx[:, at.u, 1, :], smx[:, at.u, 0, :]).then_inc(L["inv_sum"], 1)

                    def probs_lo(at):
                        after(dve, "probs_hi", at)
                        after(dve, "p_T_lo", at, back=1, per=16)
                        dve.scalar_tensor_tensor(ps[:, 1, 0:HK], sS, PSC, ps[:, 0, 0:HK], ALU.mult,
                                                 ALU.subtract).then_inc(L["probs_lo"], 1)

                    def add_attn(at):
                        after(dve, "attn_out", at)
                        dve.scalar_tensor_tensor(X[:, at.n, :], ATTN, sc[:, 3:4], X[:, at.n, :], ALU.mult,
                                                 ALU.add).then_inc(L["x_attn"], 1)

                    def lhs_scales(at):
                        after(dve, "f_ln", at)
                        dve.tensor_reduce(lsb[:, at.u, 0:1], xf, AX, ALU.max, apply_absolute_value=True).then_inc(L["absmax"], 1)
                        after(dve, "absmax", at)
                        dve.tensor_scalar(lsb[:, at.u, 1:2], lsb[:, at.u, 0:1], TINY, 1.0 / INT8_MAX, ALU.max,
                                          ALU.mult).then_inc(L["lhs_scale"], 1)
                        after(dve, "lhs_scale", at)
                        dve.reciprocal(lsb[:, at.u, 2:3], lsb[:, at.u, 1:2]).then_inc(L["lhs_inv"], 1)

                    def quantise(at):
                        after(dve, "lhs_inv", at)
                        after(dve, "quant_int", at, back=1)
                        dve.tensor_scalar(xq, xf, lsb[:, at.u, 2:3], MAGIC, ALU.mult, ALU.add).then_inc(L["quant"], 1)

                    def scale_ffn0(at):
                        after(dve, "ffn0_out", at)
                        after(dve, "x_ffn0", at, back=1)
                        dve.scalar_tensor_tensor(dq, FFN0, lsb[:, at.u, 1:2], cg, ALU.mult,
                                                 ALU.mult).then_inc(L["ffn0_scaled"], 1)

                    def weigh_hidden(at):
                        dve.wait_ge(L["route"], at.n * 8 + 8)
                        after(dve, "hidden", at)
                        after(dve, "h_lo", at, back=1)
                        dve.scalar_tensor_tensor(hw.rearrange("p (n r) -> p n r", r=RANK),
                                                 HIDDEN.rearrange("p (n r) -> p n r", r=RANK), HS / (WS * XS),
                                                 wt[:].unsqueeze(2).to_broadcast([P, PROTOS, RANK]), ALU.mult,
                                                 ALU.mult).then_inc(L["weighted"], 1)

                    def h_lo(at):
                        after(dve, "h_hi", at)
                        dve.tensor_tensor(hs[:, D:2 * D], hw, hs[:, 0:D], ALU.subtract).then_inc(L["h_lo"], 1)
                        after(dve, "w_hi", at)
                        hi, lo = (slice(2 * D + k * PROTOS, 2 * D + (k + 1) * PROTOS) for k in (1, 2))
                        dve.scalar_tensor_tensor(hs[:, lo], wt[:], WTS, hs[:, hi], ALU.mult,
                                                 ALU.subtract).then_inc(L["w_lo"], 1)

                    def d_lo(at):
                        after(dve, "d_hi", at)
                        dve.scalar_tensor_tensor(ds[:, 1], xf, XS, ds[:, 0], ALU.mult,
                                                 ALU.subtract).then_inc(L["d_lo"], 1)

                    def add_ffn1(at):
                        after(dve, "ffn1_out", at)
                        dve.scalar_tensor_tensor(X[:, at.n, :], FFN1, sc[:, 11:12], X[:, at.n, :], ALU.mult,
                                                 ALU.add).then_inc(L["x_ffn1"], 1)

                    def nearest(at):
                        after(dve, "dots", at)
                        after(dve, "best_at", at, back=1)
                        dve.scalar_tensor_tensor(rt[:, 0], DOTS[:, 0:PROTOS], sc[:, 13:14], p2, ALU.mult,
                                                 ALU.subtract).then_inc(L["dist_a"], 1)
                        after(dve, "dist_a", at)
                        after(dve, "sq_sum", at)
                        dve.tensor_scalar(rt[:, 1], rt[:, 0], x2[:, at.u:at.u + 1], 0.0, ALU.subtract,
                                          ALU.min).then_inc(L["dist_b"], 1)
                        after(dve, "dist_b", at, alone=True)
                        dve.max(m8[:], rt[:, 1]).then_inc(L["best"], 1)
                        after(dve, "best", at, alone=True)
                        dve.max_index(i8[:], m8[:], rt[:, 1]).then_inc(L["best_at"], 1)

                    def step(s, u, batch):
                        tile = [At(s, u, batch, k) for k in range(5)]
                        if tile[0].on:
                            statistics(tile[0], 0, "", None)
                        if layer == 1 and tile[4].on:
                            weigh_hidden(tile[4])
                        if tile[3].on and layer == 0:
                            layernorm(tile[3], 1, "f_", xf, [("quant", 1)])
                            lhs_scales(tile[3])
                            quantise(tile[3])
                        if layer == 1 and tile[3].on:
                            layernorm(tile[3], 1, "f_", xf, [("d_lo", 1), ("sq_sum", 1)])
                        if tile[0].on:
                            layernorm(tile[0], 0, "", xn, [("ln_lo", 1)])
                        if tile[2].on:
                            probs_lo(tile[2])
                        if layer == 1 and tile[3].on:
                            d_lo(tile[3])
                        if layer == 1 and tile[4].on:
                            h_lo(tile[4])
                        if tile[0].on:
                            ln_lo(tile[0])
                        if tile[1].on:
                            shift_scores(tile[1])
                            sums(tile[1])
                        if tile[2].on:
                            add_attn(tile[2])
                            statistics(tile[2], 1, "f_", "x_attn")
                        if layer == 0 and tile[3].on:
                            scale_ffn0(tile[3])
                        if layer == 1 and tile[3].on:
                            nearest(tile[3])
                        if layer == 1 and tile[4].on:
                            add_ffn1(tile[4])
                    steps(dve, step)

                @block.sync
                def _(sp):
                    def turn(out, halves, name):
                        sp.dma_start_transpose(out, halves).then_inc(L[name], 16)

                    def turn_probs(at, half):
                        after(sp, ("probs_hi", "probs_lo")[half], at, alone=True)
                        after(sp, "attn_out", at, back=1, alone=True)
                        turn(pT[:, half], ps[:, half], ("p_T_hi", "p_T_lo")[half])

                    def turn_ln(at):
                        after(sp, "ln_lo", at, alone=True)
                        after(sp, "scores", at, back=1, alone=True)
                        turn(xT.rearrange("p w f t -> p (w f) t"), xs.rearrange("p w d -> p (w d)"), "x_T")

                    def turn_quant(at):
                        after(sp, "quant_int", at, alone=True)
                        after(sp, "ffn0_out", at, back=1, alone=True)
                        turn(qT, qs, "q_T")

                    def turn_d(at):
                        after(sp, "d_lo", at, alone=True)
                        after(sp, "hidden", at, back=1, alone=True)
                        turn(dT.rearrange("p w f t -> p (w f) t"), ds.rearrange("p w d -> p (w d)"), "d_T")

                    def turn_hidden(at):
                        after(sp, "w_lo", at, alone=True)
                        after(sp, "ffn1_out", at, back=1, alone=True)
                        turn(hT, hs, "h_T")

                    def store(at):
                        after(sp, "x_ffn1", at)
                        sp.dma_start(rows_out[:, at.n, :], X[:, at.n, :]).then_inc(L["stored"], 16)

                    rows_out = out.rearrange("b (t p) d -> p (b t) d", p=P)
                    if layer == 0:
                        rows = Bw.rearrange("n r d -> (n r) d")
                        for j in range(FT):
                            sp.dma_start(early[:, j, :], rows[P * j:P * j + P, :]).then_inc(s_early, 16)
                        for j in range(FT):
                            sp.dma_start(early[:, FT + j, :].rearrange("p (n r) -> p n r", r=RANK),
                                         Aw[:, P * j:P * j + P, :].rearrange("n o r -> o n r")).then_inc(s_early, 16)
                    sp.wait_ge(s_pad, (1, 3)[layer])

                    def step(s, u, batch):
                        tile = [At(s, u, batch, k) for k in range(6)]
                        if tile[2].on:
                            turn_probs(tile[2], 0)
                            turn_probs(tile[2], 1)
                        if layer == 1 and tile[3].on:
                            turn_d(tile[3])
                        if layer == 1 and tile[4].on:
                            turn_hidden(tile[4])
                        if tile[0].on:
                            turn_ln(tile[0])
                        if layer == 0 and tile[3].on:
                            turn_quant(tile[3])
                        if layer == 1 and tile[5].on:
                            store(tile[5])
                    steps(sp, step)
                    if layer == 1:
                        store(At(LAST, LAST % 2, None, 5))
                        sp.wait_ge(L["stored"], 16 * TILES)


        setup(0)
        loop(0)
        setup(1)
        loop(1)


_INS = ['x', 'ctx_1024', 'mask_BxS2_ff1', 'g_xattn', 'g_ffn', 'L0_xattn_Wq', 'L0_xattn_bq', 'L0_xattn_Wk', 'L0_xattn_bk',
        'L0_xattn_Wv', 'L0_xattn_bv', 'L0_xattn_Wo', 'L0_xattn_bo', 'L0_ffn_rhs', 'L1_xattn_Wq', 'L1_xattn_Wk',
        'L1_xattn_Wv', 'L1_xattn_Wo', 'L1_xattn_bo', 'L1_ffn_prototypes', 'L1_ffn_B', 'L1_ffn_A', 'L1_ffn_bias',
        'L1_ffn_temp']


def kernel(**inputs):
    import numpy as _np
    import concourse.bacc as _bacc
    from concourse.bass_utils import run_bass_kernel_spmd as _run

    nc = _bacc.Bacc("TRN2", target_bir_lowering=False, num_devices=1)
    arrays, args = {}, []
    for name in _INS:
        a = _np.ascontiguousarray(inputs[name])
        a = a.reshape(a.shape or (1,))
        arrays[f"in_{name}"] = a
        args.append(nc.dram_tensor(f"in_{name}", a.shape, F32, kind="ExternalInput").ap())
    args.append(nc.dram_tensor("out", (B, T, D), F32, kind="ExternalOutput").ap())
    build(nc, *args)
    return _run(nc, [arrays], core_ids=[0]).results[0]["out"]
```

```python
from contextlib import ExitStack

import concourse.bass as bass
from concourse import mybir

P = 128
D = 512
FT = D // P
B, T = 2, 2048
TILES = B * T // P
PER_B = T // P
HEADS = 16
KEYS = 77
HK = HEADS * KEYS
BANK_HEADS = (6, 6, 4)
ROWT = (HK + 1 + P - 1) // P
HKP = ROWT * P
PROTOS, RANK = 32, 16
EPS = 1e-5
TINY = 1e-12
INT8_MAX = 127.0
MAGIC = 1.5 * 2.0 ** 23
NEG = -(2.0 ** 127)
XS = 2.0 ** 11
PSC = 2.0 ** 15
WS = 2.0 ** 14
QSC = 2.0 ** -19
OSC = 2.0 ** -14
HS = 2.0 ** 6
WTS = 2.0 ** 5
SLOTS = 6
ARENA_WORDS = 60 * 256

ALU = mybir.AluOpType
ACT = mybir.ActivationFunctionType
AX = mybir.AxisListType.X
F32 = mybir.dt.float32
F16 = mybir.dt.float16
BF16 = mybir.dt.bfloat16
U32 = mybir.dt.uint32
RMAX = bass.bass_isa.ReduceOp.max


def build(nc, x, ctx_in, mask, g_xattn, g_ffn, Wq0, bq0, Wk0, bk0, Wv0, bv0, Wo0, bo0, rhs,
          Wq1, Wk1, Wv1, Wo1, bo1, protos, Bw, Aw, biasw, temp, out):
    with ExitStack() as ctx:
        def sb(name, shape, dt=F32):
            return ctx.enter_context(nc.sbuf_tensor(name, shape, dt))

        def sem(name):
            return ctx.enter_context(nc.semaphore(name))

        PS = ctx.enter_context(nc.psum_tensor("PS", [P, 8, 512], F32))
        S_BANK, G6 = 0, 6
        ATTN = PS[:, 3, :]
        FFN0, QT, OT = (PS[:, k, :] for k in (4, 5, 6))
        HIDDEN, DOTS, FFN1 = (PS[:, k, :] for k in (4, 5, 6))

        X = sb("X", [P, TILES, D])
        KF = sb("KF", [P, B * 2 * FT * HK], F16)
        VW = sb("VW", [P, B * 2 * ROWT * D], F16)
        Kf = KF[:, :].rearrange("p (b w f k) -> p b w f k", b=B, w=2, f=FT)
        Vw = VW[:, :].rearrange("p (b w i o) -> p b w i o", b=B, w=2, i=ROWT)

        ARENA = sb("ARENA", [P, ARENA_WORDS])
        at = [0]

        def arena(words, dt=F32, start=None):
            a = at[0] if start is None else start
            at[0] = a + words
            assert at[0] <= ARENA_WORDS
            return ARENA[:, a:a + words] if dt == F32 else ARENA[:, a:a + words].bitcast(dt)

        xn = arena(D)
        xs = arena(D, F16).rearrange("p (w d) -> p w d", w=2)
        xT = arena(D, F16).rearrange("p (w f t) -> p w f t", w=2, f=FT)
        sS = arena(HK)
        ps = arena(HKP, F16).rearrange("p (w k) -> p w k", w=2)
        pT = arena(HKP, F16).rearrange("p (w i t) -> p w i t", w=2, i=ROWT)
        xf = arena(D)
        ffn = at[0]
        xq = arena(D)
        qs = arena(D // 2, F16)
        qT = arena(D // 2, F16).rearrange("p (f t) -> p f t", f=FT)
        dq = arena(D)
        loop_end = [at[0]]
        ds = arena(D, F16, start=ffn).rearrange("p (w d) -> p w d", w=2)
        dT = arena(D, F16).rearrange("p (w f t) -> p w f t", w=2, f=FT)
        hw = arena(D)
        hs = arena(D + P // 2, F16)
        hT = arena(D + P // 2, F16).rearrange("p (i t) -> p i t", t=P)
        junk = arena(D // 2, F16)
        loop_end.append(at[0])
        rq = arena(FT * D // 2, F16, start=loop_end[0]).rearrange("p (f o) -> p f o", f=FT)
        cg = arena(D)
        row = arena(B * HK // 2, BF16).rearrange("p (b k) -> p b k", b=B)
        spare = at[0]
        early = arena(2 * FT * D).rearrange("p (c d) -> p c d", c=2 * FT)
        rraw = arena(FT * D, start=spare).rearrange("p (f o) -> p f o", f=FT)
        rabs = arena(D)
        rests = [None, arena(HK), None]
        bt = arena(FT * D, F16, start=loop_end[1]).rearrange("p (w f n) -> p w f n", w=2, f=FT)
        ad = arena(FT * D, F16).rearrange("p (w f n) -> p w f n", w=2, f=FT)
        pw = arena(FT * PROTOS, F16).rearrange("p (w f n) -> p w f n", w=2, f=FT)
        p2 = arena(PROTOS)
        bs = arena(D // 2, F16)
        bsf = arena(D)

        VB = arena(8 * 384, start=0)
        VT = arena(8 * B * KEYS)
        WOT = arena(8 * D).rearrange("p (j d) -> p j d", j=8)
        assert at[0] <= loop_end[1]
        BO = arena(D, start=spare + 2 * FT * D)
        rests[2] = arena(D)
        WQT0 = arena(FT * D, start=3 * D).rearrange("p (j n) -> p j n", j=FT)
        WOT0 = arena(FT * D).rearrange("p (j d) -> p j d", j=FT)
        f32vw = VW[:, :].bitcast(F32)
        ring = f32vw[:, 0:SLOTS * D].rearrange("p (s d) -> p s d", s=SLOTS)
        wqn = f32vw[:, SLOTS * D:SLOTS * D + 8 * D].rearrange("p (j d) -> p j d", j=8)
        KB = f32vw[:, SLOTS * D + 8 * D:SLOTS * D + 8 * D + HEADS * B * KEYS]
        f32kf = KF[:, :].bitcast(F32)
        craw = f32kf[:, 0:B * D].rearrange("p (b d) -> p b d", b=B)
        cT = f32kf[:, 1024:1024 + FT * B * KEYS].rearrange("p (f k) -> p f k", f=FT)
        WT = f32kf[:, 2048:2048 + 2 * D].rearrange("p (u f n) -> p u f n", u=2, f=FT)
        def tiles_of(layer):
            return 4 * (layer + 1)

        def per_tile(layer):
            return HEADS // tiles_of(layer)

        def first_row_tile(layer, j):
            return per_tile(layer) * KEYS * j // P

        def last_row_tile(layer, j):
            return (per_tile(layer) * KEYS * (j + 1) - 1) // P

        def part(region, start, words, dt=F16):
            return region[:, start:start + words].bitcast(dt)

        blocks_v = [(b, j, i) for b in range(B) for j in range(FT) for i in range(first_row_tile(0, j), last_row_tile(0, j) + 1)]
        block_no = {key: n for n, key in enumerate(blocks_v)}
        groups_v = [blocks_v[n:n + 4] for n in range(0, len(blocks_v), 4)]
        kw, vw = HEADS * B * KEYS, len(blocks_v) * P
        Wq16 = part(f32kf, 0, FT * D).rearrange("p (w j f n) -> p w j f n", w=2, j=FT, f=FT)
        K16 = part(f32kf, FT * D, kw).rearrange("p (w j b k) -> p w j b k", w=2, j=FT, b=B)
        V16 = part(f32kf, FT * D + kw, vw).rearrange("p (w n d) -> p w n d", w=2, d=P)
        rests[0] = f32kf[:, FT * D + kw + vw:FT * D + kw + vw + HK]
        qT16, oT16 = (part(f32kf, FT * D + kw + vw + k * D, D).rearrange("p (w j t) -> p w j t", w=2, j=FT)
                      for k in range(2))
        Wo16 = part(f32vw, 0, FT * D).rearrange("p (w j d) -> p w j d", w=2, j=FT)
        rowbo = part(f32vw, FT * D, D // 2, BF16)
        sS0 = f32vw[:, FT * D + D // 2:FT * D + D // 2 + HK]
        V0 = f32vw[:, SLOTS * D:SLOTS * D + B * FT * 512]
        weights0 = [(part(f32kf, 0, FT * D).rearrange("p (w n) -> p w n", w=2), WQT0.rearrange("p j n -> p (j n)"), 8),
                    (part(f32kf, FT * D, kw).rearrange("p (w n) -> p w n", w=2), KB, 9),
                    (part(f32vw, 0, FT * D).rearrange("p (w n) -> p w n", w=2), WOT0.rearrange("p j d -> p (j d)"), 11)]
        btf = f32kf[:, 3072:3072 + FT * D].rearrange("p (f n) -> p f n", f=FT)
        adf = f32kf[:, 5120:5120 + FT * D].rearrange("p (f n) -> p f n", f=FT)
        ptf = f32kf[:, 7168:7168 + FT * PROTOS].rearrange("p (f n) -> p f n", f=FT)
        psq = f32kf[:, 7296:7296 + FT * PROTOS].rearrange("p (f n) -> p f n", f=FT)
        praw = f32kf[:, 7424:7424 + D]

        ident = sb("ident", [P, P])
        sel16 = sb("sel16", [P, P], BF16)
        ones32 = sb("ones32", [P, P])
        e80 = sb("e80", [P, P])
        iota32 = sb("iota32", [P, PROTOS])
        gates = sb("gates", [P, 4])
        tinv = sb("tinv", [P, 1])
        magic = sb("magic", [P, 2])
        half = sb("half", [P, 2])
        mone = sb("mone", [P, 1])
        bias_q = sb("bias_q", [P, 3, 4])
        mk = sb("mk", [P, B, KEYS])
        amx = sb("amx", [P, 6, 8])
        amr = sb("amr", [P, 6, 8])
        amxe = sb("amxe", [P, 4])
        amre = sb("amre", [P, 4])
        sc = sb("sc", [P, 16])
        st = sb("st", [P, 2, 2, 6])
        mv = sb("mv", [P, 2, 2, 2])
        rstd = sb("rstd", [P, 2, 2, 3])
        mx = sb("mx", [P, 2, HEADS])
        smx = sb("smx", [P, 2, 3, HEADS])
        lsb = sb("lsb", [P, 2, 4])
        rt = sb("rt", [P, 2, PROTOS])
        m8 = sb("m8", [P, 8])
        i8 = sb("i8", [P, 8], U32)
        rw = sb("rw", [P, 16])
        x2 = sb("x2", [P, 2])
        oh = sb("oh", [P, 2, PROTOS])
        wt = sb("wt", [P, PROTOS])
        tg = sb("tg", [P, 8])

        def scores_bank(k):
            return PS[:, S_BANK + k, 0:BANK_HEADS[k] * KEYS]

        def by_head(ap):
            return ap.rearrange("p (h k) -> p h k", k=KEYS)

        def scores_parts():
            two = PS[:, S_BANK:S_BANK + 2, 0:6 * KEYS].rearrange("p b (h k) -> p b h k", k=KEYS)
            return [(two, slice(0, 12 * KEYS), slice(0, 12), (2, 6)),
                    (by_head(PS[:, S_BANK + 2, 0:4 * KEYS]), slice(12 * KEYS, HK), slice(12, 16), (4,))]

        def cut(ap, shape):
            return ap.rearrange("p (a b) -> p a b", a=shape[0]) if len(shape) == 2 else ap

        KBlk = [KB.rearrange("p (j b k) -> p j b k", j=tiles_of(l), b=B) for l in range(2)]
        VBlk = VB.rearrange("p (j c) -> p j c", j=8)
        VTl = VT.rearrange("p (j b k) -> p j b k", j=8, b=B)

        s_const = sem("consts_made")
        s_x = [sem(f"x_loaded_in_{name}_steps") for name in ("even", "odd")]
        s_hi = sem("weights0_hi")
        s_v_turned = sem("values0_turned")
        s_v_hi = sem("values0_hi")
        s_v_lo = sem("values0_lo")
        s_small = sem("small_inputs_loaded")
        s_ctx = sem("context_loaded")
        s_slot = [sem(f"chunk_slot{i}_loaded") for i in range(SLOTS)]
        s_wq = sem("wq_loaded")
        s_early = sem("experts_loaded")
        s_measured = sem("experts_measured")
        s_praw = sem("prototypes_loaded")
        s_bo = sem("bo_loaded")
        s_zero = sem("setup_zeroed")
        s_pad = sem("probs_padded")
        s_cT_ps = sem("context_turned")
        s_cT = sem("context_turned_copied")
        s_turn = sem("chunk_turned")
        s_turned = sem("chunk_turned_copied")
        s_kv_ps = sem("kv_projected")
        s_kv = sem("kv_copied")
        s_am = sem("absmax_per_partition")
        s_amr = sem("absmax_over_partitions")
        s_ame = sem("expert_absmax_per_partition")
        s_amre = sem("expert_absmax_over_partitions")
        s_sc = sem("scales_step")
        s_scale = sem("scales_ready")
        s_escale = sem("expert_scales_ready")
        s_kf_ps = sem("folded_keys_product")
        s_kfh = sem("folded_keys_hi")
        s_kfl = sem("folded_keys_lo")
        s_vb = sem("value_window_filled")
        s_vw_ps = sem("folded_values_product")
        s_vwh = sem("folded_values_hi")
        s_vwl = sem("folded_values_lo")
        s_row_ps = sem("score_row_product")
        s_row = [sem(f"row{i}_step") for i in range(3)]
        s_row_whole = sem("whole_rows")
        s_rhs = sem("rhs_loaded")
        s_rmax = sem("rhs_absmax")
        s_rmaxr = sem("rhs_absmax_over_partitions")
        s_rq = sem("rhs_step")
        s_pr_ps = sem("prototypes_turned")
        s_pr = sem("prototypes_step")
        s_p2_ps = sem("prototype_norms")
        s_dw = sem("expert_weights_hi")
        s_dwl = sem("expert_weights_lo")
        s_gate = sem("gates_ready")

        L = {}
        for name in ("stats", "mean_var", "var_eps", "rstd", "ln", "ln_hi", "ln_lo", "x_T", "scores", "max",
                     "shifted", "exp", "sum", "inv_sum", "probs", "probs_hi", "probs_lo", "p_T_hi", "p_T_lo", "attn_out",
                     "x_attn", "f_stats", "f_mean_var", "f_var_eps", "f_rstd", "f_ln", "absmax", "lhs_scale",
                     "lhs_inv", "quant", "quant_int", "q_T", "ffn0_out", "ffn0_scaled", "x_ffn0",
                     "q", "q_hi", "q_lo", "pv", "pv_hi", "pv_lo", "scaled_inv", "ln_bias", "f_ln_bias", "quant_scaled", "quant_round", "ffn0_col",
                     "sq_sum", "d_hi", "d_lo", "d_T", "hidden", "dots", "dist_a", "dist_b", "best", "best_at",
                     "route", "gap", "gap_exp", "weighted", "h_hi", "w_hi", "h_lo", "w_lo", "h_T", "ffn1_out",
                     "x_ffn1", "stored"):
            L[name] = sem(name)

        def chunk_list(layer):
            n = tiles_of(layer)
            by_rows = ((Wk0, Wv0, Wq0), (Wk1, Wv1))[layer]
            wo = (Wo0, Wo1)[layer]
            src = [w[P * j:P * j + P, :] for w in by_rows for j in range(n)]
            src += [wo[:, P * j:P * j + P].rearrange("(q p) c -> p q c", p=P) for j in range(n)]
            return src

        chunks0 = 4 * tiles_of(0)
        n_exp = 2 * FT
        first_kv = 2 * tiles_of(0)
        first_link = 9
        units = B * FT
        x_first = 4
        VALUE_BANKS = 5
        LN_AT = B * ROWT - 7

        def values_bank(v):
            return (6, 7, 3, 4, 5)[v % VALUE_BANKS]


        x_rows = x.rearrange("b (t p) d -> p (b t) d", p=P)

        def setup0():
            J, hpt = tiles_of(0), per_tile(0)
            dhd = P // hpt
            chunks = chunk_list(0)
            n_kv = 2 * J

            with nc.Block() as block:
                @block.sync
                def _(sp):
                    sp.dma_start(craw[0:KEYS], ctx_in.rearrange("b k d -> k b d")).then_inc(s_ctx, 16)
                    for c, src in enumerate(chunks):
                        if c >= SLOTS:
                            sp.wait_ge(s_turn, c - SLOTS + 1)
                        dst = ring[:, c % SLOTS, :]
                        if c >= n_kv + J:
                            dst = dst.rearrange("p (q c) -> p q c", q=FT)
                        sp.dma_start(dst, src).then_inc(s_slot[c % SLOTS], 16)
                        if c in (n_kv + J - 1, len(chunks) - 1):
                            k = c // (len(chunks) - 1)
                            tiles = slice(x_first * k, x_first * k + x_first)
                            sp.dma_start(X[:, tiles, :], x_rows[:, tiles, :]).then_inc(s_x[k], 16)
                    sp.dma_start(rraw, rhs.rearrange("(f p) o -> p f o", p=P)).then_inc(s_rhs, 16)
                    sp.wait_ge(L["ln_lo"], 1)
                    sp.dma_start_transpose(xT.rearrange("p w f t -> p (w f) t"),
                                           xs.rearrange("p w d -> p (w d)")).then_inc(L["x_T"], 16)

                @block.gpsimd
                def _(pool):
                    pool.memset(ident[:], 0.0).then_inc(s_const, 1)
                    pool.memset(e80[:], 0.0).then_inc(s_const, 1)
                    pool.memset(sel16[:], 0.0).then_inc(s_const, 1)
                    pool.wait_ge(s_const, 3)
                    pool.affine_select(out=ident[:], in_=ident[:], compare_op=ALU.not_equal, fill=1.0, base=0,
                                       pattern=[[-1, P]], channel_multiplier=1)
                    pool.affine_select(out=e80[:], in_=e80[:], compare_op=ALU.not_equal, fill=1.0,
                                       base=-(HK % P), pattern=[[1, P]], channel_multiplier=P).then_inc(s_const, 1)
                    pool.memset(amx[:], 0.0)
                    pool.memset(amxe[:], 0.0)
                    pool.memset(KB, 0.0).then_inc(s_zero, 1)
                    pool.memset(V0, 0.0).then_inc(s_zero, 1)
                    pool.memset(ones32[:], 1.0)
                    pool.memset(magic[:, 0:1], MAGIC)
                    pool.memset(magic[:, 1:2], -MAGIC)
                    pool.memset(half[:, 0:1], -0.5)
                    pool.memset(half[:, 1:2], 0.5)
                    pool.memset(mone[:], -1.0)
                    pool.iota(iota32[:], [[1, PROTOS]], base=0, channel_multiplier=0,
                              allow_small_or_imprecise_dtypes=True).then_inc(s_zero, 1)
                    pool.wait_ge(s_zero, 3)
                    pool.wait_ge(L["mean_var"], 1)
                    pool.tensor_scalar(rstd[:, 0, 0, 0:1], mv[:, 0, 0, 1:2], EPS, None, ALU.add).then_inc(L["var_eps"], 1)
                    pool.wait_ge(L["var_eps"], 1)
                    pool.tensor_tensor(rstd[:, 0, 0, 1:2], rstd[:, 0, 0, 0:1], half[:, 0:1],
                                       ALU.pow).then_inc(L["rstd"], 1)
                    pool.wait_ge(L["rstd"], 1)
                    pool.tensor_scalar(rstd[:, 0, 0, 2:3], mv[:, 0, 0, 0:1], rstd[:, 0, 0, 1:2], -1.0, ALU.mult,
                                       ALU.mult).then_inc(L["ln_bias"], 1)
                    pool.wait_ge(L["ln_bias"], 1)
                    pool.wait_ge(s_am, 1)
                    pool.partition_all_reduce(amr[:].rearrange("p a b -> p (a b)"), amx[:].rearrange("p a b -> p (a b)"),
                                              P, RMAX).then_inc(s_amr, 1)
                    pool.wait_ge(s_amr, 1)
                    for n in range(2):
                        for item in range(3):
                            row_rest(pool, item, n)

                @block.scalar
                def _(act):
                    act.dma_start(tg[:, 0:2], g_xattn.partition_broadcast(P)).then_inc(s_small, 16)
                    act.dma_start(tg[:, 2:4], g_ffn.partition_broadcast(P)).then_inc(s_small, 16)
                    act.dma_start(tg[:, 4:5], temp.partition_broadcast(P)).then_inc(s_small, 16)
                    act.dma_start(mk[32:33], mask.rearrange("(a b) k -> a b k", a=1)).then_inc(s_small, 16)
                    for k, vec in enumerate((bq0, bk0, bv0)):
                        act.dma_start(bias_q[:, k, :], vec.rearrange("(j p) -> p j", p=P),
                                      allow_slow_non_contiguous=True).then_inc(s_small, 16)
                    act.dma_start(BO, bo0.partition_broadcast(P)).then_inc(s_bo, 16)
                    act.wait_ge(s_small, 16 * 7)
                    act.activation(gates[:], tg[:, 0:4], ACT.Tanh).then_inc(s_gate, 1)
                    act.wait_ge(s_cT_ps, 1)
                    act.copy(cT, PS[:, 0:2, 0:2 * B * KEYS].rearrange("p a (f k) -> p a f k", f=2)).then_inc(s_cT, 1)
                    for c in range(len(chunks)):
                        act.wait_ge(s_turn, c + 1)
                        src = PS[:, G6 + c % 2, :]
                        if 2 <= c < n_kv:
                            act.wait_ge(s_kv_ps, c - 1)
                        if c < n_kv:
                            dst = WT[:, c % 2].rearrange("p f n -> p (f n)")
                        else:
                            dst = WQT0[:, c - n_kv] if c < n_kv + J else WOT0[:, c - n_kv - J]
                        act.copy(dst, src).then_inc(s_turned, 1)
                    act.wait_ge(L["ln_bias"], 1)
                    act.activation(xn, X[:, 0, :], ACT.Identity, bias=rstd[:, 0, 0, 2:3],
                                   scale=rstd[:, 0, 0, 1:2]).then_inc(L["ln"], 1)
                    act.wait_ge(L["ln"], 1)
                    act.activation(xs[:, 0], xn, ACT.Copy, scale=XS).then_inc(L["ln_hi"], 1)
                    act.wait_ge(s_scale, 1)
                    for n, (halves16, raw, k) in enumerate(weights0):
                        act.activation(halves16[:, 0], raw, ACT.Copy, scale=sc[:, k:k + 1]).then_inc(s_hi, 1)
                        if n == 1:
                            for item in range(3):
                                row_piece(act, item, 0)
                    for n, group in enumerate(groups_v):
                        act.wait_ge(s_v_turned, n + 1)
                        act.activation(V16[:, 0, 4 * n:4 * n + len(group), :].rearrange("p n d -> p (n d)"),
                                       PS[:, G6 + n % 2, 0:P * len(group)], ACT.Copy,
                                       scale=sc[:, 10:11]).then_inc(s_v_hi, 1)
                        if 2 <= n < 5:
                            row_piece(act, n - 2, 1)
                    for item in range(3):
                        row_piece(act, item, 2)

                @block.tensor
                def _(pe):
                    def turn(c):
                        pe.wait_ge(s_slot[c % SLOTS], 16 * (c // SLOTS + 1))
                        if c >= 2:
                            pe.wait_ge(s_turned, c - 1)
                        for q in range(FT):
                            mm = pe.transpose(PS[:, G6 + c % 2, P * q:P * q + P], ring[:, c % SLOTS, P * q:P * q + P],
                                              ident[:])
                        mm.then_inc(s_turn, 1)

                    def project(c):
                        pe.wait_ge(s_turned, c + 1)
                        if c >= 2:
                            pe.wait_ge(s_kv, c - 1)
                        for f in range(FT):
                            mm = pe.matmul(PS[:, 4 + c % 2, 0:B * KEYS], WT[:, c % 2, f, :], cT[:, f, :],
                                           start=(f == 0), stop=(f == FT - 1))
                        mm.then_inc(s_kv_ps, 1)

                    pe.wait_ge(s_const, 4)
                    pe.wait_ge(s_ctx, 16)
                    for b in range(B):
                        for f in range(FT):
                            mm = pe.transpose(PS[:, f // 2, B * KEYS * (f % 2) + KEYS * b:B * KEYS * (f % 2) + KEYS * b + KEYS],
                                              craw[0:KEYS, b, P * f:P * f + P], ident[0:KEYS, 0:KEYS])
                    mm.then_inc(s_cT_ps, 1)
                    turn(0)
                    pe.wait_ge(s_cT, 1)
                    for c in range(len(chunks)):
                        if c + 1 < len(chunks):
                            turn(c + 1)
                        if c < n_kv:
                            project(c)
                    pe.wait_ge(s_kv, n_kv)
                    for b in range(B):
                        for p in range(HEADS // 2):
                            j, r = divmod(2 * p, hpt)
                            mm = pe.matmul(PS[:, 3 * b + p // 3, 2 * KEYS * (p % 3):2 * KEYS * (p % 3) + 2 * KEYS],
                                           bias_q[:, 0, j:j + 1].to_broadcast([P, P]),
                                           KBlk[0][:, j, b, KEYS * r:KEYS * r + 2 * KEYS], start=True, stop=True)
                        mm.then_inc(s_row_ps, 1)
                    pe.wait_ge(s_turned, len(chunks))
                    for n, group in enumerate(groups_v):
                        if n >= 2:
                            pe.wait_ge(s_v_lo, n - 1)
                        for m, (b, j, i) in enumerate(group):
                            c = 512 * (FT * b + j) + P * (i - first_row_tile(0, j))
                            mm = pe.transpose(PS[:, G6 + n % 2, P * m:P * m + P], V0[:, c:c + P], ident[:])
                        mm.then_inc(s_v_turned, 1)

                @block.vector
                def _(dve):
                    done = [0]

                    def link(ins):
                        done[0] += 1
                        ins.then_inc(s_sc, 1)
                        dve.wait_ge(s_sc, done[0])

                    def largest(kind, j, src):
                        return dve.tensor_reduce(amx[:, kind, j:j + 1], src, AX, ALU.max, apply_absolute_value=True)

                    def lo_half(n):
                        halves16, raw, k = weights0[n]
                        dve.wait_ge(s_hi, n + 1)
                        dve.scalar_tensor_tensor(halves16[:, 1], raw, sc[:, k:k + 1], halves16[:, 0], ALU.mult,
                                                 ALU.subtract)

                    dve.wait_ge(s_const, 4)
                    for q in range(0, P, 32):
                        dve.memset(sel16[q:q + 1, :], 1.0)
                    dve.wait_ge(s_zero, 2)
                    dve.wait_ge(s_small, 16 * 7)
                    dve.tensor_reduce(amx[:, 5, 0:2], bias_q[:, 1:3, :], AX, ALU.max, apply_absolute_value=True)
                    for c in range(n_kv):
                        dve.wait_ge(s_kv_ps, c + 1)
                        j = c % J
                        src = PS[:, 4 + c % 2, 0:B * KEYS]
                        largest(1 + c // J, j, src)
                        src = src.rearrange("p (b k) -> p b k", b=B)
                        off = 0 if c < J else hpt * KEYS * j - P * first_row_tile(0, j)
                        block_of = KBlk[0] if c < J else V0.rearrange("p (b j c) -> p j b c", b=B, j=J)
                        for r in range(hpt):
                            rows = slice(dhd * r, dhd * r + dhd)
                            ins = dve.tensor_scalar(block_of[rows, j, :, off + KEYS * r:off + KEYS * r + KEYS], src[rows],
                                                    bias_q[rows, 1 + c // J, j:j + 1], None, ALU.add)
                        ins.then_inc(s_kv, 1)
                    dve.wait_ge(s_x[0], 16)
                    dve.bn_stats(st[:, 0, 0, :], X[:, 0, :]).then_inc(L["stats"], 1)
                    dve.wait_ge(L["stats"], 1)
                    dve.bn_aggr(mv[:, 0, 0, :], st[:, 0, 0, :]).then_inc(L["mean_var"], 1)
                    for c in range(2 * J):
                        dve.wait_ge(s_turned, n_kv + c + 1)
                        ins = largest(0, c, WQT0[:, c]) if c < J else largest(3, c - J, WOT0[:, c - J])
                    ins.then_inc(s_am, 1)
                    dve.wait_ge(s_amr, 1)
                    link(dve.tensor_reduce(sc[:, 4:8], amr[:, 0:4], AX, ALU.max))
                    link(dve.tensor_tensor(sc[:, 5:7], sc[:, 5:7], amr[:, 5, 0:2], ALU.add))
                    link(dve.tensor_scalar(sc[:, 4:8], sc[:, 4:8], TINY, None, ALU.max))
                    link(dve.reciprocal(sc[:, 8:12], sc[:, 4:8]))
                    link(dve.tensor_scalar(sc[:, 8:12], sc[:, 8:12], WS, None, ALU.mult))
                    dve.scalar_tensor_tensor(sc[:, 2:3], sc[:, 4:5], float(dhd) ** -0.5 / (XS * QSC * WS * WS), sc[:, 5:6],
                                             ALU.mult, ALU.mult)
                    dve.scalar_tensor_tensor(sc[:, 12:13], sc[:, 8:9], XS * QSC, sc[:, 9:10], ALU.mult, ALU.mult)
                    dve.wait_ge(s_gate, 1)
                    link(dve.scalar_tensor_tensor(sc[:, 3:4], sc[:, 6:7], 1.0 / (PSC * OSC * WS * WS), sc[:, 7:8],
                                                  ALU.mult, ALU.mult))
                    dve.tensor_scalar(sc[:, 3:4], sc[:, 3:4], gates[:, 0:1], None, ALU.mult)
                    dve.scalar_tensor_tensor(sc[:, 13:14], sc[:, 10:11], PSC * OSC, sc[:, 11:12], ALU.mult,
                                             ALU.mult).then_inc(s_scale, 1)
                    dve.wait_ge(L["ln_hi"], 1)
                    dve.scalar_tensor_tensor(xs[:, 1], xn, XS, xs[:, 0], ALU.mult, ALU.subtract).then_inc(L["ln_lo"], 1)
                    dve.wait_ge(s_scale, 1)
                    for item in range(3):
                        row_whole(dve, item)
                    lo_half(0)
                    lo_half(1)
                    for item in range(3):
                        row_mask(dve, item)
                    lo_half(2)
                    for n, group in enumerate(groups_v):
                        dve.wait_ge(s_v_hi, n + 1)
                        lo, hi = (V16[:, w, 4 * n:4 * n + len(group), :].rearrange("p n d -> p (n d)") for w in (1, 0))
                        dve.scalar_tensor_tensor(lo, PS[:, G6 + n % 2, 0:P * len(group)], sc[:, 10:11], hi, ALU.mult,
                                                 ALU.subtract).then_inc(s_v_lo, 1)
                    link(dve.tensor_scalar(tg[:, 5:6], tg[:, 4:5], -1.0, None, ALU.mult))
                    link(dve.tensor_tensor(tg[:, 5:6], tg[:, 5:6], tg[:, 4:5], ALU.max))
                    link(dve.tensor_scalar(tg[:, 5:6], tg[:, 5:6], 0.1, None, ALU.max))
                    dve.reciprocal(tinv[:], tg[:, 5:6])

        def row_terms(item, rows):
            if item == 2:
                return [(BO[rows], slice(0, D), False)]
            return [(PS[rows, 3 * item:3 * item + 2, 0:6 * KEYS], slice(0, 12 * KEYS), True),
                    (PS[rows, 3 * item + 2, 0:4 * KEYS], slice(12 * KEYS, HK), False)]

        def row_of(item):
            return row[:, item, :] if item < 2 else rowbo

        def halves(ap, two):
            return ap.rearrange("p (a k) -> p a k", a=2) if two else ap

        def row_piece(act, item, n):
            dst = row_of(item)
            rows = slice((0, 64, 96)[n], P)
            if n == 0:
                act.wait_ge(s_row_whole, item + 1)
                k = 12 + item // 2
                for src, cols, two in row_terms(item, rows):
                    ins = act.activation(halves(dst[:, cols], two), src, ACT.Copy, scale=sc[:, k:k + 1])
            else:
                act.wait_ge(s_row[item], 2 * n)
                ins = act.copy(dst[rows], rests[item][rows])
            ins.then_inc(s_row[item], 1)

        def row_whole(dve, item):
            rows, k = slice(64, P), 12 + item // 2
            if item < 2:
                dve.wait_ge(s_row_ps, item + 1)
            else:
                dve.wait_ge(s_bo, 16)
            for src, cols, two in row_terms(item, rows):
                ins = dve.tensor_scalar(halves(rests[item][rows, cols], two), src, sc[rows, k:k + 1], None, ALU.mult)
            ins.then_inc(s_row_whole, 1)

        def row_rest(pool, item, n):
            dst, rest = row_of(item), rests[item]
            rows = slice((64, 96)[n], P)
            pool.wait_ge(s_row[item], 2 * n + 1)
            pool.wait_ge(s_row_whole, item + 1)
            pool.tensor_tensor(rest[rows], rest[rows], dst[rows], ALU.subtract).then_inc(s_row[item], 1)
            pool.wait_ge(s_row[item], 2 * n + 2)

        def row_mask(dve, item):
            dst = row_of(item)
            dve.wait_ge(s_row[item], 1)
            if item == 2:
                dve.memset(dst[32:33], 0.0)
            else:
                dve.tensor_scalar(by_head(dst[32:33]), mk[32:33, item:item + 1, :].to_broadcast([1, HEADS, KEYS]),
                                  1.0, NEG, ALU.not_equal, ALU.mult)

        def rhs_absmax(dve):
            dve.wait_ge(s_rhs, 16)
            dve.tensor_reduce(rabs, rraw.rearrange("p f o -> p o f"), AX, ALU.max,
                              apply_absolute_value=True).then_inc(s_rmax, 1)

        def rhs_scales(dve):
            dve.wait_ge(s_rmaxr, 1)
            dve.tensor_scalar(cg, cg, TINY, 1.0 / INT8_MAX, ALU.max, ALU.mult).then_inc(s_rq, 1)
            dve.wait_ge(s_rq, 1)
            dve.reciprocal(rabs, cg).then_inc(s_rq, 1)
            dve.tensor_scalar(cg, cg, gates[:, 2:3], None, ALU.mult)

        def divide_rhs(dve):
            dve.wait_ge(s_rq, 2)
            dve.tensor_tensor(rraw, rraw, rabs.unsqueeze(1).to_broadcast([P, FT, D]), ALU.mult).then_inc(s_rq, 1)

        def quantise_rhs(dve):
            dve.wait_ge(s_rq, 3)
            dve.tensor_scalar(rraw, rraw, MAGIC, MAGIC + INT8_MAX, ALU.add, ALU.min).then_inc(s_rq, 1)
            dve.wait_ge(s_rq, 4)
            dve.tensor_scalar(rq, rraw, MAGIC - INT8_MAX, -MAGIC, ALU.max, ALU.add).then_inc(s_rq, 1)

        def setup1():
            J, hpt = tiles_of(1), per_tile(1)
            dhd = P // hpt
            chunks = chunk_list(1)
            n_kv = 2 * J
            l0 = chunks0
            e0 = chunks0
            a0 = e0 + n_exp
            turned_all = a0 + len(chunks)
            kv0 = first_kv
            n0 = TILES
            scaling = float(dhd) ** -0.5

            with nc.Block() as block:
                @block.sync
                def _(sp):
                    sp.dma_start(craw[0:KEYS], ctx_in.rearrange("b k d -> k b d")).then_inc(s_ctx, 16)
                    for c, src in enumerate(chunks):
                        if c >= SLOTS:
                            sp.wait_ge(s_turn, a0 + c - SLOTS + 1)
                        dst = ring[:, (l0 + c) % SLOTS, :]
                        if c >= n_kv:
                            dst = dst.rearrange("p (q c) -> p q c", q=FT)
                        sp.dma_start(dst, src).then_inc(s_slot[(l0 + c) % SLOTS], 16)
                    sp.wait_ge(L["ln_lo"], n0 + 1)
                    sp.dma_start_transpose(xT.rearrange("p w f t -> p (w f) t"),
                                           xs.rearrange("p w d -> p (w d)")).then_inc(L["x_T"], 16)

                @block.gpsimd
                def _(pool):
                    pool.memset(BO, 0.0)
                    pool.memset(KB, 0.0).then_inc(s_zero, 1)
                    pool.memset(VB, 0.0).then_inc(s_zero, 1)
                    pool.wait_ge(s_zero, 5)

                    def fill_window(b, j):
                        off = hpt * KEYS * j - P * first_row_tile(1, j)
                        for r in range(hpt):
                            rows = slice(dhd * r, dhd * r + dhd)
                            last = pool.tensor_copy(VBlk[rows, j, off + KEYS * r:off + KEYS * r + KEYS],
                                                    VTl[rows, j, b, :])
                        last.then_inc(s_vb, 1)

                    for j in range(J):
                        if j == 0:
                            pool.wait_ge(s_ame, 1)
                            pool.partition_all_reduce(amre[:], amxe[:], P, RMAX).then_inc(s_amre, 1)
                            pool.wait_ge(s_amre, 1)
                        pool.wait_ge(s_kv, kv0 + J + j + 1)
                        fill_window(0, j)
                    pool.wait_ge(s_vb, J)
                    for n, kinds in enumerate((slice(0, 2), slice(2, 5))):
                        pool.wait_ge(s_am, n + 2)
                        pool.partition_all_reduce(amr[:, kinds].rearrange("p a b -> p (a b)"),
                                                  amx[:, kinds].rearrange("p a b -> p (a b)"),
                                                  P, RMAX).then_inc(s_amr, 1)
                        pool.wait_ge(s_amr, n + 2)
                    for j in range(J):
                        pool.wait_ge(s_vw_ps, last_row_tile(1, j) + 1)
                        fill_window(1, j)
                    pool.wait_ge(s_vb, B * J)
                    pool.wait_ge(L["mean_var"], n0 + 1)
                    pool.tensor_scalar(rstd[:, 0, 0, 0:1], mv[:, 0, 0, 1:2], EPS, None, ALU.add).then_inc(L["var_eps"], 1)
                    pool.wait_ge(L["var_eps"], n0 + 1)
                    pool.tensor_tensor(rstd[:, 0, 0, 1:2], rstd[:, 0, 0, 0:1], half[:, 0:1],
                                       ALU.pow).then_inc(L["rstd"], 1)
                    pool.wait_ge(L["rstd"], n0 + 1)
                    pool.tensor_scalar(rstd[:, 0, 0, 2:3], mv[:, 0, 0, 0:1], rstd[:, 0, 0, 1:2], -1.0, ALU.mult,
                                       ALU.mult).then_inc(L["ln_bias"], 1)

                @block.scalar
                def _(act):
                    act.dma_start(praw[0:PROTOS, :], protos).then_inc(s_praw, 16)
                    for c in range(n_exp):
                        act.wait_ge(s_turn, e0 + c + 1)
                        dst = (btf if c < FT else adf)[:, :, P * (c % FT):P * (c % FT) + P]
                        act.copy(dst, PS[:, G6 + c % 2, :].rearrange("p (f n) -> p f n", f=FT)).then_inc(s_turned, 1)
                    act.wait_ge(s_cT_ps, 2)
                    act.copy(cT, PS[:, 0:2, 0:2 * B * KEYS].rearrange("p a (f k) -> p a f k", f=2)).then_inc(s_cT, 1)
                    act.wait_ge(s_measured, 2)
                    for q in range(3):
                        act.dma_start(bsf[PROTOS * q:PROTOS * q + PROTOS, :], biasw).then_inc(s_small, 16)
                    act.dma_start(wqn[:, 0:J, :], Wq1.rearrange("(j p) d -> p j d", p=P)).then_inc(s_wq, 16)
                    act.wait_ge(s_zero, 4)
                    act.dma_start(BO[0:1, :], bo1.rearrange("(a d) -> a d", a=1)).then_inc(s_bo, 16)
                    for c in range(len(chunks)):
                        act.wait_ge(s_turn, a0 + c + 1)
                        src = PS[:, G6 + c % 2, :]
                        if c < n_kv:
                            if c >= 2:
                                act.wait_ge(s_kv_ps, kv0 + c - 1)
                            act.copy(WT[:, c % 2].rearrange("p f n -> p (f n)"), src).then_inc(s_turned, 1)
                        else:
                            act.copy(WOT[:, c - n_kv, :], src).then_inc(s_turned, 1)
                        if 10 <= c < 13:
                            if c == 10:
                                act.wait_ge(s_escale, 1)
                            dst, raw, k = ((bt, btf, 8), (ad, adf, 9), (pw, ptf, 10))[c - 10]
                            act.activation(dst[:, 0], raw, ACT.Copy, scale=sc[:, k:k + 1]).then_inc(s_dw, 1)
                        if c == 13:
                            rows = slice(0, 3 * PROTOS)
                            act.activation(bs[rows], bsf[rows], ACT.Copy, scale=sc[rows, 14:15]).then_inc(s_dw, 1)
                    act.wait_ge(s_scale, 2)
                    act.wait_ge(s_dwl, 1)
                    for u in range(units):
                        b, f = divmod(u, FT)
                        k0 = 3 * (u % 2)
                        act.wait_ge(s_kf_ps, u + 1)
                        act.activation(Kf[:, b, 0, f, 0:12 * KEYS].rearrange("p (a k) -> p a k", a=2),
                                       PS[:, k0:k0 + 2, 0:6 * KEYS], ACT.Copy, scale=sc[:, 0:1]).then_inc(s_kfh, 1)
                        act.activation(Kf[:, b, 0, f, 12 * KEYS:HK], PS[:, k0 + 2, 0:4 * KEYS], ACT.Copy,
                                       scale=sc[:, 0:1]).then_inc(s_kfh, 1)
                    act.wait_ge(s_scale, 3)
                    for v in range(B * ROWT):
                        b, i = divmod(v, ROWT)
                        act.wait_ge(s_vw_ps, v + 1)
                        act.activation(Vw[:, b, 0, i, :], PS[:, values_bank(v), :], ACT.Copy,
                                       scale=sc[:, 1:2]).then_inc(s_vwh, 1)
                        if v == LN_AT + 2:
                            act.wait_ge(L["ln_bias"], n0 + 1)
                            act.activation(xn, X[:, 0, :], ACT.Identity, bias=rstd[:, 0, 0, 2:3],
                                           scale=rstd[:, 0, 0, 1:2]).then_inc(L["ln"], 1)
                            act.wait_ge(L["ln"], n0 + 1)
                            act.activation(xs[:, 0], xn, ACT.Copy, scale=XS).then_inc(L["ln_hi"], 1)

                @block.tensor
                def _(pe):
                    def turn(c, src):
                        if a0 + c >= 2:
                            pe.wait_ge(s_turned, a0 + c - 1)
                        for q in range(FT):
                            mm = pe.transpose(PS[:, G6 + c % 2, P * q:P * q + P], src[:, P * q:P * q + P], ident[:])
                        mm.then_inc(s_turn, 1)

                    def turn_loaded(c):
                        loads = (l0 + c) // SLOTS + 1
                        pe.wait_ge(s_slot[(l0 + c) % SLOTS], 16 * loads)
                        turn(c, ring[:, (l0 + c) % SLOTS, :])

                    def project(c):
                        pe.wait_ge(s_turned, a0 + c + 1)
                        if c >= 2:
                            pe.wait_ge(s_kv, kv0 + c - 1)
                        for f in range(FT):
                            mm = pe.matmul(PS[:, 4 + c % 2, 0:B * KEYS], WT[:, c % 2, f, :], cT[:, f, :],
                                           start=(f == 0), stop=(f == FT - 1))
                        mm.then_inc(s_kv_ps, 1)

                    pe.wait_ge(s_early, 16 * n_exp)
                    for c in range(n_exp):
                        turn(c - n_exp, early[:, c, :])
                    pe.wait_ge(s_ctx, 32)
                    for b in range(B):
                        for f in range(FT):
                            mm = pe.transpose(PS[:, f // 2, B * KEYS * (f % 2) + KEYS * b:B * KEYS * (f % 2) + KEYS * b + KEYS],
                                              craw[0:KEYS, b, P * f:P * f + P], ident[0:KEYS, 0:KEYS])
                    mm.then_inc(s_cT_ps, 1)
                    pe.wait_ge(s_praw, 16)
                    for f in range(FT):
                        mm = pe.transpose(PS[:, 2, PROTOS * f:PROTOS * f + PROTOS], praw[0:PROTOS, P * f:P * f + P],
                                          ident[0:PROTOS, 0:PROTOS])
                    mm.then_inc(s_pr_ps, 1)
                    turn_loaded(0)
                    pe.wait_ge(s_cT, 2)
                    for c in range(len(chunks)):
                        if c + 1 < len(chunks):
                            turn_loaded(c + 1)
                        if c < n_kv:
                            project(c)
                        if c == 0:
                            pe.wait_ge(s_pr, 2)
                            for f in range(FT):
                                mm = pe.matmul(PS[:, 3, 0:PROTOS], ones32[:], psq[:, f, :], start=(f == 0),
                                               stop=(f == FT - 1))
                            mm.then_inc(s_p2_ps, 1)

                    pe.wait_ge(s_wq, 16)
                    pe.wait_ge(s_kv, kv0 + n_kv)
                    pe.wait_ge(s_dwl, 1)
                    for u in range(units):
                        b, f = divmod(u, FT)
                        if u >= 2:
                            pe.wait_ge(s_kfl, u - 1)
                        for p in range(HEADS // 2):
                            j, r = divmod(2 * p, hpt)
                            mm = pe.matmul(PS[:, 3 * (u % 2) + p // 3, 2 * KEYS * (p % 3):2 * KEYS * (p % 3) + 2 * KEYS],
                                           wqn[:, j, P * f:P * f + P], KBlk[1][:, j, b, KEYS * r:KEYS * r + 2 * KEYS],
                                           start=True, stop=True)
                        mm.then_inc(s_kf_ps, 1)
                    pe.wait_ge(s_bo, 32)
                    pe.wait_ge(s_turned, turned_all)
                    for v in range(B * ROWT):
                        b, i = divmod(v, ROWT)
                        if v == 2:
                            pe.wait_ge(s_kfl, units)
                        reach = [j for j in range(J) if first_row_tile(1, j) <= i <= last_row_tile(1, j)]
                        pe.wait_ge(s_vb, b * J + reach[-1] + 1)
                        if v >= VALUE_BANKS:
                            pe.wait_ge(s_vwl, v - VALUE_BANKS + 1)
                        todo = [(VBlk[:, j, P * (i - first_row_tile(1, j)):P * (i - first_row_tile(1, j)) + P],
                                 WOT[:, j, :]) for j in reach]
                        if i == HK // P:
                            todo.append((e80[:], BO))
                        for n, (lhsT, r) in enumerate(todo):
                            mm = pe.matmul(PS[:, values_bank(v), :], lhsT, r, start=(n == 0), stop=(n == len(todo) - 1))
                        mm.then_inc(s_vw_ps, 1)

                @block.vector
                def _(dve):
                    done = [first_link]

                    def link(ins):
                        done[0] += 1
                        ins.then_inc(s_sc, 1)
                        dve.wait_ge(s_sc, done[0])

                    def largest(kind, j, src):
                        return dve.tensor_reduce(amx[:, kind, j:j + 1], src, AX, ALU.max, apply_absolute_value=True)

                    dve.wait_ge(s_early, 16 * n_exp)
                    for k in range(2):
                        dve.tensor_reduce(amxe[:, k:k + 1], early[:, FT * k:FT * k + FT, :].rearrange("p c d -> p (c d)"),
                                          AX, ALU.max, apply_absolute_value=True).then_inc(s_measured, 1)
                    dve.wait_ge(s_zero, 4)
                    prototypes(dve)
                    for c in range(n_kv):
                        dve.wait_ge(s_kv_ps, kv0 + c + 1)
                        j = c % J
                        src = PS[:, 4 + c % 2, 0:B * KEYS].rearrange("p (b k) -> p b k", b=B)
                        if c >= J:
                            dst = VTl[:, j]
                            ins = dve.tensor_copy(dst, src)
                        else:
                            for r in range(hpt):
                                rows = slice(dhd * r, dhd * r + dhd)
                                dst = KBlk[1][rows, j, :, KEYS * r:KEYS * r + KEYS]
                                ins = dve.tensor_copy(dst, src[rows])
                        ins.then_inc(s_kv, 1)
                        dve.wait_ge(s_kv, kv0 + c + 1)
                        if c < J:
                            largest(1, j, KBlk[1][:, j].rearrange("p b k -> p (b k)"))
                        else:
                            largest(2, j, VTl[:, j].rearrange("p b k -> p (b k)"))
                            if j == 0:
                                dve.wait_ge(s_wq, 16)
                            ins = largest(0, j, wqn[:, j, :])
                            if j == J - 1:
                                ins.then_inc(s_am, 1)
                        expert_weights(dve, link, c)
                    dve.wait_ge(s_amr, 2)
                    link(dve.tensor_reduce(sc[:, 4:6], amr[:, 0:2], AX, ALU.max))
                    link(dve.tensor_scalar(sc[:, 4:6], sc[:, 4:6], TINY, None, ALU.max))
                    link(dve.scalar_tensor_tensor(sc[:, 2:3], sc[:, 4:5], float(dhd), sc[:, 5:6], ALU.mult, ALU.mult))
                    link(dve.reciprocal(sc[:, 0:1], sc[:, 2:3]))
                    link(dve.tensor_scalar(sc[:, 0:1], sc[:, 0:1], WS, None, ALU.mult))
                    dve.tensor_scalar(sc[:, 4:5], sc[:, 0:1], XS, None, ALU.mult)
                    dve.tensor_scalar(sc[:, 2:3], sc[:, 2:3], scaling / (WS * XS), None, ALU.mult).then_inc(s_scale, 1)
                    for u in range(units):
                        b, f = divmod(u, FT)
                        k0 = 3 * (u % 2)
                        dve.wait_ge(s_kfh, 2 * u + 1)
                        dve.scalar_tensor_tensor(Kf[:, b, 1, f, 0:12 * KEYS].rearrange("p (a k) -> p a k", a=2),
                                                 PS[:, k0:k0 + 2, 0:6 * KEYS], sc[:, 0:1],
                                                 Kf[:, b, 0, f, 0:12 * KEYS].rearrange("p (a k) -> p a k", a=2),
                                                 ALU.mult, ALU.subtract)
                        dve.wait_ge(s_kfh, 2 * u + 2)
                        dve.scalar_tensor_tensor(Kf[:, b, 1, f, 12 * KEYS:HK], PS[:, k0 + 2, 0:4 * KEYS], sc[:, 0:1],
                                                 Kf[:, b, 0, f, 12 * KEYS:HK], ALU.mult, ALU.subtract).then_inc(s_kfl, 1)
                        for j in range(u * J // 4, (u + 1) * J // 4):
                            if j < J:
                                dve.wait_ge(s_turned, a0 + n_kv + j + 1)
                                largest(3, j, WOT[:, j, :])
                        if u == 3:
                            dve.wait_ge(s_bo, 32)
                            dve.tensor_reduce(amx[:, 4, 0:1], BO, AX, ALU.max, apply_absolute_value=True).then_inc(s_am, 1)
                        if u == 5:
                            dve.wait_ge(s_amr, 3)
                            link(dve.tensor_reduce(sc[:, 5:8], amr[:, 2:5], AX, ALU.max))
                            link(dve.tensor_scalar(sc[:, 5:8], sc[:, 5:8], TINY, None, ALU.max))
                            link(dve.scalar_tensor_tensor(sc[:, 3:4], sc[:, 5:6], float(dhd), sc[:, 6:7], ALU.mult, ALU.mult))
                            link(dve.tensor_tensor(sc[:, 3:4], sc[:, 3:4], sc[:, 7:8], ALU.max))
                            link(dve.reciprocal(sc[:, 1:2], sc[:, 3:4]))
                            dve.wait_ge(s_gate, 1)
                            dve.tensor_scalar(sc[:, 1:2], sc[:, 1:2], WS, None, ALU.mult)
                            dve.tensor_scalar(sc[:, 3:4], sc[:, 3:4], 1.0 / (WS * PSC), gates[:, 1:2],
                                              ALU.mult, ALU.mult).then_inc(s_scale, 1)
                    for v in range(B * ROWT):
                        b, i = divmod(v, ROWT)
                        dve.wait_ge(s_vwh, v + 1)
                        dve.scalar_tensor_tensor(Vw[:, b, 1, i, :], PS[:, values_bank(v), :], sc[:, 1:2], Vw[:, b, 0, i, :],
                                                 ALU.mult, ALU.subtract).then_inc(s_vwl, 1)
                        if v == LN_AT - 3:
                            dve.bn_stats(st[:, 0, 0, :], X[:, 0, :]).then_inc(L["stats"], 1)
                            dve.wait_ge(L["stats"], n0 + 1)
                            dve.bn_aggr(mv[:, 0, 0, :], st[:, 0, 0, :]).then_inc(L["mean_var"], 1)
                        if v == LN_AT + 3:
                            dve.wait_ge(L["ln_hi"], n0 + 1)
                            dve.scalar_tensor_tensor(xs[:, 1], xn, XS, xs[:, 0], ALU.mult,
                                                     ALU.subtract).then_inc(L["ln_lo"], 1)

        def prototypes(dve):
            dve.wait_ge(s_pr_ps, 1)
            dve.tensor_copy(ptf, PS[:, 2, 0:FT * PROTOS].rearrange("p (f n) -> p f n", f=FT)).then_inc(s_pr, 1)
            dve.wait_ge(s_pr, 1)
            dve.tensor_tensor(psq, ptf, ptf, ALU.mult).then_inc(s_pr, 1)

        def expert_weights(dve, link, c):
            if c == 2:
                dve.wait_ge(s_small, 16 * 10)
                dve.tensor_reduce(amxe[:, 2:3], ptf.rearrange("p f n -> p (f n)"), AX, ALU.max, apply_absolute_value=True)
                dve.tensor_reduce(amxe[0:PROTOS, 3:4], bsf[0:PROTOS], AX, ALU.max,
                                  apply_absolute_value=True).then_inc(s_ame, 1)
            if c == 7:
                dve.wait_ge(s_amre, 1)
                link(dve.tensor_scalar(sc[:, 11:15], amre[:], TINY, None, ALU.max))
                link(dve.tensor_tensor(sc[:, 12:13], sc[:, 11:12], sc[:, 12:13], ALU.mult))
                link(dve.tensor_tensor(sc[:, 12:13], sc[:, 12:13], sc[:, 14:15], ALU.max))
                link(dve.reciprocal(sc[:, 8:11], sc[:, 11:14]))
                link(dve.tensor_scalar(sc[:, 8:11], sc[:, 8:11], WS, None, ALU.mult))
                link(dve.tensor_scalar(sc[:, 14:15], sc[:, 9:10], HS / WTS, None, ALU.mult))
                link(dve.tensor_tensor(sc[:, 9:10], sc[:, 9:10], sc[:, 11:12], ALU.mult))
                link(dve.tensor_scalar(sc[:, 11:12], sc[:, 12:13], 1.0 / (HS * WS), gates[:, 3:4], ALU.mult, ALU.mult))
                dve.tensor_scalar(sc[:, 13:14], sc[:, 13:14], 2.0 / (WS * XS), None, ALU.mult).then_inc(s_escale, 1)
            if 12 <= c < 15:
                dst, src, k = ((bt, btf, 8), (ad, adf, 9), (pw, ptf, 10))[c - 12]
                dve.wait_ge(s_dw, c - 11)
                ins = dve.scalar_tensor_tensor(dst[:, 1].rearrange("p f n -> p (f n)"), src.rearrange("p f n -> p (f n)"),
                                               sc[:, k:k + 1], dst[:, 0].rearrange("p f n -> p (f n)"), ALU.mult,
                                               ALU.subtract)
            if c == 15:
                lo = slice(PROTOS, 2 * PROTOS)
                dve.wait_ge(s_dw, 4)
                dve.scalar_tensor_tensor(bs[lo], bsf[lo], sc[lo, 14:15], bs[lo], ALU.mult, ALU.subtract)
                dve.wait_ge(s_p2_ps, 1)
                dve.tensor_copy(p2, PS[:, 3, 0:PROTOS]).then_inc(s_dwl, 1)

        def loop(layer):
            base = TILES * layer

            LAST = TILES + (6, 4)[layer]
            LOOPS = (((6, PER_B + 2, 0), (PER_B + 4, TILES, 1)), ((6, PER_B, 0), (PER_B + 2, TILES, 1)))[layer]
            UNROLL = (4, 2)[layer]
            SC, OUT, FF = ((2, 4, 5), (1, 2, 3))[layer]
            PROB = ((sS, sS0), (sS, sS))[layer]
            PROB_BUFS = (2, 1)[layer]
            RHS_AT = 1
            X_FROM, X_TO = LOOPS[0][:2]

            def loading(s, batch):
                return layer == 0 and batch == 0 and not isinstance(s, int)

            def x_loads(s, u):
                return 8 * (s - X_FROM - u) + 16

            def steps(eng, step):
                s = 1
                while s < LAST:
                    span = [x for x in LOOPS if x[0] == s]
                    if span:
                        first, end, batch = span[0]
                        with eng.Fori(0, (end - first) // UNROLL) as i:
                            for u in range(UNROLL):
                                step(first + UNROLL * i + u, u % 2, batch)
                        s = end
                    else:
                        step(s, s % 2, None)
                        s += 1

            class At:

                def __init__(self, s, u, batch, lag):
                    self.n = s - lag
                    self.u = (u - lag) % 2
                    self.on = batch is not None or 0 <= s - lag < TILES
                    self.b = batch if batch is not None else (s - lag) // PER_B

            def after(eng, name, at, back=0, per=1, alone=False):
                if isinstance(at.n, int) and at.n - back < 0:
                    return
                wait(eng, L[name], (at.n + (base_of(name) + 1 - back)) * per, alone)

            def wait(eng, signal, value, alone):
                if alone and not isinstance(value, int):
                    value = eng.snap(value)
                    eng.to_reg(value)
                    eng.wait_ge(s_const, 4)
                eng.wait_ge(signal, value)

            def base_of(name):
                shared = ("stats", "mean_var", "var_eps", "rstd", "ln", "ln_hi", "ln_lo", "x_T", "scores", "max",
                          "shifted", "exp", "sum", "inv_sum", "probs", "probs_hi", "probs_lo", "p_T_hi", "p_T_lo",
                          "attn_out", "x_attn", "f_stats", "f_mean_var", "f_var_eps", "f_rstd", "f_ln",
                          "scaled_inv", "ln_bias", "f_ln_bias")
                return base if name in shared else 0

            with nc.Block() as block:
                @block.gpsimd
                def _(pool):
                    def inv_std(at, k, stage):
                        after(pool, stage + "mean_var", at, alone=True)
                        pool.tensor_scalar(rstd[:, k, at.u, 0:1], mv[:, k, at.u, 1:2], EPS, None,
                                           ALU.add).then_inc(L[stage + "var_eps"], 1)
                        after(pool, stage + "var_eps", at)
                        pool.tensor_tensor(rstd[:, k, at.u, 1:2], rstd[:, k, at.u, 0:1], half[:, 0:1],
                                           ALU.pow).then_inc(L[stage + "rstd"], 1)
                        after(pool, stage + "rstd", at, alone=True)
                        pool.tensor_scalar(rstd[:, k, at.u, 2:3], mv[:, k, at.u, 0:1], rstd[:, k, at.u, 1:2], -1.0,
                                           ALU.mult, ALU.mult).then_inc(L[stage + "ln_bias"], 1)

                    def normalise(at):
                        after(pool, "scaled_inv", at)
                        pool.tensor_tensor(by_head(PROB[at.u]), by_head(PROB[at.u]),
                                           smx[:, at.u, 2, :].unsqueeze(2).to_broadcast([P, HEADS, KEYS]),
                                           ALU.mult).then_inc(L["probs"], 1)

                    def probs_lo(at):
                        after(pool, "p_T_lo", at, back=1, per=16)
                        after(pool, "probs_hi", at)
                        pool.tensor_tensor(ps[:, 1, 0:HK], PROB[at.u], ps[:, 0, 0:HK],
                                           ALU.subtract).then_inc(L["probs_lo"], 1)

                    def scale_columns(at):
                        after(pool, "ffn0_scaled", at)
                        pool.tensor_tensor(dq, dq, cg, ALU.mult).then_inc(L["ffn0_col"], 1)

                    def add_ffn0(at):
                        after(pool, "ffn0_col", at, alone=True)
                        pool.tensor_tensor(X[:, at.n, :], X[:, at.n, :], dq, ALU.add).then_inc(L["x_ffn0"], 1)

                    def route(at):
                        n = [0]

                        def link(ins):
                            n[0] += 1
                            ins.then_inc(L["route"], 1)
                            wait(pool, L["route"], at.n * 8 + n[0], True)

                        after(pool, "best_at", at, alone=True)
                        link(pool.tensor_scalar(rw[:, 0:2], m8[:, 0:2], -1.0, None, ALU.mult))
                        link(pool.tensor_tensor(rw[:, 2:4], rw[:, 0:2], half[:, 1:2].to_broadcast([P, 2]), ALU.pow))
                        pool.tensor_copy(rw[:, 4:6], i8[:, 0:2])
                        pool.tensor_tensor(rw[:, 6:7], rw[:, 2:3], rw[:, 3:4], ALU.subtract).then_inc(L["gap"], 1)
                        after(pool, "gap_exp", at, alone=True)
                        link(pool.tensor_scalar(rw[:, 8:9], rw[:, 7:8], 1.0, None, ALU.add))
                        link(pool.tensor_tensor(rw[:, 9:10], rw[:, 8:9], mone[:, 0:1], ALU.pow))
                        link(pool.tensor_tensor(rw[:, 10:11], rw[:, 9:10], rw[:, 7:8], ALU.mult))
                        link(pool.tensor_scalar(oh[:, 0], iota32[:], rw[:, 4:5], rw[:, 9:10], ALU.is_equal, ALU.mult))
                        link(pool.tensor_scalar(oh[:, 1], iota32[:], rw[:, 5:6], rw[:, 10:11], ALU.is_equal, ALU.mult))
                        after(pool, "w_lo", at, back=1)
                        link(pool.tensor_tensor(wt[:], oh[:, 0], oh[:, 1], ALU.add))

                    pool.memset(ps[:, 0, HK:HK + 1], PSC)
                    pool.memset(ps[:, 0, HK + 1:HKP], 0.0)
                    pool.memset(ps[:, 1, HK:HKP], 0.0).then_inc(s_pad, 1)
                    if layer == 1:
                        pool.memset(hs[:, 2 * D + 3 * PROTOS:], 0.0).then_inc(s_pad, 1)

                    def step(s, u, batch):
                        tile = [At(s, u, batch, k) for k in range(7)]
                        if tile[SC + 1].on:
                            probs_lo(tile[SC + 1])
                        if layer == 0 and tile[0].on:
                            inv_std(tile[0], 0, "")
                        if layer == 0 and tile[FF + 1].on:
                            scale_columns(tile[FF + 1])
                        if layer == 0 and tile[OUT].on:
                            inv_std(tile[OUT], 1, "f_")
                        if layer == 1 and tile[4].on:
                            route(tile[4])
                        if layer == 1 and tile[0].on:
                            inv_std(tile[0], 0, "")
                        if tile[SC].on:
                            normalise(tile[SC])
                        if layer == 0 and tile[FF + 1].on:
                            add_ffn0(tile[FF + 1])
                        if layer == 1 and tile[OUT].on:
                            inv_std(tile[OUT], 1, "f_")
                        if layer == 0 and isinstance(s, int) and s == RHS_AT:
                            pool.wait_ge(L["ln_bias"], RHS_AT + 1)
                            pool.wait_ge(s_rmax, 1)
                            pool.partition_all_reduce(cg, rabs, P, RMAX).then_inc(s_rmaxr, 1)
                            pool.wait_ge(s_rmaxr, 1)
                    steps(pool, step)

                @block.scalar
                def _(act):
                    def layernorm(at, k, stage, dst, used):
                        for name in used:
                            after(act, name, at, back=1)
                        after(act, stage + "ln_bias", at)
                        act.activation(dst, X[:, at.n, :], ACT.Identity, bias=rstd[:, k, at.u, 2:3],
                                       scale=rstd[:, k, at.u, 1:2]).then_inc(L[stage + "ln"], 1)

                    def ln_hi(at):
                        after(act, "ln", at)
                        after(act, "x_T", at, back=1, per=16)
                        act.activation(xs[:, 0], xn, ACT.Copy, scale=XS).then_inc(L["ln_hi"], 1)

                    def probs_hi(at):
                        after(act, "probs", at)
                        after(act, "p_T_hi", at, back=1, per=16)
                        act.copy(ps[:, 0, 0:HK], PROB[at.u]).then_inc(L["probs_hi"], 1)

                    def exponentials(at):
                        after(act, "shifted", at)
                        act.activation(PROB[at.u], PROB[at.u], ACT.Exp, scale=sc[:, 2:3]).then_inc(L["exp"], 1)

                    def quant_scaled(at):
                        after(act, "lhs_inv", at)
                        after(act, "quant_int", at, back=1)
                        act.activation(xq, xf, ACT.Copy, scale=lsb[:, at.u, 2:3]).then_inc(L["quant_scaled"], 1)

                    def quant_int(at):
                        after(act, "quant", at)
                        act.activation(xq, xq, ACT.Identity, bias=magic[:, 0:1]).then_inc(L["quant_round"], 1)
                        after(act, "q_T", at, back=1, per=16)
                        after(act, "quant_round", at)
                        act.activation(qs, xq, ACT.Identity, bias=magic[:, 1:2]).then_inc(L["quant_int"], 1)

                    def q_hi(at):
                        after(act, "scores", at, back=1)
                        after(act, "q", at)
                        act.activation(qT16[:, 0].rearrange("p j t -> p (j t)"), QT, ACT.Copy,
                                       scale=QSC).then_inc(L["q_hi"], 1)

                    def pv_hi(at):
                        after(act, "attn_out", at, back=1)
                        after(act, "pv", at)
                        act.activation(oT16[:, 0].rearrange("p j t -> p (j t)"), OT, ACT.Copy,
                                       scale=OSC).then_inc(L["pv_hi"], 1)

                    def scale_ffn0(at):
                        after(act, "x_ffn0", at, back=1)
                        after(act, "ffn0_out", at)
                        act.activation(dq, FFN0, ACT.Copy, scale=lsb[:, at.u, 1:2]).then_inc(L["ffn0_scaled"], 1)

                    def gap_exp(at):
                        after(act, "gap", at)
                        act.activation(rw[:, 7:8], rw[:, 6:7], ACT.Exp, scale=tinv[:, 0:1]).then_inc(L["gap_exp"], 1)

                    def h_hi(at):
                        after(act, "weighted", at)
                        after(act, "h_T", at, back=1, per=16)
                        act.copy(hs[:, 0:D], hw).then_inc(L["h_hi"], 1)
                        act.activation(hs[:, 2 * D:2 * D + 2 * PROTOS].rearrange("p (c n) -> p c n", c=2),
                                       wt[:].unsqueeze(1).to_broadcast([P, 2, PROTOS]), ACT.Copy,
                                       scale=WTS).then_inc(L["w_hi"], 1)

                    def d_hi(at):
                        after(act, "f_ln", at)
                        after(act, "d_T", at, back=1, per=16)
                        act.activation(ds[:, 0], xf, ACT.Copy, scale=XS).then_inc(L["d_hi"], 1)

                    def sq_sum(at):
                        after(act, "f_ln", at)
                        act.activation(junk, xf, ACT.Square, accum_out=x2[:, at.u:at.u + 1]).then_inc(L["sq_sum"], 1)

                    def step(s, u, batch):
                        tile = [At(s, u, batch, k) for k in range(7)]
                        if layer == 0 and tile[OUT].on:
                            pv_hi(tile[OUT])
                        if layer == 0 and tile[FF].on:
                            quant_scaled(tile[FF])
                        if tile[SC + 1].on:
                            probs_hi(tile[SC + 1])
                        if layer == 0:
                            if tile[FF].on:
                                quant_int(tile[FF])
                            if tile[FF + 1].on:
                                scale_ffn0(tile[FF + 1])
                            if tile[SC].on:
                                exponentials(tile[SC])
                            if tile[0].on:
                                layernorm(tile[0], 0, "", xn, ["ln_lo"])
                                ln_hi(tile[0])
                            if tile[1].on:
                                q_hi(tile[1])
                            if tile[OUT].on:
                                layernorm(tile[OUT], 1, "f_", xf, ["quant_scaled"])
                        else:
                            if tile[FF].on:
                                layernorm(tile[FF], 1, "f_", xf, ["d_lo", "sq_sum"])
                                d_hi(tile[FF])
                                sq_sum(tile[FF])
                            if tile[4].on:
                                gap_exp(tile[4])
                                h_hi(tile[4])
                            if tile[0].on:
                                layernorm(tile[0], 0, "", xn, ["ln_lo"])
                                ln_hi(tile[0])
                            if tile[SC].on:
                                exponentials(tile[SC])
                        if layer == 0 and isinstance(s, int) and s in EARLY:
                            act.wait_ge(s_rq, 5)
                            for c in EARLY[s]:
                                j = c % FT
                                if c < FT:
                                    act.dma_start(early[:, j, :], Bw.rearrange("n r d -> (n r) d")[P * j:P * j + P, :]
                                                  ).then_inc(s_early, 16)
                                else:
                                    act.dma_start(early[:, FT + j, :].rearrange("p (n r) -> p n r", r=RANK),
                                                  Aw[:, P * j:P * j + P, :].rearrange("n o r -> o n r")
                                                  ).then_inc(s_early, 16)
                    EARLY = {X_TO: (0, 1), X_TO + 1: (2, 3), TILES: (4, 5), TILES + 1: (6, 7)}
                    steps(act, step)

                @block.tensor
                def _(pe):
                    THREE = ((0, 0), (1, 0), (0, 1))

                    def q(at):
                        after(pe, "x_T", at, per=16)
                        after(pe, "q_lo", at, back=1)
                        for j in range(FT):
                            for f in range(FT):
                                for w, half in THREE:
                                    mm = pe.matmul(QT[:, P * j:P * j + P], Wq16[:, w, j, f, :], xT[:, half, f, :],
                                                   start=(f == 0 and (w, half) == THREE[0]),
                                                   stop=(f == FT - 1 and (w, half) == THREE[-1]))
                        mm.then_inc(L["q"], 1)

                    def scores0(at):
                        after(pe, "q_lo", at)
                        after(pe, "shifted", at, back=1)
                        for k in range(3):
                            pe.matmul(scores_bank(k), sel16[:], row[:, at.b, KEYS * 6 * k:KEYS * 6 * k + KEYS * BANK_HEADS[k]],
                                      start=True, stop=False)
                        for w, half in THREE:
                            for j, first, heads, k, col, last in ((0, 0, 4, 0, 0, False), (1, 0, 2, 0, 4, True),
                                                                  (1, 2, 2, 1, 0, False), (2, 0, 4, 1, 2, True),
                                                                  (3, 0, 4, 2, 0, True)):
                                mm = pe.matmul(PS[:, S_BANK + k, KEYS * col:KEYS * (col + heads)], qT16[:, half, j, :],
                                               K16[:, w, j, at.b, KEYS * first:KEYS * (first + heads)], start=False,
                                               stop=(last and (w, half) == THREE[-1]))
                        mm.then_inc(L["scores"], 1)

                    def pv(at):
                        after(pe, "p_T_hi", at, per=16)
                        after(pe, "pv_lo", at, back=1)
                        for half, of_weights in ((0, (0, 1)), (1, (0,))):
                            if half == 1:
                                after(pe, "p_T_lo", at, per=16)
                            for j in range(FT):
                                first, last = first_row_tile(0, j), last_row_tile(0, j)
                                for i in range(first, last + 1):
                                    for w in of_weights:
                                        mm = pe.matmul(OT[:, P * j:P * j + P],
                                                       V16[:, w, block_no[at.b, j, i], :], pT[:, half, i, :],
                                                       start=(half == 0 and w == 0 and i == j == 0),
                                                       stop=(half == 1 and i == last and j == FT - 1))
                        mm.then_inc(L["pv"], 1)

                    def attn_out0(at):
                        after(pe, "pv_lo", at)
                        after(pe, "x_attn", at, back=1)
                        pe.matmul(ATTN, sel16[:], rowbo, start=True, stop=False)
                        for w, half in THREE:
                            for j in range(FT):
                                mm = pe.matmul(ATTN, oT16[:, half, j, :], Wo16[:, w, j, :], start=False,
                                               stop=((w, half) == THREE[-1] and j == FT - 1))
                        mm.then_inc(L["attn_out"], 1)

                    def scores(at):
                        after(pe, "x_T", at, per=16)
                        after(pe, "shifted", at, back=1)
                        for f in range(FT):
                            for w, half in THREE:
                                for k in range(3):
                                    c = 6 * KEYS * k
                                    mm = pe.matmul(scores_bank(k), xT[:, half, f, :],
                                                   Kf[:, at.b, w, f, c:c + KEYS * BANK_HEADS[k]],
                                                   start=(f == 0 and (w, half) == THREE[0]),
                                                   stop=(f == FT - 1 and (w, half) == THREE[-1]))
                        mm.then_inc(L["scores"], 1)

                    def attn_out(at):
                        after(pe, "x_attn", at, back=1)
                        for w, half in THREE:
                            if w == 0:
                                after(pe, ("p_T_hi", "p_T_lo")[half], at, per=16)
                            for i in range(ROWT):
                                mm = pe.matmul(ATTN, pT[:, half, i, :], Vw[:, at.b, w, i, :],
                                               start=((w, half) == THREE[0] and i == 0),
                                               stop=((w, half) == THREE[-1] and i == ROWT - 1))
                        mm.then_inc(L["attn_out"], 1)

                    def ffn0_out(at):
                        after(pe, "q_T", at, per=16)
                        after(pe, "ffn0_scaled", at, back=1)
                        for f in range(FT):
                            mm = pe.matmul(FFN0, qT[:, f, :], rq[:, f, :], start=(f == 0), stop=(f == FT - 1))
                        mm.then_inc(L["ffn0_out"], 1)

                    def three(outp, hi, lo, w, start=True):
                        for f in range(FT):
                            pe.matmul(outp, hi[:, f, :], w[:, 0, f, :], start=(start and f == 0), stop=False)
                            pe.matmul(outp, hi[:, f, :], w[:, 1, f, :], start=False, stop=False)
                            mm = pe.matmul(outp, lo[:, f, :], w[:, 0, f, :], start=False, stop=(f == FT - 1))
                        return mm

                    def hidden(at):
                        after(pe, "d_T", at, per=16)
                        after(pe, "dist_a", at, back=1)
                        three(DOTS[:, 0:PROTOS], dT[:, 0], dT[:, 1], pw).then_inc(L["dots"], 1)
                        after(pe, "weighted", at, back=1)
                        three(HIDDEN, dT[:, 0], dT[:, 1], bt).then_inc(L["hidden"], 1)

                    def ffn1_out(at):
                        after(pe, "h_T", at, per=16)
                        after(pe, "x_ffn1", at, back=1)
                        pe.matmul(FFN1, hT[0:3 * PROTOS, 2 * FT, :], bs[0:3 * PROTOS, :], start=True, stop=False)
                        three(FFN1, hT[:, 0:FT], hT[:, FT:2 * FT], ad, start=False).then_inc(L["ffn1_out"], 1)

                    def step(s, u, batch):
                        tile = [At(s, u, batch, k) for k in range(7)]
                        if layer == 0:
                            if tile[SC].on:
                                scores0(tile[SC])
                            if tile[FF + 1].on:
                                ffn0_out(tile[FF + 1])
                            if tile[OUT].on:
                                attn_out0(tile[OUT])
                            if tile[1].on:
                                q(tile[1])
                            if tile[3].on:
                                pv(tile[3])
                            if isinstance(s, int) and s == FF:
                                pe.wait_ge(s_rq, 5)
                        else:
                            if tile[SC].on:
                                scores(tile[SC])
                            if tile[OUT].on:
                                attn_out(tile[OUT])
                            if tile[FF].on:
                                hidden(tile[FF])
                            if tile[4].on:
                                ffn1_out(tile[4])
                    steps(pe, step)

                @block.vector
                def _(dve):
                    def statistics(at, k, stage, src):
                        if src:
                            after(dve, src, at, alone=True)
                        dve.bn_stats(st[:, k, at.u, :], X[:, at.n, :]).then_inc(L[stage + "stats"], 1)
                        after(dve, stage + "stats", at, alone=True)
                        dve.bn_aggr(mv[:, k, at.u, :], st[:, k, at.u, :]).then_inc(L[stage + "mean_var"], 1)

                    def q_lo(at):
                        after(dve, "q_hi", at)
                        dve.scalar_tensor_tensor(qT16[:, 1].rearrange("p j t -> p (j t)"), QT, QSC,
                                                 qT16[:, 0].rearrange("p j t -> p (j t)"), ALU.mult,
                                                 ALU.subtract).then_inc(L["q_lo"], 1)

                    def pv_lo(at):
                        after(dve, "pv_hi", at)
                        dve.scalar_tensor_tensor(oT16[:, 1].rearrange("p j t -> p (j t)"), OT, OSC,
                                                 oT16[:, 0].rearrange("p j t -> p (j t)"), ALU.mult,
                                                 ALU.subtract).then_inc(L["pv_lo"], 1)

                    def ln_lo(at):
                        after(dve, "ln_hi", at)
                        dve.scalar_tensor_tensor(xs[:, 1], xn, XS, xs[:, 0], ALU.mult,
                                                 ALU.subtract).then_inc(L["ln_lo"], 1)

                    def shift_scores(at):
                        after(dve, "scores", at)
                        for src, cols, heads, shape in scores_parts():
                            ins = dve.tensor_reduce(cut(mx[:, at.u, heads], shape), src, AX, ALU.max)
                        ins.then_inc(L["max"], 1)
                        after(dve, "max", at)
                        after(dve, "probs_lo", at, back=PROB_BUFS)
                        for src, cols, heads, shape in scores_parts():
                            o = PROB[at.u][:, cols]
                            o = o.rearrange("p (a h k) -> p a h k", a=2, k=KEYS) if len(shape) == 2 else by_head(o)
                            m = cut(mx[:, at.u, heads], shape)
                            m = m.unsqueeze(len(shape) + 1).to_broadcast([P, *shape, KEYS])
                            ins = dve.tensor_tensor(o, src, m, ALU.subtract)
                        ins.then_inc(L["shifted"], 1)

                    def sums(at):
                        after(dve, "exp", at)
                        dve.tensor_reduce(smx[:, at.u, 0, :], by_head(PROB[at.u]), AX, ALU.add).then_inc(L["sum"], 1)
                        after(dve, "sum", at)
                        dve.reciprocal(smx[:, at.u, 1, :], smx[:, at.u, 0, :]).then_inc(L["inv_sum"], 1)
                        after(dve, "inv_sum", at)
                        dve.tensor_scalar(smx[:, at.u, 2, :], smx[:, at.u, 1, :], PSC, None,
                                          ALU.mult).then_inc(L["scaled_inv"], 1)

                    def add_attn(at):
                        after(dve, "attn_out", at)
                        dve.scalar_tensor_tensor(X[:, at.n, :], ATTN, sc[:, 3:4], X[:, at.n, :], ALU.mult,
                                                 ALU.add).then_inc(L["x_attn"], 1)

                    def lhs_scales(at):
                        after(dve, "f_ln", at)
                        dve.tensor_reduce(lsb[:, at.u, 0:1], xf, AX, ALU.max, apply_absolute_value=True).then_inc(L["absmax"], 1)
                        after(dve, "absmax", at)
                        dve.tensor_scalar(lsb[:, at.u, 1:2], lsb[:, at.u, 0:1], TINY, 1.0 / INT8_MAX, ALU.max,
                                          ALU.mult).then_inc(L["lhs_scale"], 1)
                        after(dve, "lhs_scale", at)
                        dve.reciprocal(lsb[:, at.u, 2:3], lsb[:, at.u, 1:2]).then_inc(L["lhs_inv"], 1)

                    def clamp(at):
                        after(dve, "quant_scaled", at)
                        dve.tensor_scalar(xq, xq, INT8_MAX, -INT8_MAX, ALU.min, ALU.max).then_inc(L["quant"], 1)

                    def weigh_hidden(at):
                        dve.wait_ge(L["route"], at.n * 8 + 8)
                        after(dve, "hidden", at)
                        after(dve, "h_lo", at, back=1)
                        dve.scalar_tensor_tensor(hw.rearrange("p (n r) -> p n r", r=RANK),
                                                 HIDDEN.rearrange("p (n r) -> p n r", r=RANK), HS / (WS * XS),
                                                 wt[:].unsqueeze(2).to_broadcast([P, PROTOS, RANK]), ALU.mult,
                                                 ALU.mult).then_inc(L["weighted"], 1)

                    def h_lo(at):
                        after(dve, "h_hi", at)
                        dve.tensor_tensor(hs[:, D:2 * D], hw, hs[:, 0:D], ALU.subtract).then_inc(L["h_lo"], 1)
                        after(dve, "w_hi", at)
                        hi, lo = (slice(2 * D + k * PROTOS, 2 * D + (k + 1) * PROTOS) for k in (1, 2))
                        dve.scalar_tensor_tensor(hs[:, lo], wt[:], WTS, hs[:, hi], ALU.mult,
                                                 ALU.subtract).then_inc(L["w_lo"], 1)

                    def d_lo(at):
                        after(dve, "d_hi", at)
                        dve.scalar_tensor_tensor(ds[:, 1], xf, XS, ds[:, 0], ALU.mult,
                                                 ALU.subtract).then_inc(L["d_lo"], 1)

                    def add_ffn1(at):
                        after(dve, "ffn1_out", at)
                        dve.scalar_tensor_tensor(X[:, at.n, :], FFN1, sc[:, 11:12], X[:, at.n, :], ALU.mult,
                                                 ALU.add).then_inc(L["x_ffn1"], 1)

                    def nearest(at):
                        after(dve, "dots", at)
                        after(dve, "best_at", at, back=1)
                        dve.scalar_tensor_tensor(rt[:, 0], DOTS[:, 0:PROTOS], sc[:, 13:14], p2, ALU.mult,
                                                 ALU.subtract).then_inc(L["dist_a"], 1)
                        after(dve, "dist_a", at)
                        after(dve, "sq_sum", at)
                        dve.tensor_scalar(rt[:, 1], rt[:, 0], x2[:, at.u:at.u + 1], 0.0, ALU.subtract,
                                          ALU.min).then_inc(L["dist_b"], 1)
                        after(dve, "dist_b", at, alone=True)
                        dve.max(m8[:], rt[:, 1]).then_inc(L["best"], 1)
                        after(dve, "best", at, alone=True)
                        dve.max_index(i8[:], m8[:], rt[:, 1]).then_inc(L["best_at"], 1)

                    def step(s, u, batch):
                        tile = [At(s, u, batch, k) for k in range(7)]
                        if layer == 0 and tile[OUT].on:
                            pv_lo(tile[OUT])
                        if loading(s, batch):
                            wait(dve, s_x[u], x_loads(s, u), True)
                        elif layer == 0 and isinstance(s, int) and s == x_first:
                            dve.wait_ge(s_x[1], 16)
                        elif layer == 0 and isinstance(s, int) and s in (X_TO, X_TO + 1):
                            dve.wait_ge(s_x[u], x_loads(s, u))
                        if tile[0].on:
                            statistics(tile[0], 0, "", None)
                        if layer == 0:
                            if tile[FF].on:
                                clamp(tile[FF])
                            if tile[SC].on:
                                shift_scores(tile[SC])
                            if tile[OUT].on:
                                add_attn(tile[OUT])
                                statistics(tile[OUT], 1, "f_", "x_attn")
                            if tile[SC].on:
                                sums(tile[SC])
                            if tile[1].on:
                                q_lo(tile[1])
                            if tile[OUT].on:
                                lhs_scales(tile[OUT])
                            if tile[0].on:
                                ln_lo(tile[0])
                            if isinstance(s, int) and RHS_AT <= s < RHS_AT + 4:
                                (rhs_absmax, rhs_scales, divide_rhs, quantise_rhs)[s - RHS_AT](dve)
                        else:
                            if tile[FF].on:
                                d_lo(tile[FF])
                            if tile[SC].on:
                                shift_scores(tile[SC])
                            if tile[4].on:
                                weigh_hidden(tile[4])
                                h_lo(tile[4])
                            if tile[0].on:
                                ln_lo(tile[0])
                            if tile[SC].on:
                                sums(tile[SC])
                            if tile[OUT].on:
                                add_attn(tile[OUT])
                                statistics(tile[OUT], 1, "f_", "x_attn")
                            if tile[FF].on:
                                nearest(tile[FF])
                            if tile[4].on:
                                add_ffn1(tile[4])
                    steps(dve, step)

                @block.sync
                def _(sp):
                    def turn(out, halves, name):
                        sp.dma_start_transpose(out, halves).then_inc(L[name], 16)

                    def turn_probs(at, half):
                        after(sp, ("probs_hi", "probs_lo")[half], at, alone=True)
                        after(sp, ("pv", "attn_out")[layer], at, back=1, alone=True)
                        turn(pT[:, half], ps[:, half], ("p_T_hi", "p_T_lo")[half])

                    def turn_ln(at):
                        after(sp, "ln_lo", at, alone=True)
                        after(sp, ("q", "scores")[layer], at, back=1, alone=True)
                        turn(xT.rearrange("p w f t -> p (w f) t"), xs.rearrange("p w d -> p (w d)"), "x_T")

                    def turn_quant(at):
                        after(sp, "quant_int", at, alone=True)
                        after(sp, "ffn0_out", at, back=1, alone=True)
                        turn(qT, qs, "q_T")

                    def turn_d(at):
                        after(sp, "d_lo", at, alone=True)
                        after(sp, "hidden", at, back=1, alone=True)
                        turn(dT.rearrange("p w f t -> p (w f) t"), ds.rearrange("p w d -> p (w d)"), "d_T")

                    def turn_hidden(at):
                        after(sp, "w_lo", at, alone=True)
                        after(sp, "ffn1_out", at, back=1, alone=True)
                        turn(hT, hs, "h_T")

                    def store(at):
                        after(sp, "x_ffn1", at)
                        sp.dma_start(rows_out[:, at.n, :], X[:, at.n, :]).then_inc(L["stored"], 16)

                    rows_out = out.rearrange("b (t p) d -> p (b t) d", p=P)
                    sp.wait_ge(s_pad, (1, 3)[layer])

                    def step(s, u, batch):
                        tile = [At(s, u, batch, k) for k in range(7)]
                        if layer == 0:
                            if tile[SC + 1].on:
                                turn_probs(tile[SC + 1], 0)
                            if tile[SC + 1].on:
                                turn_probs(tile[SC + 1], 1)
                            if tile[FF].on:
                                turn_quant(tile[FF])
                            if tile[0].on:
                                turn_ln(tile[0])
                            if loading(s, batch):
                                sp.wait_ge(s_x[u], x_loads(s, u))
                                n = x_first * 2 + 2 * (s - X_FROM)
                                sp.dma_start(X[:, bass.ds(n, 2), :], x_rows[:, bass.ds(n, 2), :]).then_inc(s_x[u], 16)
                        else:
                            if tile[SC + 1].on:
                                turn_probs(tile[SC + 1], 0)
                                turn_probs(tile[SC + 1], 1)
                            if tile[FF].on:
                                turn_d(tile[FF])
                            if tile[4].on:
                                turn_hidden(tile[4])
                            if tile[0].on:
                                turn_ln(tile[0])
                            if tile[5].on:
                                store(tile[5])
                    steps(sp, step)
                    if layer == 1:
                        store(At(LAST, LAST % 2, None, 5))
                        sp.wait_ge(L["stored"], 16 * TILES)


        setup0()
        loop(0)
        setup1()
        loop(1)


_INS = ['x', 'ctx_1024', 'mask_BxS2_ff1', 'g_xattn', 'g_ffn', 'L0_xattn_Wq', 'L0_xattn_bq', 'L0_xattn_Wk', 'L0_xattn_bk',
        'L0_xattn_Wv', 'L0_xattn_bv', 'L0_xattn_Wo', 'L0_xattn_bo', 'L0_ffn_rhs', 'L1_xattn_Wq', 'L1_xattn_Wk',
        'L1_xattn_Wv', 'L1_xattn_Wo', 'L1_xattn_bo', 'L1_ffn_prototypes', 'L1_ffn_B', 'L1_ffn_A', 'L1_ffn_bias',
        'L1_ffn_temp']


def kernel(**inputs):
    import numpy as _np
    import concourse.bacc as _bacc
    from concourse.bass_utils import run_bass_kernel_spmd as _run

    nc = _bacc.Bacc("TRN2", target_bir_lowering=False, num_devices=1)
    arrays, args = {}, []
    for name in _INS:
        a = _np.ascontiguousarray(inputs[name])
        a = a.reshape(a.shape or (1,))
        arrays[f"in_{name}"] = a
        args.append(nc.dram_tensor(f"in_{name}", a.shape, F32, kind="ExternalInput").ap())
    args.append(nc.dram_tensor("out", (B, T, D), F32, kind="ExternalOutput").ap())
    build(nc, *args)
    return _run(nc, [arrays], core_ids=[0]).results[0]["out"]
```
